# Optimizing a Trainium2 kernel written in Bass

```python
import numpy as np
import jax
import jax.numpy as jnp

def _softmax(x, axis=-1):
    return jax.nn.softmax(x, axis=axis)

def _gelu(x):
    return jax.nn.gelu(x, approximate=True)

def _silu(x):
    return jax.nn.silu(x)

def _sigmoid(x):
    return jax.nn.sigmoid(x)

def _layernorm(x, axis=-1, eps=1e-05):
    m = jnp.mean(x, axis=axis, keepdims=True)
    v = jnp.var(x, axis=axis, keepdims=True)
    return (x - m) / jnp.sqrt(v + eps)

def _scatter_add(tgt, idx, src, axis=0):
    return tgt.at[idx].add(src)

def _segment_sum(src, seg, n):
    return jax.ops.segment_sum(src, seg, n)
kernel_name = 'mk_decoder_preln_d1_seqx_r4_6b45a3'

def setup_inputs(seed: int=0):
    np.random.seed(seed)
    _w = jnp.asarray

    def _rec_inputs():
        import jax
        import jax.numpy as jnp
        _rk = jax.random.key(seed)
        x = -0.0002928 + 1 * jax.random.normal(jax.random.fold_in(_rk, 1), (8, 512, 256), jnp.float32)
        _lenS = 512 - jax.random.randint(jax.random.fold_in(_rk, 7), (8,), 0, max(1, 512 // 4) + 1, jnp.int32)
        _lenS2 = 512 - jax.random.randint(jax.random.fold_in(_rk, 8), (8,), 0, max(1, 512 // 4) + 1, jnp.int32)
        _ctx_1024P = jax.random.normal(jax.random.fold_in(_rk, 11), (8, 16, 256), jnp.float32)
        _ctx_1024c = jax.random.dirichlet(jax.random.fold_in(_rk, 511), 0.3 * jnp.ones((16,), jnp.float32), (8, 512))
        _ctx_1024t = jnp.einsum('bsk,bkd->bsd', _ctx_1024c, _ctx_1024P)
        _ctx_1024t = _ctx_1024t * jax.lax.rsqrt(jnp.mean(jnp.square(_ctx_1024t)) + 1e-12) * 0.953939
        ctx_1024 = -1.39393e-06 + 0.999914 * (_ctx_1024t + 0.3 * jax.random.normal(jax.random.fold_in(_rk, 611), (8, 512, 256), jnp.float32))
        _validS = jnp.arange(512)[None, :] < _lenS[:, None]
        _validS2 = jnp.arange(512)[None, :] < _lenS2[:, None]
        _causal = jnp.tril(jnp.ones((512, 512), dtype=bool))
        mask_Bx1xSxS2_ik1 = jnp.where(jnp.broadcast_to(_validS2[:, None, None, :], (8, 1, 512, 512)), 1, 0).astype(jnp.int32)
        return (x, ctx_1024, mask_Bx1xSxS2_ik1)
    x, ctx_1024, mask_Bx1xSxS2_ik1 = _rec_inputs()

    def _L0_attn_setup():
        import jax, jax.numpy as jnp
        import numpy as np
        B, S, E = (4, 512, 256)
        HIDDEN = 256
        HEADS = 16
        key = jax.random.key(seed)
        k0, k1, k2, k3, k4 = jax.random.split(key, 5)
        inputs = jax.random.normal(k0, (B, S, E), dtype=jnp.float32)
        W_qkv = jax.random.normal(k1, (E, 3 * HIDDEN), dtype=jnp.float32) * 0.02
        b_qkv = jnp.zeros((3 * HIDDEN,), dtype=jnp.float32)
        W_out = jax.random.normal(k2, (HIDDEN, HIDDEN), dtype=jnp.float32) * 0.02
        b_out = jnp.zeros((HIDDEN,), dtype=jnp.float32)
        return {'inputs': inputs, 'W_qkv': W_qkv, 'b_qkv': b_qkv, 'W_out': W_out, 'b_out': b_out}
    _L0_attn_all = _L0_attn_setup()
    _L0_attn_in = {k: v for k, v in _L0_attn_all.items() if k in ('W_qkv', 'b_qkv', 'W_out', 'b_out')}
    del _L0_attn_all

    def _L0_xattn_setup():
        import jax, jax.numpy as jnp
        import numpy as np
        B, S, E, H = (2, 512, 256, 16)
        D = E // H
        key = jax.random.key(seed)
        ks = jax.random.split(key, 14)
        inp = {'query': jax.random.normal(ks[0], (B, S, E), jnp.float32), 'key': jax.random.normal(ks[1], (B, S, E), jnp.float32), 'value': jax.random.normal(ks[2], (B, S, E), jnp.float32), 'adj': jax.random.normal(ks[3], (S, S), jnp.float32), 'mask': jax.random.randint(ks[4], (B, 1, S, S), 0, 2, jnp.int32)}
        sc = 1.0 / np.sqrt(E)
        inp['Wq'] = jax.random.normal(ks[5], (E, E), jnp.float32) * sc
        inp['bq'] = jax.random.normal(ks[6], (E,), jnp.float32) * sc
        inp['Wk'] = jax.random.normal(ks[7], (E, E), jnp.float32) * sc
        inp['bk'] = jax.random.normal(ks[8], (E,), jnp.float32) * sc
        inp['Wv'] = jax.random.normal(ks[9], (E, E), jnp.float32) * sc
        inp['bv'] = jax.random.normal(ks[10], (E,), jnp.float32) * sc
        inp['Wo'] = jax.random.normal(ks[11], (E, E), jnp.float32) * sc
        inp['bo'] = jax.random.normal(ks[12], (E,), jnp.float32) * sc
        return inp
    _L0_xattn_all = _L0_xattn_setup()
    _L0_xattn_in = {k: v for k, v in _L0_xattn_all.items() if k in ('adj', 'Wq', 'bq', 'Wk', 'bk', 'Wv', 'bv', 'Wo', 'bo')}
    del _L0_xattn_all

    def _L0_ffn_setup():
        import jax, jax.numpy as jnp
        import numpy as np
        E = 8
        TOP_K = 2
        ROUTE_SCALE = 1.0
        ALPHA = 1.702
        LIMIT = 7.0
        D = 256
        F = 256
        B, S = (2, 256)

        def swiglu(h):
            g = jnp.minimum(h[..., ::2], LIMIT)
            l = jnp.clip(h[..., 1::2], -LIMIT, LIMIT)
            return g * jax.nn.sigmoid(ALPHA * g) * (l + 1.0)
        if __name__ == '__main__':
            out = reference(**setup_inputs())
            print(out.shape, out.dtype)
        key = jax.random.key(seed)
        ks = jax.random.split(key, 16)
        sd = 1.0 / np.sqrt(D)
        sf = 1.0 / np.sqrt(F)
        return {'x': jax.random.normal(ks[0], (B, S, D), jnp.float32), 'gate_w': jax.random.normal(ks[1], (E, D), jnp.float32) * sd, 'gate_b': jax.random.normal(ks[2], (E,), jnp.float32) * 0.01, 'w1': jax.random.normal(ks[3], (E, 2 * F, D), jnp.float32) * sd, 'b1': jax.random.normal(ks[4], (E, 2 * F), jnp.float32) * 0.01, 'w3': jax.random.normal(ks[5], (E, 2 * F, D), jnp.float32) * sd, 'b3': jax.random.normal(ks[6], (E, 2 * F), jnp.float32) * 0.01, 'w2': jax.random.normal(ks[7], (E, D, F), jnp.float32) * sf, 'b2': jax.random.normal(ks[8], (E, D), jnp.float32) * 0.01, 'sw1': jax.random.normal(ks[9], (2 * F, D), jnp.float32) * sd, 'sb1': jax.random.normal(ks[10], (2 * F,), jnp.float32) * 0.01, 'sw3': jax.random.normal(ks[11], (2 * F, D), jnp.float32) * sd, 'sb3': jax.random.normal(ks[12], (2 * F,), jnp.float32) * 0.01, 'sw2': jax.random.normal(ks[13], (D, F), jnp.float32) * sf, 'sb2': jax.random.normal(ks[14], (D,), jnp.float32) * 0.01}
    _L0_ffn_all = _L0_ffn_setup()
    _L0_ffn_in = {k: v for k, v in _L0_ffn_all.items() if k in ('gate_w', 'gate_b', 'w1', 'b1', 'w3', 'b3', 'w2', 'b2', 'sw1', 'sb1', 'sw3', 'sb3', 'sw2', 'sb2')}
    del _L0_ffn_all
    return {'x': x, 'ctx_1024': ctx_1024, 'mask_Bx1xSxS2_ik1': mask_Bx1xSxS2_ik1, 'L0_attn_W_qkv': _L0_attn_in['W_qkv'], 'L0_attn_b_qkv': _L0_attn_in['b_qkv'], 'L0_attn_W_out': _L0_attn_in['W_out'], 'L0_attn_b_out': _L0_attn_in['b_out'], 'L0_xattn_adj': _L0_xattn_in['adj'], 'L0_xattn_Wq': _L0_xattn_in['Wq'], 'L0_xattn_bq': _L0_xattn_in['bq'], 'L0_xattn_Wk': _L0_xattn_in['Wk'], 'L0_xattn_bk': _L0_xattn_in['bk'], 'L0_xattn_Wv': _L0_xattn_in['Wv'], 'L0_xattn_bv': _L0_xattn_in['bv'], 'L0_xattn_Wo': _L0_xattn_in['Wo'], 'L0_xattn_bo': _L0_xattn_in['bo'], 'L0_ffn_gate_w': _L0_ffn_in['gate_w'], 'L0_ffn_gate_b': _L0_ffn_in['gate_b'], 'L0_ffn_w1': _L0_ffn_in['w1'], 'L0_ffn_b1': _L0_ffn_in['b1'], 'L0_ffn_w3': _L0_ffn_in['w3'], 'L0_ffn_b3': _L0_ffn_in['b3'], 'L0_ffn_w2': _L0_ffn_in['w2'], 'L0_ffn_b2': _L0_ffn_in['b2'], 'L0_ffn_sw1': _L0_ffn_in['sw1'], 'L0_ffn_sb1': _L0_ffn_in['sb1'], 'L0_ffn_sw3': _L0_ffn_in['sw3'], 'L0_ffn_sb3': _L0_ffn_in['sb3'], 'L0_ffn_sw2': _L0_ffn_in['sw2'], 'L0_ffn_sb2': _L0_ffn_in['sb2']}

def reference(x, ctx_1024, mask_Bx1xSxS2_ik1, L0_attn_W_qkv, L0_attn_b_qkv, L0_attn_W_out, L0_attn_b_out, L0_xattn_adj, L0_xattn_Wq, L0_xattn_bq, L0_xattn_Wk, L0_xattn_bk, L0_xattn_Wv, L0_xattn_bv, L0_xattn_Wo, L0_xattn_bo, L0_ffn_gate_w, L0_ffn_gate_b, L0_ffn_w1, L0_ffn_b1, L0_ffn_w3, L0_ffn_b3, L0_ffn_w2, L0_ffn_b2, L0_ffn_sw1, L0_ffn_sb1, L0_ffn_sw3, L0_ffn_sb3, L0_ffn_sw2, L0_ffn_sb2):
    import jax
    import jax.numpy as jnp

    def _L0_attn_ref(inputs, W_qkv, b_qkv, W_out, b_out):
        import jax, jax.numpy as jnp
        import numpy as np
        B, S, E = (4, 512, 256)
        HIDDEN = 256
        HEADS = 16
        Bv, Sv, Ev = inputs.shape
        x = inputs @ W_qkv + b_qkv
        x = x.reshape(Bv, HEADS, Sv, -1)
        q, k, v = jnp.split(x, 3, axis=-1)
        scale = (2 * HIDDEN) ** (-0.5)
        qk = jnp.einsum('bhse,bhte->bhst', q, k) * scale
        mask = jnp.triu(jnp.full((Sv, Sv), -jnp.inf, dtype=qk.dtype), k=1)
        attn = jax.nn.softmax(qk + mask, axis=-1)
        sa = jnp.einsum('bhst,bhte->bhse', attn, v).reshape(Bv, Sv, -1)
        return sa @ W_out + b_out

    def _L0_xattn_ref(query, key, value, adj, mask, Wq, bq, Wk, bk, Wv, bv, Wo, bo):
        import jax, jax.numpy as jnp
        import numpy as np
        B, S, E, H = (2, 512, 256, 16)
        D = E // H
        b, s, _ = query.shape

        def heads(x, W, bias):
            y = jnp.einsum('bse,ef->bsf', x, W.T) + bias
            return y.reshape(b, s, H, D).transpose(0, 2, 1, 3)
        Q = heads(query, Wq, bq)
        K = heads(key, Wk, bk)
        V = heads(value, Wv, bv)
        scores = jnp.einsum('bhqd,bhkd->bhqk', Q, K) / jnp.sqrt(jnp.float32(D))
        scores = scores + adj[None, None, :, :]
        scores = jnp.where(mask == 0, jnp.float32(-jnp.inf), scores)
        weights = jax.nn.softmax(scores, axis=-1)
        out = jnp.einsum('bhqk,bhkd->bhqd', weights, V)
        out = out.transpose(0, 2, 1, 3).reshape(b, s, E)
        return jnp.einsum('bse,ef->bsf', out, Wo.T) + bo

    def _L0_ffn_ref(x, gate_w, gate_b, w1, b1, w3, b3, w2, b2, sw1, sb1, sw3, sb3, sw2, sb2):
        import jax, jax.numpy as jnp
        import numpy as np
        E = 8
        TOP_K = 2
        ROUTE_SCALE = 1.0
        ALPHA = 1.702
        LIMIT = 7.0
        D = 256
        F = 256
        B, S = (2, 256)

        def swiglu(h):
            g = jnp.minimum(h[..., ::2], LIMIT)
            l = jnp.clip(h[..., 1::2], -LIMIT, LIMIT)
            return g * jax.nn.sigmoid(ALPHA * g) * (l + 1.0)
        if __name__ == '__main__':
            out = reference(**setup_inputs())
            print(out.shape, out.dtype)
        inp_shape = x.shape
        xt = x.reshape(-1, D)
        logits = xt @ gate_w.T
        scores = jax.nn.softmax(logits.astype(jnp.float32), axis=-1)
        biased = scores + gate_b.astype(jnp.float32)
        idx = jax.lax.top_k(biased, TOP_K)[1]
        weights = (jnp.take_along_axis(scores, idx, axis=-1) * ROUTE_SCALE).astype(x.dtype)
        cw = jnp.sum(jax.nn.one_hot(idx, E, dtype=x.dtype) * weights[..., None], axis=1)
        h1 = jnp.einsum('td,efd->etf', xt, w1) + b1[:, None, :]
        h3 = jnp.einsum('td,efd->etf', xt, w3) + b3[:, None, :]
        a = swiglu(h1 * h3)
        y = jnp.einsum('etf,edf->etd', a, w2) + b2[:, None, :]
        routed = jnp.einsum('te,etd->td', cw, y)
        sh = swiglu((xt @ sw1.T + sb1) * (xt @ sw3.T + sb3))
        shared = sh @ sw2.T + sb2
        return (routed + shared).reshape(inp_shape)
    x = x + _L0_attn_ref(_layernorm(x, axis=-1), L0_attn_W_qkv, L0_attn_b_qkv, L0_attn_W_out, L0_attn_b_out)
    x = x + _L0_xattn_ref(_layernorm(x, axis=-1), ctx_1024, ctx_1024, L0_xattn_adj, mask_Bx1xSxS2_ik1, L0_xattn_Wq, L0_xattn_bq, L0_xattn_Wk, L0_xattn_bk, L0_xattn_Wv, L0_xattn_bv, L0_xattn_Wo, L0_xattn_bo)
    x = x + _L0_ffn_ref(_layernorm(x, axis=-1), L0_ffn_gate_w, L0_ffn_gate_b, L0_ffn_w1, L0_ffn_b1, L0_ffn_w3, L0_ffn_b3, L0_ffn_w2, L0_ffn_b2, L0_ffn_sw1, L0_ffn_sb1, L0_ffn_sw3, L0_ffn_sb3, L0_ffn_sw2, L0_ffn_sb2)
    return x

_drawn_inputs = setup_inputs


def setup_inputs(seed=0):
    import zlib

    import numpy as np

    out = dict(_drawn_inputs(seed))
    spreads = {'L0_attn_b_qkv': (0.0, 0.438), 'L0_attn_b_out': (0.0, 0.1)}
    factors = {'L0_attn_W_qkv': 3.048,
     'L0_xattn_bk': 8.0,
     'L0_ffn_b1': 8.0,
     'L0_ffn_b3': 8.0,
     'L0_ffn_b2': 8.0,
     'L0_ffn_sb1': 7.106,
     'L0_ffn_sb3': 7.401,
     'L0_ffn_sb2': 8.0}
    for name, (base, spread) in spreads.items():
        noise = np.random.default_rng([zlib.crc32(name.encode()), seed]).standard_normal(out[name].shape)
        drawn = base * np.exp(spread * noise) if base else spread * noise
        out[name] = jnp.asarray(drawn.astype(out[name].dtype))
    for name, factor in factors.items():
        out[name] = (out[name] * factor).astype(out[name].dtype)
    return out
```

```python
from contextlib import ExitStack

import concourse.bass as bass
from concourse import mybir

ALU = mybir.AluOpType
ACT = mybir.ActivationFunctionType
F32 = mybir.dt.float32
BF16 = mybir.dt.bfloat16
I32 = mybir.dt.int32
AX_X = mybir.AxisListType.X

P = 128
B, S, D = 8, 512, 256
HEADS, HD = 16, 16
TT = S // P
DK = D // P
NE = 8
FF = 256
QUAD = 4
NQUAD = HEADS // QUAD
UNITS = HEADS * TT
Q_SLOTS = (0, 1, 2, 0, 1, 0)
K_SLOTS = (0, 0, 0, 1, 1, 2)
NS = len(Q_SLOTS)
EPS = 1e-5
FILL = -1e30
HUGE = 3e38


class Scope:

    def __init__(self, nc, ctx, tag):
        self.nc, self.ctx, self.tag = nc, ctx, tag
        self.sems = []

    def sb(self, name, shape, dt=F32):
        return self.ctx.enter_context(self.nc.sbuf_tensor(f"{self.tag}_{name}", shape, dt))

    def ps(self, name, shape, dt=F32):
        return self.ctx.enter_context(self.nc.psum_tensor(f"{self.tag}_{name}", shape, dt))

    def sem(self, name):
        self.sems.append(self.nc.alloc_semaphore(name=f"{self.tag}_{name}"))
        return self.sems[-1]

    def end(self):
        self.nc.clear_and_free_semaphores(self.sems)
        self.nc.all_engine_barrier()


def wait_apart(eng, k, sem, value):
    eng.wait_ge(sem, value)
    eng.sem_inc(k["passed"], 1)


def over_batches(eng, body, n=B):
    body(0)
    with eng.Fori(1, n) as b:
        body(b)


def prepare_weights(nc, ctx, w, k):
    keep = Scope(nc, ctx, "k")
    k["passed"] = keep.sem("passed")
    k["ident"] = keep.sb("ident", [P, P])
    k["identb"] = keep.sb("identb", [P, P], BF16)
    k["eps"] = keep.sb("eps", [P, 1])
    k["causal"] = keep.sb("causal", [P, TT, S])
    k["wqkv"] = keep.sb("wqkv", [P, DK, 3 * D])
    k["bqkv"] = keep.sb("bqkv", [P, 3 * D])
    k["wout"] = keep.sb("wout", [P, DK, D])
    k["bout"] = keep.sb("bout", [P, D])
    k["xw"] = keep.sb("xw", [P, 4, DK, D])
    k["bqk"] = keep.sb("bqk", [P, 2, DK])
    k["bv"] = keep.sb("bv", [P, D])
    k["bo"] = keep.sb("bo", [P, D])
    k["gateT"] = keep.sb("gateT", [P, DK, NE])
    k["gateb"] = keep.sb("gateb", [P, NE])
    with ExitStack() as c:
        s = Scope(nc, c, "pw")
        raw = s.sb("raw", [P, 4, DK, D])
        graw = s.sb("graw", [NE, D])
        bq = s.sb("bq", [P, 3 * D])
        tp = s.ps("tp", [P, 4, S])
        tg = s.ps("tg", [P, S])
        loaded, ident_z, ident_1, ident_ok, identb_ok = (s.sem(n) for n in (
            "loaded", "ident_z", "ident_1", "ident_ok", "identb_ok"))
        turned, scaled, kept, causal_0, causal_1 = (s.sem(n) for n in (
            "turned", "scaled", "kept", "causal_0", "causal_1"))
        with nc.Block() as block:
            @block.sync
            def _(sp):
                sp.dma_start(k["wqkv"][:], w["W_qkv"].rearrange("(c p) f -> p c f", p=P)).then_inc(loaded, 16)
                sp.dma_start(k["wout"][:], w["W_out"].rearrange("(c p) f -> p c f", p=P)).then_inc(loaded, 16)
                for n, name in enumerate(("Wq", "Wk", "Wv", "Wo")):
                    sp.dma_start(raw[:, n], w[name].rearrange("(c p) e -> p c e", p=P)).then_inc(loaded, 16)
                sp.dma_start(graw[:], w["gate_w"]).then_inc(loaded, 16)
                for dst, name in ((bq, "b_qkv"), (k["bout"], "b_out"), (k["bv"], "bv"), (k["bo"], "bo"),
                                  (k["gateb"], "gate_b")):
                    n = w[name].shape[0]
                    sp.dma_start(dst[:], w[name].rearrange("(o f) -> o f", o=1).broadcast_to([P, n])).then_inc(loaded, 16)
                for n, name in enumerate(("bq", "bk")):
                    sp.dma_start(k["bqk"][:, n], w[name].rearrange("(c p) -> p c", p=P),
                                 allow_slow_non_contiguous=True).then_inc(loaded, 16)
                sp.wait_ge(loaded, 14 * 16)

            @block.gpsimd
            def _(pool):
                nc.gpsimd.memset(k["ident"][:], 0.0).then_inc(ident_z, 1)
                nc.gpsimd.memset(k["causal"][:], 0.0).then_inc(causal_0, 1)
                pool.wait_ge(ident_z, 1)
                nc.gpsimd.affine_select(out=k["ident"][:], in_=k["ident"][:], compare_op=ALU.not_equal, fill=1.0,
                                        base=0, pattern=[[-1, P]], channel_multiplier=1).then_inc(ident_ok, 1)
                pool.wait_ge(causal_0, 1)
                nc.gpsimd.affine_select(out=k["causal"][:], in_=k["causal"][:], compare_op=ALU.is_ge,
                                        fill=FILL, base=0, pattern=[[P, TT], [-1, S]],
                                        channel_multiplier=1).then_inc(causal_1, 1)
                pool.wait_ge(causal_1, 1)

            @block.tensor
            def _(pe):
                pe.wait_ge(loaded, 14 * 16)
                pe.wait_ge(ident_ok, 1)
                for n in range(4):
                    for ek in range(DK):
                        for fk in range(DK):
                            last = nc.tensor.transpose(tp[:, n, (ek * DK + fk) * P:(ek * DK + fk + 1) * P],
                                                       raw[:, n, fk, ek * P:(ek + 1) * P], k["ident"][:])
                    last.then_inc(turned, 1)
                for ek in range(DK):
                    last = nc.tensor.transpose(tg[:, ek * NE:(ek + 1) * NE], graw[:, ek * P:(ek + 1) * P],
                                               k["ident"][0:NE, 0:NE])
                last.then_inc(turned, 1)

            @block.vector
            def _(dve):
                nc.vector.memset(k["eps"][:], EPS).then_inc(kept, 1)
                dve.wait_ge(ident_ok, 1)
                nc.vector.tensor_copy(k["identb"][:], k["ident"][:]).then_inc(identb_ok, 1)
                dve.wait_ge(loaded, 14 * 16)
                sc = float((2 * D) ** -0.5)
                wq = k["wqkv"][:].rearrange("p c (n f) -> p (c n) f", f=3 * HD)[:, :, 0:HD]
                nc.vector.tensor_scalar(wq, wq, sc, None, ALU.mult).then_inc(scaled, 1)
                nc.vector.tensor_copy(k["bqkv"][:], bq[:]).then_inc(scaled, 1)
                dve.wait_ge(scaled, 2)
                bqs = k["bqkv"][:].rearrange("p (n f) -> p n f", f=3 * HD)[:, :, 0:HD]
                nc.vector.tensor_scalar(bqs, bqs, sc, None, ALU.mult).then_inc(scaled, 1)
                nc.vector.tensor_scalar(k["bqk"][:, 0], k["bqk"][:, 0], float(HD) ** -0.5, None,
                                        ALU.mult).then_inc(scaled, 1)
                for n in range(4):
                    dve.wait_ge(turned, n + 1)
                    nc.vector.tensor_copy(k["xw"][:, n].rearrange("p c f -> p (c f)"), tp[:, n]).then_inc(kept, 1)
                dve.wait_ge(turned, 5)
                nc.vector.tensor_copy(k["gateT"][:].rearrange("p c e -> p (c e)"), tg[:, 0:DK * NE]).then_inc(kept, 1)
                dve.wait_ge(kept, 6)
                dve.wait_ge(scaled, 4)
                dve.wait_ge(identb_ok, 1)
        s.end()


def norm_stats(nc, dve, k, x_of, stats, mv, stats_done, mv_done, b):
    for t in range(TT):
        last = nc.vector.bn_stats(stats[:, t], x_of(t))
    last.then_inc(stats_done, 1)
    wait_apart(dve, k, stats_done, b + 1)
    for t in range(TT):
        last = nc.vector.bn_aggr(mv[:, t], stats[:, t])
    last.then_inc(mv_done, 1)


def norm_sqrt(nc, act, k, mv, sd, mv_done, sd_done, b):
    act.wait_ge(mv_done, b + 1)
    nc.scalar.activation(sd[:], mv[:, :, 1], ACT.Sqrt, bias=k["eps"][:]).then_inc(sd_done, 1)


def norm_apply(nc, dve, x_of, xn_of, mv, sd, rstd, sd_done, rstd_done, xn_done, b):
    dve.wait_ge(sd_done, b + 1)
    nc.vector.reciprocal(rstd[:], sd[:]).then_inc(rstd_done, 1)
    dve.wait_ge(rstd_done, b + 1)
    for t in range(TT):
        nc.vector.tensor_scalar(xn_of(t), x_of(t), mv[:, t, 0:1], rstd[:, t:t + 1],
                                ALU.subtract, ALU.mult).then_inc(xn_done, 1)


def project_self(nc, w, k, scratch):
    with ExitStack() as c:
        s = Scope(nc, c, "ps")
        x = s.sb("x", [P, TT, D])
        xn = s.sb("xn", [P, TT, D])
        xnT = s.sb("xnT", [P, DK, S])
        stats, mv, sd, rstd = s.sb("stats", [P, TT, 6]), s.sb("mv", [P, TT, 2]), s.sb("sd", [P, TT]), s.sb("rstd", [P, TT])
        qkv = s.sb("qkv", [P, TT, 3 * D])
        tp = s.ps("tp", [P, DK, S])
        acc = s.ps("acc", [P, 2, 2 * S])
        x_in = [s.sem(f"x_in{t}") for t in range(TT)]
        stored = [s.sem(f"stored{t}") for t in range(TT)]
        stats_done, mv_done, sd_done, rstd_done, xn_done, turned, xnT_done, acc_done, qkv_done = (s.sem(n) for n in (
            "stats_done", "mv_done", "sd_done", "rstd_done", "xn_done", "turned", "xnT_done", "acc_done", "qkv_done"))
        xr = w["x"].rearrange("b (t p) d -> b t p d", p=P)
        out = scratch["qkv"].rearrange("(b t p r) f -> b t p (r f)", t=TT, p=P, r=HEADS)

        with nc.Block() as block:
            def load(sp, b):
                for t in range(TT):
                    sp.dma_start(x[:, t], xr[bass.ds(b, 1), t].rearrange("o p d -> (o p) d")).then_inc(x_in[t], 16)

            def store(sp, b):
                for t in range(TT):
                    sp.wait_ge(qkv_done, b * TT + t + 1)
                    sp.dma_start(out[bass.ds(b, 1), t].rearrange("o p d -> (o p) d"), qkv[:, t]).then_inc(stored[t], 16)

            @block.sync
            def _(sp):
                load(sp, 0)
                def batch(b):
                    sp.wait_ge(xn_done, b * TT + TT)
                    load(sp, b + 1)
                    store(sp, b)

                over_batches(sp, batch, B - 1)
                store(sp, B - 1)
                for t in range(TT):
                    sp.wait_ge(stored[t], 16 * B)

            def norm(dve, b):
                for t in range(TT):
                    dve.wait_ge(x_in[t], b * 16 + 16)
                norm_stats(nc, dve, k, lambda t: x[:, t], stats, mv, stats_done, mv_done, b)
                dve.wait_ge(turned, b)
                norm_apply(nc, dve, lambda t: x[:, t], lambda t: xn[:, t], mv, sd, rstd, sd_done, rstd_done, xn_done, b)

            def add_bias(dve, b):
                for t in range(TT):
                    dve.wait_ge(acc_done, b * TT + t + 1)
                    dve.wait_ge(stored[t], b * 16)
                    nc.vector.tensor_tensor(qkv[:, t, 0:S], acc[:, t % 2, 0:S], k["bqkv"][:, 0:S], ALU.add)
                    nc.vector.tensor_tensor(qkv[:, t, S:3 * D], acc[:, t % 2, S:3 * D], k["bqkv"][:, S:3 * D],
                                            ALU.add).then_inc(qkv_done, 1)

            @block.vector
            def _(dve):
                norm(dve, 0)
                def batch(b):
                    norm(dve, b + 1)
                    add_bias(dve, b)

                over_batches(dve, batch, B - 1)
                add_bias(dve, B - 1)

            @block.scalar
            def _(act):
                def batch(b):
                    norm_sqrt(nc, act, k, mv, sd, mv_done, sd_done, b)
                    for c_ in range(DK):
                        act.wait_ge(turned, b + 1)
                        if c_ == 0:
                            act.wait_ge(acc_done, b * TT)
                        nc.scalar.copy(xnT[:, c_], tp[:, c_]).then_inc(xnT_done, 1)

                over_batches(act, batch)

            @block.tensor
            def _(pe):
                def batch(b):
                    pe.wait_ge(xnT_done, b * DK)
                    for t in range(TT):
                        pe.wait_ge(xn_done, b * TT + t + 1)
                        for c_ in range(DK):
                            last = nc.tensor.transpose(tp[:, c_, t * P:(t + 1) * P], xn[:, t, c_ * P:(c_ + 1) * P],
                                                       k["ident"][:])
                    last.then_inc(turned, 1)
                    pe.wait_ge(xnT_done, b * DK + DK)
                    for t in range(TT):
                        if t >= 2:
                            pe.wait_ge(qkv_done, b * TT + t - 1)
                        else:
                            pe.wait_ge(qkv_done, b * TT)
                        for lo, hi in ((0, S), (S, 3 * D)):
                            for c_ in range(DK):
                                last = nc.tensor.matmul(acc[:, t % 2, lo:hi], xnT[:, c_, t * P:(t + 1) * P],
                                                        k["wqkv"][:, c_, lo:hi], start=c_ == 0, stop=c_ == DK - 1)
                        last.then_inc(acc_done, 1)

                over_batches(pe, batch)
        s.end()



def split_self(nc, w, k, scratch):
    with ExitStack() as c:
        s = Scope(nc, c, "ss")
        G = 2
        GH = HEADS // G
        src = s.sb("src", [P, G, TT, 2, GH, HD])
        parts = s.sb("parts", [P, 2 * G, 3, S], BF16)
        rest = s.sb("rest", [P, 2 * G, S])
        tp = s.ps("tp", [P, 2 * G, S])
        src_in = [s.sem(f"src_in{g}") for g in range(G)]
        stored = [s.sem(f"stored{u}") for u in range(2 * G)]
        turned, hi_done, rest_done, mid_done, lo_done = (s.sem(n) for n in (
            "turned", "hi_done", "rest_done", "mid_done", "lo_done"))
        rows_of = scratch["qkv"].rearrange("(b g h t p) f -> b g t p h f", b=B, g=G, t=TT, p=P)
        out = scratch["parts"]
        U = 2 * G

        with nc.Block() as block:
            def load(sp, b, g):
                for t in range(TT):
                    for qk in range(2):
                        sp.dma_start(src[:, g, t, qk], rows_of[bass.ds(b, 1), g, t, :, :, qk * HD:(qk + 1) * HD].rearrange(
                            "o p h e -> (o p) h e")).then_inc(src_in[g], 16)

            @block.sync
            def _(sp):
                for g in range(G):
                    load(sp, 0, g)
                def batch(b):
                    for g in range(G):
                        sp.wait_ge(turned, b * U + 2 * g + 2)
                        load(sp, b + 1, g)

                over_batches(sp, batch, B - 1)

            @block.gpsimd
            def _(pool):
                def batch(b):
                    for u in range(U):
                        wait_apart(pool, k, lo_done, b * U + u + 1)
                        pool.dma_start(out[bass.ds(b, 1), u % 2, :, (u // 2) * P:(u // 2 + 1) * P].rearrange("o c p s -> (o p) c s"),
                                       parts[:, u]).then_inc(stored[u], 16)

                over_batches(pool, batch)
                for u in range(U):
                    pool.wait_ge(stored[u], 16 * B)

            @block.tensor
            def _(pe):
                def batch(b):
                    for u in range(U):
                        g, qk = u // 2, u % 2
                        if qk == 0:
                            pe.wait_ge(src_in[g], (b + 1) * 16 * 2 * TT)
                        if u == 0:
                            pe.wait_ge(rest_done, b * U)
                        for t in range(TT):
                            last = nc.tensor.transpose(tp[:, u, t * P:(t + 1) * P], src[:, g, t, qk].rearrange("p h e -> p (h e)"),
                                                       k["ident"][:])
                        last.then_inc(turned, 1)

                over_batches(pe, batch)

            @block.scalar
            def _(act):
                def batch(b):
                    for u in range(U):
                        act.wait_ge(turned, b * U + u + 1)
                        act.wait_ge(stored[u], b * 16)
                        nc.scalar.copy(parts[:, u, 0], tp[:, u]).then_inc(hi_done, 1)
                        act.wait_ge(rest_done, b * U + u + 1)
                        nc.scalar.copy(parts[:, u, 1], rest[:, u]).then_inc(mid_done, 1)

                over_batches(act, batch)

            @block.vector
            def _(dve):
                def batch(b):
                    for u in range(U):
                        dve.wait_ge(hi_done, b * U + u + 1)
                        nc.vector.tensor_tensor(rest[:, u], tp[:, u], parts[:, u, 0], ALU.subtract).then_inc(rest_done, 1)
                        dve.wait_ge(mid_done, b * U + u + 1)
                        nc.vector.tensor_tensor(parts[:, u, 2], rest[:, u], parts[:, u, 1], ALU.subtract).then_inc(lo_done, 1)

                over_batches(dve, batch)
        s.end()


def attention(nc, w, k, scratch, cross):
    with ExitStack() as c:
        s = Scope(nc, c, "xa" if cross else "sa")
        NSC, NPT, NA, NP_, NM = 2, 4, 4, 8, UNITS
        TURN, COPY = 4, 5
        qs = s.sb("qs", [NS * HD, 2, QUAD, S], BF16)
        ks = s.sb("ks", [NS * HD, 2, QUAD, S], BF16)
        v = s.sb("v", [P, 2, QUAD, TT, 32])
        neg = s.sb("neg", [P, NA, S])
        nmax = s.sb("nmax", [P, NM])
        prob = s.sb("prob", [P, NP_, S])
        pT = s.sb("pT", [P, 2, QUAD, TT, TT, P])
        oT = s.sb("oT", [P, S])
        rsum = s.sb("rsum", [P, TT, QUAD])
        o = s.sb("o", [P, 2, TT, QUAD, HD])
        sc = s.ps("sc", [P, NSC, S])
        ptp = s.ps("ptp", [P, NPT, S])
        acc = s.ps("acc", [P, S])
        otp = s.ps("otp", [P, S])
        if cross:
            adj = s.sb("adj", [P, TT, S])
            mask = s.sb("mask", [P, TT, S], I32)
            fill = s.sb("fill", [P, TT, S])
            bias = s.sb("bias", [P, TT, S])
            den, inv = s.sb("den", [P, TT, QUAD]), s.sb("inv", [P, TT, QUAD])
            adj_in, mask_in, fill_done, bias_done, den_done, inv_done = (s.sem(n) for n in (
                "adj_in", "mask_in", "fill_done", "bias_done", "den_done", "inv_done"))
        else:
            bias = k["causal"]
        q_in, k_in, v_in, o_out = ([s.sem(f"{n}{i}") for i in range(2)] for n in ("q_in", "k_in", "v_in", "o_out"))
        (ones_done, sc_done, neg_done, prob_done, turned, copied_d, copied_a, pv_done, oT_done, oturned, rsum_done,
         o_done) = (s.sem(n) for n in ("ones_done", "sc_done", "neg_done", "prob_done", "turned", "copied_d",
                                       "copied_a", "pv_done", "oT_done", "oturned", "rsum_done", "o_done"))
        QU = QUAD * TT

        def width(t):
            return S if cross else (t + 1) * P

        def on_dve(j):
            return j % 2 == 0

        def copied_by(j, dve_side):
            n = j + 1
            return (n + 1) // 2 if dve_side else n // 2

        def wait_copied(eng, b, j):
            eng.wait_ge(copied_d, b * (UNITS // 2) + copied_by(j, True))
            eng.wait_ge(copied_a, b * (UNITS // 2) + copied_by(j, False))

        def steps(emit):
            def run(eng):
                emit(eng, 0, range(UNITS), True)
                with eng.Fori(1, B) as b:
                    emit(eng, b, range(UNITS), False)
                emit(eng, B - 1, range(UNITS, UNITS + 2 * QU), False)
            return run

        parts = scratch["parts"]
        if cross:
            vrows = scratch["v"].rearrange("(b t p) (q h e) -> b q t p h e", b=B, p=P, h=QUAD, e=HD)
        else:
            vrows = scratch["qkv"].rearrange("(b q h t p) f -> b q p h t f", b=B, q=NQUAD, h=QUAD, p=P)

        with nc.Block() as block:
            def load_quad(sp, b, q):
                hs = slice(q * QUAD * HD, (q + 1) * QUAD * HD)
                for which, (dst, slots, sem) in enumerate(((qs, Q_SLOTS, q_in), (ks, K_SLOTS, k_in))):
                    for n, part in enumerate(slots):
                        sp.dma_start(dst[n * HD:(n + 1) * HD, q % 2],
                                     parts[bass.ds(b, 1), which, part, hs].rearrange("o (h e) s -> (o e) h s", e=HD)
                                     ).then_inc(sem[q % 2], 16)

            def load_v(sp, b, q):
                if cross:
                    for t in range(TT):
                        sp.dma_start(v[:, q % 2, :, t, 0:HD], vrows[bass.ds(b, 1), q, t].rearrange("o p h e -> (o p) h e")
                                     ).then_inc(v_in[q % 2], 16)
                else:
                    for h in range(QUAD):
                        sp.dma_start(v[:, q % 2, h, :, 0:HD],
                                     vrows[bass.ds(b, 1), q, :, h, :, 2 * HD:3 * HD].rearrange("o p t e -> (o p) t e")
                                     ).then_inc(v_in[q % 2], 16)

            def loads(sp, b, first):
                if cross:
                    if not first:
                        sp.wait_ge(fill_done, b * TT)
                    sp.dma_start(mask[:], w["mask"][bass.ds(b, 1)].rearrange("o u (t p) s -> (o p) (u t) s", p=P)
                                 ).then_inc(mask_in, 16)
                for q in range(NQUAD):
                    if not (first and q < 2):
                        sp.wait_ge(sc_done, b * UNITS + (q - 1) * QU)
                    load_quad(sp, b, q)
                    if not (first and q < 2):
                        sp.wait_ge(pv_done, b * NQUAD + q - 1)
                    load_v(sp, b, q)

            @block.sync
            def _(sp):
                sp.wait_ge(ones_done, 1)
                if cross:
                    sp.dma_start(adj[:], w["adj"].rearrange("(t p) s -> p t s", p=P)).then_inc(adj_in, 16)
                loads(sp, 0, True)
                with sp.Fori(1, B) as b:
                    loads(sp, b, False)

            @block.gpsimd
            def _(pool):
                nc.gpsimd.memset(v[:].rearrange("p a h t e -> p (a h t e)"), 1.0).then_inc(ones_done, 1)
                def batch(b):
                    for q in range(NQUAD):
                        wait_apart(pool, k, o_done, b * NQUAD + q + 1)
                        if cross:
                            dst = scratch["o"].rearrange("(b t p) (q f) -> b q p t f", b=B, p=P, q=NQUAD)
                            pool.dma_start(dst[bass.ds(b, 1), q].rearrange("o p t f -> (o p) t f"),
                                           o[:, q % 2].rearrange("p t h e -> p t (h e)")).then_inc(o_out[q % 2], 16)
                        else:
                            dst = scratch["o"].rearrange("r (c e) -> (r c) e", e=HD).rearrange(
                                "(b q h t p) e -> b q p t h e", b=B, q=NQUAD, h=QUAD, p=P)
                            for t in range(TT):
                                pool.dma_start(dst[bass.ds(b, 1), q, :, t].rearrange("o p h e -> (o p) h e"),
                                               o[:, q % 2, t]).then_inc(o_out[q % 2], 16)

                over_batches(pool, batch)
                for i in range(2):
                    pool.wait_ge(o_out[i], 16 * (B * NQUAD // 2) * (1 if cross else TT))

            def pe_steps(pe, b, js, first):
                for j in js:
                    q, jj, t = j // QU, j % QU, j % TT
                    if j < UNITS:
                        h, W = jj // TT, width(t)
                        if jj == 0:
                            n = 2 * b + q // 2 + 1
                            pe.wait_ge(q_in[q % 2], n * 16 * NS)
                            pe.wait_ge(k_in[q % 2], n * 16 * NS)
                        if not (first and j < NSC):
                            pe.wait_ge(neg_done, b * UNITS + j - NSC + 1)
                        nc.tensor.matmul(sc[:, j % NSC, 0:W],
                                         qs[:, q % 2, h, t * P:(t + 1) * P], ks[:, q % 2, h, 0:W],
                                         start=True, stop=True).then_inc(sc_done, 1)
                    i = j - TURN
                    if not (first and i < 0) and i < UNITS:
                        it = i % TT
                        pe.wait_ge(prob_done, b * UNITS + i + 1)
                        if not (first and i < NPT):
                            wait_copied(pe, b, i - NPT)
                        for kt in range(width(it) // P):
                            last = nc.tensor.transpose(ptp[:, i % NPT, kt * P:(kt + 1) * P],
                                                       prob[:, i % NP_, kt * P:(kt + 1) * P], k["ident"][:])
                        last.then_inc(turned, 1)
                    if jj in (7, 9, 11, 13) and not (first and q < 1) and q - 1 < NQUAD:
                        pq, kt = q - 1, (jj - 7) // 2
                        if kt == 0:
                            wait_copied(pe, b, pq * QU + QU - 1)
                            pe.wait_ge(v_in[pq % 2], (2 * b + pq // 2 + 1) * 16 * 4)
                            if not (first and pq < 1):
                                pe.wait_ge(oT_done, b * NQUAD + pq)
                        t0 = 0 if cross else kt
                        for h in range(QUAD):
                            last = nc.tensor.matmul(acc[32 * h:32 * h + 32, t0 * P:S], v[:, pq % 2, h, kt, :],
                                                    pT[:, pq % 2, h, t0:TT, kt, :], start=kt == 0, stop=kt == TT - 1,
                                                    tile_position=(0, 32 * h))
                        if kt == TT - 1:
                            last.then_inc(pv_done, 1)
                    if jj == 1 and not (first and q < 2) and q - 2 < NQUAD:
                        pe.wait_ge(oT_done, b * NQUAD + q - 1)
                        if not (first and q < 3):
                            pe.wait_ge(o_done, b * NQUAD + q - 2)
                        for t_ in range(TT):
                            last = nc.tensor.transpose(otp[:, t_ * P:(t_ + 1) * P], oT[:, t_ * P:(t_ + 1) * P], k["ident"][:])
                        last.then_inc(oturned, 1)

            block.tensor(steps(pe_steps))

            def dve_steps(dve, b, js, first):
                for j in js:
                    q, jj, t = j // QU, j % QU, j % TT
                    if j < UNITS:
                        W = width(t)
                        if cross and j == 0:
                            if first:
                                dve.wait_ge(adj_in, 16)
                            dve.wait_ge(mask_in, b * 16 + 16)
                            for t_ in range(TT):
                                nc.vector.tensor_scalar(fill[:, t_], mask[:, t_], 0, FILL, ALU.is_equal,
                                                        ALU.mult).then_inc(fill_done, 1)
                        if cross and j < TT:
                            dve.wait_ge(fill_done, b * TT + j + 1)
                            nc.vector.scalar_tensor_tensor(bias[:, j], fill[:, j], 1.0, adj[:, j], ALU.mult,
                                                           ALU.add).then_inc(bias_done, 1)
                            dve.wait_ge(bias_done, b * TT + j + 1)
                        if not (first and j < NA):
                            dve.wait_ge(prob_done, b * UNITS + j - NA + 1)
                        wait_apart(dve, k, sc_done, b * UNITS + j + 1)
                        nc.vector.tensor_tensor_reduce(out=neg[:, j % NA, 0:W], in0=sc[:, j % NSC, 0:W],
                                                       in1=bias[:, t, 0:W], scale=-1.0, scalar=HUGE, op0=ALU.add,
                                                       op1=ALU.min, accum_out=nmax[:, j % NM:j % NM + 1]
                                                       ).then_inc(neg_done, 1)
                    i = j - COPY
                    if not (first and i < 0) and i < UNITS and on_dve(i):
                        copy_out(dve, nc.vector.tensor_copy, copied_d, b, i, first)
                    if jj == 3 and not (first and q < 2) and q - 2 < NQUAD:
                        pq = q - 2
                        dve.wait_ge(oturned, b * NQUAD + pq + 1)
                        if not (first and pq < 2):
                            dve.wait_ge(o_out[pq % 2], (2 * b + pq // 2) * 16 * (1 if cross else TT))
                        ov = otp[:].rearrange("p (n e) -> p n e", e=32)
                        rs = rsum[:].rearrange("p t h -> p (t h)")
                        if cross:
                            m0 = (pq * QU) % NM
                            nm = nmax[:, m0:m0 + QU].rearrange("p (h t) -> p t h", t=TT)
                            nc.vector.scalar_tensor_tensor(den[:], nm, -FILL / 2, ov[:, :, HD].rearrange(
                                "p (t h) -> p t h", h=QUAD), ALU.is_lt, ALU.mult).then_inc(den_done, 1)
                            dve.wait_ge(den_done, b * NQUAD + pq + 1)
                            nc.vector.reciprocal(inv[:], den[:]).then_inc(inv_done, 1)
                            dve.wait_ge(inv_done, b * NQUAD + pq + 1)
                            nc.vector.scalar_tensor_tensor(rsum[:], nm, -FILL / 2, inv[:], ALU.is_lt,
                                                           ALU.mult).then_inc(rsum_done, 1)
                        else:
                            nc.vector.reciprocal(rs, ov[:, :, HD]).then_inc(rsum_done, 1)
                        dve.wait_ge(rsum_done, b * NQUAD + pq + 1)
                        nc.vector.tensor_tensor(o[:, pq % 2].rearrange("p t h e -> p (t h) e"), ov[:, :, 0:HD],
                                                rsum[:].rearrange("p t (h o) -> p (t h) o", o=1).broadcast_to([P, TT * QUAD, HD]),
                                                ALU.mult).then_inc(o_done, 1)

            def copy_out(eng, copy, sem, b, i, first):
                iq, ih, it = i // QU, (i % QU) // TT, i % TT
                eng.wait_ge(turned, b * UNITS + i + 1)
                if i % QU < 2 and not (first and iq < 2):
                    eng.wait_ge(pv_done, b * NQUAD + iq - 1)
                W = width(it)
                copy(pT[:, iq % 2, ih, it, 0:W // P].rearrange("p a s -> p (a s)"), ptp[:, i % NPT, 0:W]).then_inc(sem, 1)

            block.vector(steps(dve_steps))

            def act_steps(act, b, js, first):
                for j in js:
                    q, jj, t = j // QU, j % QU, j % TT
                    if j < UNITS:
                        W = width(t)
                        act.wait_ge(neg_done, b * UNITS + j + 1)
                        if not (first and j < NP_):
                            act.wait_ge(turned, b * UNITS + j - NP_ + 1)
                        nc.scalar.activation(prob[:, j % NP_, 0:W], neg[:, j % NA, 0:W], ACT.Exp,
                                             bias=nmax[:, j % NM:j % NM + 1], scale=-1.0).then_inc(prob_done, 1)
                    i = j - COPY
                    if not (first and i < 0) and i < UNITS and not on_dve(i):
                        copy_out(act, nc.scalar.copy, copied_a, b, i, first)
                    if jj == 15 and not (first and q < 1) and q - 1 < NQUAD:
                        act.wait_ge(pv_done, b * NQUAD + q)
                        if not (first and q < 2):
                            act.wait_ge(oturned, b * NQUAD + q - 1)
                        nc.scalar.copy(oT[:], acc[:]).then_inc(oT_done, 1)

            block.scalar(steps(act_steps))
        s.end()




def batch_rows(ap, b):
    return ap.rearrange("(b t p) f -> b p t f", t=TT, p=P)[bass.ds(b, 1)].rearrange("o p t f -> (o p) t f")


def turn_batch(nc, pe, k, dst, src, ready, ready_base, done):
    for t in range(TT):
        if ready is not None:
            pe.wait_ge(ready, ready_base + t + 1)
        for c_ in range(DK):
            last = nc.tensor.transpose(dst[:, c_, t * P:(t + 1) * P], src[:, t, c_ * P:(c_ + 1) * P], k["ident"][:])
    last.then_inc(done, 1)


def project_cross(nc, w, k, scratch):
    with ExitStack() as c:
        s = Scope(nc, c, "pc")
        U = 4
        UNIT = ((1, 0), (1, 1), (0, 0), (0, 1))
        x, o, cx, xn, x1 = (s.sb(n, [P, TT, D]) for n in ("x", "o", "cx", "xn", "x1"))
        oT, cT, xnT = (s.sb(n, [P, DK, S]) for n in ("oT", "cT", "xnT"))
        vv = s.sb("v", [P, TT, D])
        full, rest = s.sb("full", [P, U, S]), s.sb("rest", [P, U, S])
        parts = s.sb("parts", [P, U, 3, S], BF16)
        stats, mv, sd, rstd = (s.sb("stats", [P, TT, 6]), s.sb("mv", [P, TT, 2]), s.sb("sd", [P, TT]),
                               s.sb("rstd", [P, TT]))
        tp, at, qk = s.ps("tp", [P, DK, S]), s.ps("at", [P, TT, D]), s.ps("qk", [P, 2, S])
        vp = s.ps("vp", [P, TT, D])
        (x_in, o_in, cx_in, x1_out, v_out, xb_done, turned, tp_free, at_done, x1_done, stats_done, mv_done, sd_done,
         rstd_done, xn_done, qk_done, full_done, hi_done, rest_done, mid_done, lo_done, vp_done, v_done) = (
            s.sem(n) for n in (
                "x_in", "o_in", "cx_in", "x1_out", "v_out", "xb_done", "turned", "tp_free", "at_done", "x1_done",
                "stats_done", "mv_done", "sd_done", "rstd_done", "xn_done", "qk_done", "full_done", "hi_done",
                "rest_done", "mid_done", "lo_done", "vp_done", "v_done"))
        parts_out = [s.sem(f"parts_out{u}") for u in range(U)]
        xrows = w["x"].rearrange("b s d -> (b s) d")
        crows = w["ctx"].rearrange("b s d -> (b s) d")

        with nc.Block() as block:
            def load(sp, b):
                sp.dma_start(o[:], batch_rows(scratch["o"], b)).then_inc(o_in, 16)
                sp.dma_start(x[:], batch_rows(xrows, b)).then_inc(x_in, 16)
                sp.dma_start(cx[:], batch_rows(crows, b)).then_inc(cx_in, 16)

            @block.sync
            def _(sp):
                load(sp, 0)
                with sp.Fori(1, B) as b:
                    wait_apart(sp, k, turned, b * 3 - 1)
                    sp.wait_ge(x1_done, b * TT)
                    load(sp, b)

            def store_parts(pool, b, u):
                which, g = UNIT[u]
                wait_apart(pool, k, lo_done, b * U + u + 1)
                pool.dma_start(scratch["parts"][bass.ds(b, 1), which, :, g * P:(g + 1) * P].rearrange("o c p s -> (o p) c s"),
                               parts[:, u]).then_inc(parts_out[u], 16)

            @block.gpsimd
            def _(pool):
                def batch(b):
                    pool.wait_ge(x_in, b * 16 + 16)
                    for t in range(TT):
                        nc.gpsimd.tensor_tensor(x[:, t], x[:, t], k["bout"][:], ALU.add).then_inc(xb_done, 1)
                    wait_apart(pool, k, x1_done, b * TT + TT)
                    pool.dma_start(batch_rows(scratch["x1"], b), x1[:]).then_inc(x1_out, 16)
                    for u in range(2):
                        store_parts(pool, b, u)
                    wait_apart(pool, k, v_done, b * TT + TT)
                    pool.dma_start(batch_rows(scratch["v"], b), vv[:]).then_inc(v_out, 16)
                    for u in range(2, U):
                        store_parts(pool, b, u)

                over_batches(pool, batch)
                pool.wait_ge(x1_out, 16 * B)
                pool.wait_ge(v_out, 16 * B)
                for u in range(U):
                    pool.wait_ge(parts_out[u], 16 * B)

            def project_heads(pe, b, u0, srcT):
                for u in (u0, u0 + 1):
                    which, g = UNIT[u]
                    pe.wait_ge(full_done, b * U + u0)
                    for c_ in range(DK):
                        last = nc.tensor.matmul(qk[:, u % 2], k["xw"][:, which, c_, g * P:(g + 1) * P], srcT[:, c_],
                                                start=c_ == 0, stop=c_ == DK - 1)
                    last.then_inc(qk_done, 1)

            @block.tensor
            def _(pe):
                def batch(b):
                    pe.wait_ge(o_in, b * 16 + 16)
                    pe.wait_ge(tp_free, b * 3 * DK)
                    turn_batch(nc, pe, k, tp, o, None, 0, turned)
                    pe.wait_ge(tp_free, b * 3 * DK + DK)
                    pe.wait_ge(x1_done, b * TT)
                    for t in range(TT):
                        for c_ in range(DK):
                            last = nc.tensor.matmul(at[:, t], oT[:, c_, t * P:(t + 1) * P], k["wout"][:, c_],
                                                    start=c_ == 0, stop=c_ == DK - 1)
                        last.then_inc(at_done, 1)
                    pe.wait_ge(cx_in, b * 16 + 16)
                    turn_batch(nc, pe, k, tp, cx, None, 0, turned)
                    pe.wait_ge(tp_free, b * 3 * DK + 2 * DK)
                    project_heads(pe, b, 0, cT)
                    pe.wait_ge(v_done, b * TT)
                    for t in range(TT):
                        for c_ in range(DK):
                            last = nc.tensor.matmul(vp[:, t], cT[:, c_, t * P:(t + 1) * P], k["xw"][:, 2, c_],
                                                    start=c_ == 0, stop=c_ == DK - 1)
                        last.then_inc(vp_done, 1)
                    turn_batch(nc, pe, k, tp, xn, xn_done, b * TT, turned)
                    pe.wait_ge(tp_free, b * 3 * DK + 3 * DK)
                    project_heads(pe, b, 2, xnT)

                over_batches(pe, batch)

            @block.scalar
            def _(act):
                def keep_turned(b, n, dst):
                    act.wait_ge(turned, b * 3 + n + 1)
                    for c_ in range(DK):
                        nc.scalar.copy(dst[:, c_], tp[:, c_]).then_inc(tp_free, 1)

                def full_and_hi(b, u):
                    which, g = UNIT[u]
                    act.wait_ge(qk_done, b * U + u + 1)
                    nc.scalar.activation(full[:, u], qk[:, u % 2], ACT.Identity, bias=k["bqk"][:, which, g:g + 1],
                                         scale=1.0 if which else float(HD) ** -0.5).then_inc(full_done, 1)
                    act.wait_ge(full_done, b * U + u + 1)
                    act.wait_ge(parts_out[u], b * 16)
                    nc.scalar.copy(parts[:, u, 0], full[:, u]).then_inc(hi_done, 1)

                def mid(b, u):
                    act.wait_ge(rest_done, b * U + u + 1)
                    nc.scalar.copy(parts[:, u, 1], rest[:, u]).then_inc(mid_done, 1)

                def batch(b):
                    act.wait_ge(at_done, b * TT)
                    keep_turned(b, 0, oT)
                    act.wait_ge(vp_done, b * TT)
                    keep_turned(b, 1, cT)
                    norm_sqrt(nc, act, k, mv, sd, mv_done, sd_done, b)
                    full_and_hi(b, 0)
                    full_and_hi(b, 1)
                    mid(b, 0)
                    act.wait_ge(qk_done, b * U)
                    keep_turned(b, 2, xnT)
                    mid(b, 1)
                    full_and_hi(b, 2)
                    full_and_hi(b, 3)
                    mid(b, 2)
                    mid(b, 3)

                over_batches(act, batch)

            @block.vector
            def _(dve):
                def split_rest(b, u):
                    dve.wait_ge(hi_done, b * U + u + 1)
                    nc.vector.tensor_tensor(rest[:, u], full[:, u], parts[:, u, 0], ALU.subtract).then_inc(rest_done, 1)

                def split_lo(b, u):
                    dve.wait_ge(mid_done, b * U + u + 1)
                    nc.vector.tensor_tensor(parts[:, u, 2], rest[:, u], parts[:, u, 1], ALU.subtract).then_inc(lo_done, 1)

                def batch(b):
                    for t in range(TT):
                        dve.wait_ge(at_done, b * TT + (t | 1) + 1)
                        dve.wait_ge(xb_done, b * TT + t + 1)
                        dve.wait_ge(x1_out, b * 16)
                        nc.vector.tensor_tensor(x1[:, t], at[:, t], x[:, t], ALU.add).then_inc(x1_done, 1)
                    dve.wait_ge(x1_done, b * TT + TT)
                    norm_stats(nc, dve, k, lambda t: x1[:, t], stats, mv, stats_done, mv_done, b)
                    dve.wait_ge(turned, b * 3)
                    norm_apply(nc, dve, lambda t: x1[:, t], lambda t: xn[:, t], mv, sd, rstd, sd_done, rstd_done,
                               xn_done, b)
                    split_rest(b, 0)
                    split_rest(b, 1)
                    split_lo(b, 0)
                    dve.wait_ge(v_out, b * 16)
                    for t in range(TT):
                        dve.wait_ge(vp_done, b * TT + (t | 1) + 1)
                        nc.vector.tensor_tensor(vv[:, t], vp[:, t], k["bv"][:], ALU.add).then_inc(v_done, 1)
                    split_lo(b, 1)
                    split_rest(b, 2)
                    split_rest(b, 3)
                    split_lo(b, 2)
                    split_lo(b, 3)

                over_batches(dve, batch)
        s.end()


def route(nc, w, k, scratch):
    with ExitStack() as c:
        s = Scope(nc, c, "rt")
        x, o, xn, x2 = (s.sb(n, [P, TT, D]) for n in ("x", "o", "xn", "x2"))
        oT, xnT = (s.sb(n, [P, DK, S]) for n in ("oT", "xnT"))
        stats, mv, sd, rstd = (s.sb("stats", [P, TT, 6]), s.sb("mv", [P, TT, 2]), s.sb("sd", [P, TT]),
                               s.sb("rstd", [P, TT]))
        top, zero1, expg, shift, score, biased, above, equal, s2_, s4_, pick, sel, cw = (
            s.sb(n, [P, TT, NE]) for n in ("top", "zero1", "expg", "shift", "score", "biased", "above", "equal",
                                           "s2", "s4", "pick", "sel", "cw"))
        c0, c1, c2 = (s.sb(n, [P, TT, 2 * NE]) for n in ("c0", "c1", "c2"))
        gmax, gsum, ginv, nabove, need = (s.sb(n, [P, TT]) for n in ("gmax", "gsum", "ginv", "nabove", "need"))
        cwT = s.sb("cwT", [NE, S])
        ones = s.sb("ones", [1, B * S])
        tp, at, gp, ctp = (s.ps("tp", [P, DK, S]), s.ps("at", [P, TT, D]), s.ps("gp", [P, S]), s.ps("ctp", [P, S]))
        (x_in, o_in, x2_out, xnT_out, cw_out, ones_out, ones_done, xb_done, turned, tp_free, at_done, x2_done,
         stats_done, mv_done, sd_done, rstd_done, xn_done, gate_done, exp_done, g_step, cw_done, cturned,
         cwT_done, zeroed) = (
            s.sem(n) for n in (
                "x_in", "o_in", "x2_out", "xnT_out", "cw_out", "ones_out", "ones_done", "xb_done", "turned", "tp_free",
                "at_done", "x2_done", "stats_done", "mv_done", "sd_done", "rstd_done", "xn_done", "gate_done",
                "exp_done", "g_step", "cw_done", "cturned", "cwT_done", "zeroed"))
        GATE_STEPS = 16
        xnT_dram = scratch["xnT"]
        cw_dram = scratch["cw"]

        with nc.Block() as block:
            def load(sp, b):
                sp.dma_start(o[:], batch_rows(scratch["o"], b)).then_inc(o_in, 16)
                sp.dma_start(x[:], batch_rows(scratch["x1"], b)).then_inc(x_in, 16)

            @block.sync
            def _(sp):
                load(sp, 0)
                sp.wait_ge(ones_done, 1)
                sp.dma_start(cw_dram[NE:NE + 1], ones[:]).then_inc(ones_out, 16)
                with sp.Fori(1, B) as b:
                    wait_apart(sp, k, turned, b * 2 - 1)
                    sp.wait_ge(x2_done, b * TT)
                    load(sp, b)
                sp.wait_ge(ones_out, 16)

            @block.gpsimd
            def _(pool):
                nc.gpsimd.memset(ones[:], 1.0).then_inc(ones_done, 1)
                def batch(b):
                    pool.wait_ge(x_in, b * 16 + 16)
                    for t in range(TT):
                        nc.gpsimd.tensor_tensor(x[:, t], x[:, t], k["bo"][:], ALU.add).then_inc(xb_done, 1)
                    wait_apart(pool, k, x2_done, b * TT + TT)
                    pool.dma_start(batch_rows(scratch["x2"], b), x2[:]).then_inc(x2_out, 16)
                    wait_apart(pool, k, tp_free, b * 2 * DK + 2 * DK)
                    pool.dma_start(xnT_dram[bass.ds(b, 1)].rearrange("o p c s -> (o p) c s"), xnT[:]).then_inc(xnT_out, 16)
                    wait_apart(pool, k, cwT_done, b + 1)
                    pool.dma_start(cw_dram[0:NE].rearrange("e (b s) -> b e s", b=B)[bass.ds(b, 1)].rearrange("o e s -> (o e) s"),
                                   cwT[:]).then_inc(cw_out, 16)

                over_batches(pool, batch)
                for q in (x2_out, xnT_out, cw_out):
                    pool.wait_ge(q, 16 * B)

            @block.tensor
            def _(pe):
                def batch(b):
                    pe.wait_ge(o_in, b * 16 + 16)
                    pe.wait_ge(tp_free, b * 2 * DK)
                    turn_batch(nc, pe, k, tp, o, None, 0, turned)
                    pe.wait_ge(tp_free, b * 2 * DK + DK)
                    pe.wait_ge(x2_done, b * TT)
                    for t in range(TT):
                        for c_ in range(DK):
                            last = nc.tensor.matmul(at[:, t], oT[:, c_, t * P:(t + 1) * P], k["xw"][:, 3, c_],
                                                    start=c_ == 0, stop=c_ == DK - 1)
                        last.then_inc(at_done, 1)
                    turn_batch(nc, pe, k, tp, xn, xn_done, b * TT, turned)
                    pe.wait_ge(tp_free, b * 2 * DK + 2 * DK)
                    for t in range(TT):
                        for c_ in range(DK):
                            last = nc.tensor.matmul(gp[:, t * NE:(t + 1) * NE], xnT[:, c_, t * P:(t + 1) * P],
                                                    k["gateT"][:, c_], start=c_ == 0, stop=c_ == DK - 1)
                    last.then_inc(gate_done, 1)
                    pe.wait_ge(cw_done, b + 1)
                    for t in range(TT):
                        last = nc.tensor.transpose(ctp[0:NE, t * P:(t + 1) * P], cw[:, t], k["ident"][:])
                    last.then_inc(cturned, 1)

                over_batches(pe, batch)

            @block.scalar
            def _(act):
                def batch(b):
                    act.wait_ge(turned, b * 2 + 1)
                    for c_ in range(DK):
                        nc.scalar.copy(oT[:, c_], tp[:, c_]).then_inc(tp_free, 1)
                    norm_sqrt(nc, act, k, mv, sd, mv_done, sd_done, b)
                    act.wait_ge(turned, b * 2 + 2)
                    act.wait_ge(xnT_out, b * 16)
                    for c_ in range(DK):
                        nc.scalar.copy(xnT[:, c_], tp[:, c_]).then_inc(tp_free, 1)
                    act.wait_ge(g_step, b * GATE_STEPS + 2)
                    nc.scalar.activation(expg[:], shift[:], ACT.Exp).then_inc(exp_done, 1)

                over_batches(act, batch)

            @block.vector
            def _(dve):
                for z in (c0, c1, c2):
                    nc.vector.memset(z[:], 0.0).then_inc(zeroed, 1)
                dve.wait_ge(zeroed, 3)

                def batch(b):
                    for t in range(TT):
                        dve.wait_ge(at_done, b * TT + (t | 1) + 1)
                        dve.wait_ge(xb_done, b * TT + t + 1)
                        dve.wait_ge(x2_out, b * 16)
                        nc.vector.tensor_tensor(x2[:, t], at[:, t], x[:, t], ALU.add).then_inc(x2_done, 1)
                    dve.wait_ge(x2_done, b * TT + TT)
                    norm_stats(nc, dve, k, lambda t: x2[:, t], stats, mv, stats_done, mv_done, b)
                    norm_apply(nc, dve, lambda t: x2[:, t], lambda t: xn[:, t], mv, sd, rstd, sd_done, rstd_done,
                               xn_done, b)
                    steps = [0]

                    def then(ins):
                        steps[0] += 1
                        ins.then_inc(g_step, 1)
                        wait_apart(dve, k, g_step, b * GATE_STEPS + steps[0])

                    def wide(a):
                        return a.rearrange("p (t o) -> p t o", o=1).broadcast_to([P, TT, NE])

                    dve.wait_ge(gate_done, b + 1)
                    logits = gp[:, 0:TT * NE].rearrange("p (t e) -> p t e", e=NE)
                    then(nc.vector.tensor_reduce(gmax[:], logits, AX_X, ALU.max))
                    then(nc.vector.tensor_tensor(shift[:], logits, wide(gmax[:]), ALU.subtract))
                    dve.wait_ge(exp_done, b + 1)
                    then(nc.vector.tensor_reduce(gsum[:], expg[:], AX_X, ALU.add))
                    then(nc.vector.reciprocal(ginv[:], gsum[:]))
                    then(nc.vector.tensor_tensor(score[:], expg[:], wide(ginv[:]), ALU.mult))
                    then(nc.vector.tensor_tensor(biased[:], score[:], k["gateb"][:].rearrange(
                        "p (o e) -> p o e", o=1).broadcast_to([P, TT, NE]), ALU.add))
                    for t in range(TT):
                        last = nc.vector.max(top[:, t], biased[:, t])
                    then(last)
                    second = top[:, :, 1:2].broadcast_to([P, TT, NE])
                    then(nc.vector.tensor_tensor(above[:], biased[:], second, ALU.is_gt))
                    then(nc.vector.tensor_tensor(c0[:, :, NE:], biased[:], second, ALU.is_equal))
                    then(nc.vector.tensor_reduce(nabove[:], above[:], AX_X, ALU.add))
                    then(nc.vector.tensor_tensor(c1[:, :, NE:], c0[:, :, NE:], c0[:, :, NE - 1:2 * NE - 1], ALU.add))
                    then(nc.vector.tensor_tensor(c2[:, :, NE:], c1[:, :, NE:], c1[:, :, NE - 2:2 * NE - 2], ALU.add))
                    then(nc.vector.tensor_tensor(s4_[:], c2[:, :, NE:], c2[:, :, NE - 4:2 * NE - 4], ALU.add))
                    then(nc.vector.tensor_tensor(s2_[:], s4_[:], wide(nabove[:]), ALU.add))
                    then(nc.vector.scalar_tensor_tensor(pick[:], s2_[:], 2.0, c0[:, :, NE:], ALU.is_le, ALU.mult))
                    then(nc.vector.tensor_tensor(sel[:], above[:], pick[:], ALU.add))
                    nc.vector.tensor_tensor(cw[:], sel[:], score[:], ALU.mult).then_inc(cw_done, 1)
                    assert steps[0] == GATE_STEPS
                    dve.wait_ge(cturned, b + 1)
                    dve.wait_ge(cw_out, b * 16)
                    nc.vector.tensor_copy(cwT[:], ctp[0:NE, :]).then_inc(cwT_done, 1)

                over_batches(dve, batch)
        s.end()


def experts(nc, w, k, scratch, out):
    NX = NE + 1
    MF = FF // P
    ALPHA, LIMIT = 1.702, 7.0
    with ExitStack() as c:
        s = Scope(nc, c, "ex")
        w13 = s.sb("w13", [P, NX, 2, DK, 2 * FF])
        w2 = s.sb("w2", [P, NX, MF, D])
        b13 = s.sb("b13", [P, NX, 2, MF, 2])
        b2 = s.sb("b2", [NX, D])
        with ExitStack() as cw_:
            sw = Scope(nc, cw_, "ew")
            raw13 = sw.sb("raw13", [P, 2, 2, MF, 2, D])
            raw2 = sw.sb("raw2", [P, 2, DK, FF])
            tp = sw.ps("tp", [P, 8, S])
            raw_in = [sw.sem(f"raw_in{i}") for i in range(2)]
            small_in, turned, copied_a, copied_d = (sw.sem(n) for n in ("small_in", "turned", "copied_a", "copied_d"))
            G = 6
            with nc.Block() as block:
                def src(name, e):
                    if e < NE:
                        return w[name][e]
                    return w["s" + name]

                @block.sync
                def _(sp):
                    for e in range(NX):
                        for n, name in enumerate(("b1", "b3")):
                            sp.dma_start(b13[:, e, n], src(name, e).rearrange("(m p two) -> p m two", p=P, two=2),
                                         allow_slow_non_contiguous=True).then_inc(small_in, 16)
                    sp.dma_start(b2[0:NE], w["b2"]).then_inc(small_in, 16)
                    sp.dma_start(b2[NE:NX], w["sb2"].rearrange("(o d) -> o d", o=1)).then_inc(small_in, 16)
                    sp.wait_ge(small_in, 16 * (2 * NX + 2))

                @block.gpsimd
                def _(pool):
                    for e in range(NX):
                        if e >= 2:
                            pool.wait_ge(turned, G * (e - 1))
                        for n, name in enumerate(("w1", "w3")):
                            pool.dma_start(raw13[:, e % 2, n], src(name, e).rearrange("(m p two) d -> p m two d", p=P, two=2)
                                           ).then_inc(raw_in[e % 2], 16)
                        pool.dma_start(raw2[:, e % 2], src("w2", e).rearrange("(c p) f -> p c f", p=P)
                                       ).then_inc(raw_in[e % 2], 16)

                @block.tensor
                def _(pe):
                    for e in range(NX):
                        pe.wait_ge(raw_in[e % 2], 48 * (e // 2 + 1))
                        for g in range(G):
                            n = e * G + g
                            if n >= 8:
                                m_ = n - 8
                                pe.wait_ge(copied_d if m_ % 2 == 0 else copied_a, m_ // 2 + 1)
                            for i in range(4):
                                if g < 4:
                                    a = raw13[:, e % 2, g // 2, i // 2, i % 2, (g % 2) * P:(g % 2 + 1) * P]
                                elif True:
                                    fk = g - 4
                                    if i >= DK:
                                        break
                                    a = raw2[:, e % 2, i, fk * P:(fk + 1) * P]
                                last = nc.tensor.transpose(tp[:, n % 8, i * P:(i + 1) * P], a, k["ident"][:])
                            last.then_inc(turned, 1)

                def copies(eng, copy, side, sem):
                    for e in range(NX):
                        for g in range(G):
                            n = e * G + g
                            if n % 2 != side:
                                continue
                            eng.wait_ge(turned, n + 1)
                            if g < 4:
                                copy(w13[:, e, g // 2, g % 2], tp[:, n % 8]).then_inc(sem, 1)
                            else:
                                copy(w2[:, e, g - 4], tp[:, n % 8, 0:D]).then_inc(sem, 1)

                @block.vector
                def _(dve):
                    copies(dve, nc.vector.tensor_copy, 0, copied_d)

                @block.scalar
                def _(act):
                    copies(act, nc.scalar.copy, 1, copied_a)
            sw.end()

        xT = s.sb("xT", [P, DK, S])
        cwT = s.sb("cwT", [NX, S])
        cwb = s.sb("cwb", [P, NE, S])
        h1b = s.sb("h1b", [P, 2, S])
        hh = s.sb("hh", [P, 2, S])
        g, sg, gs, l, aw, a = (s.sb(n, [P, 2, S]) for n in ("g", "sg", "gs", "l", "aw", "a"))
        ysb = s.sb("ysb", [P, DK, S])
        x2 = s.sb("x2", [P, TT, D])
        res = s.sb("res", [P, TT, D])
        hp, y, yt = s.ps("hp", [P, 2, 2, S]), s.ps("y", [P, DK, S]), s.ps("yt", [P, TT, D])
        cwb_in = [s.sem(f"cwb_in{e}") for e in range(NE)]
        (xT_in, cwT_in, x2_in, out_done, h_done, h1b_done, hh_done, g_done, sg_done, gs_done, l_done, aw_done, a_done,
         y_done, ysb_done, yturned, res_done, yused) = (s.sem(n) for n in (
             "xT_in", "cwT_in", "x2_in", "out_done", "h_done", "h1b_done", "hh_done", "g_done", "sg_done", "gs_done",
             "l_done", "aw_done", "a_done", "y_done", "ysb_done", "yturned", "res_done", "yused"))
        PAIRS = NX * MF
        HALVES = 2 * PAIRS
        orow = out.rearrange("b s d -> (b s) d")
        cw_dram = scratch["cw"].rearrange("e (b s) -> b e s", b=B)

        with nc.Block() as block:
            @block.sync
            def _(sp):
                def chunk(b):
                    sp.wait_ge(y_done, b)
                    sp.dma_start(xT[:], scratch["xnT"][bass.ds(b, 1)].rearrange("o p c s -> (o p) c s")).then_inc(xT_in, 16)
                    sp.dma_start(cwT[:], cw_dram[bass.ds(b, 1)].rearrange("o e s -> (o e) s")).then_inc(cwT_in, 16)
                    for e in range(NE):
                        sp.dma_start(cwb[:, e], cw_dram[bass.ds(b, 1), e].broadcast_to([P, S])).then_inc(cwb_in[e], 16)
                    sp.wait_ge(res_done, b * 2)
                    sp.dma_start(x2[:], batch_rows(scratch["x2"], b)).then_inc(x2_in, 16)
                    sp.wait_ge(res_done, b * 2 + 2)
                    sp.dma_start(batch_rows(orow, b), res[:]).then_inc(out_done, 16)

                over_batches(sp, chunk)
                sp.wait_ge(out_done, 16 * B)

            @block.tensor
            def _(pe):
                def down(b, e, m):
                    n = e * MF + m
                    if e < NE:
                        pe.wait_ge(a_done, b * NE * MF + n + 1)
                        act_in = a[:, n % 2]
                    else:
                        pe.wait_ge(aw_done, b * PAIRS + n + 1)
                        act_in = aw[:, n % 2]
                    for c_ in range(DK):
                        last = nc.tensor.matmul(y[:, c_], w2[:, e, m, c_ * P:(c_ + 1) * P], act_in,
                                                start=False, stop=n == PAIRS - 1)
                    last.then_inc(y_done if n == PAIRS - 1 else yused, 1)

                def chunk(b):
                    pe.wait_ge(xT_in, b * 16 + 16)
                    pe.wait_ge(cwT_in, b * 16 + 16)
                    pe.wait_ge(ysb_done, b * DK)
                    for c_ in range(DK):
                        nc.tensor.matmul(y[:, c_], b2[:, c_ * P:(c_ + 1) * P], cwT[:], start=True, stop=False)
                    for e in range(NX):
                        for m in range(MF):
                            for par in range(2):
                                u = (e * MF + m) * 2 + par
                                pe.wait_ge(hh_done, b * HALVES + max(0, u - 1) if u >= 2 else b * HALVES)
                                for n in range(2):
                                    for c_ in range(DK):
                                        f0 = (m * 2 + par) * P
                                        last = nc.tensor.matmul(hp[:, u % 2, n], w13[:, e, n, c_, f0:f0 + P], xT[:, c_],
                                                                start=c_ == 0, stop=c_ == DK - 1)
                                last.then_inc(h_done, 1)
                            if e * MF + m >= 1:
                                n = e * MF + m - 1
                                down(b, n // MF, n % MF)
                    down(b, NX - 1, MF - 1)
                    pe.wait_ge(ysb_done, b * DK + DK)
                    pe.wait_ge(res_done, b * 2)
                    for t in range(TT):
                        for c_ in range(DK):
                            last = nc.tensor.transpose(yt[:, t, c_ * P:(c_ + 1) * P], ysb[:, c_, t * P:(t + 1) * P],
                                                       k["ident"][:])
                    last.then_inc(yturned, 1)

                over_batches(pe, chunk)

            @block.scalar
            def _(act):
                def batch(b):
                    for n in range(PAIRS):
                        e, m = n // MF, n % MF
                        for par in range(2):
                            u = 2 * n + par
                            act.wait_ge(h_done, b * HALVES + u + 1)
                            act.wait_ge(hh_done, b * HALVES + (u - 1 if u >= 2 else 0))
                            nc.scalar.activation(h1b[:, u % 2], hp[:, u % 2, 0], ACT.Identity,
                                                 bias=b13[:, e, 0, m, par:par + 1]).then_inc(h1b_done, 1)
                        act.wait_ge(g_done, b * PAIRS + n + 1)
                        act.wait_ge(gs_done, b * PAIRS + (n - 1 if n >= 2 else 0))
                        nc.scalar.activation(sg[:, n % 2], g[:, n % 2], ACT.Sigmoid, scale=ALPHA).then_inc(sg_done, 1)
                    act.wait_ge(y_done, b + 1)
                    act.wait_ge(yturned, b)
                    for c_ in range(DK):
                        nc.scalar.copy(ysb[:, c_], y[:, c_]).then_inc(ysb_done, 1)

                over_batches(act, batch)

            @block.vector
            def _(dve):
                def chunk(b):
                    for n in range(PAIRS):
                        e, m = n // MF, n % MF
                        for par in range(2):
                            u = 2 * n + par
                            dve.wait_ge(h1b_done, b * HALVES + u + 1)
                            nc.vector.scalar_tensor_tensor(hh[:, par], hp[:, u % 2, 1], b13[:, e, 1, m, par:par + 1],
                                                           h1b[:, u % 2], ALU.add, ALU.mult).then_inc(hh_done, 1)
                            dve.wait_ge(hh_done, b * HALVES + u + 1)
                            if par == 0:
                                nc.vector.tensor_scalar(g[:, n % 2], hh[:, 0], LIMIT, None, ALU.min).then_inc(g_done, 1)
                            else:
                                nc.vector.tensor_scalar(l[:, n % 2], hh[:, 1], LIMIT, -LIMIT, ALU.min,
                                                        ALU.max).then_inc(l_done, 1)
                        dve.wait_ge(sg_done, b * PAIRS + n + 1)
                        nc.vector.tensor_tensor(gs[:, n % 2], g[:, n % 2], sg[:, n % 2], ALU.mult).then_inc(gs_done, 1)
                        dve.wait_ge(l_done, b * PAIRS + n + 1)
                        dve.wait_ge(gs_done, b * PAIRS + n + 1)
                        if n >= 2:
                            dve.wait_ge(a_done, b * NE * MF + min(n - 1, NE * MF))
                        else:
                            dve.wait_ge(a_done, b * NE * MF)
                            dve.wait_ge(y_done, b)
                        nc.vector.scalar_tensor_tensor(aw[:, n % 2], l[:, n % 2], 1.0, gs[:, n % 2], ALU.add,
                                                       ALU.mult).then_inc(aw_done, 1)
                    dve.wait_ge(yturned, b + 1)
                    dve.wait_ge(x2_in, b * 16 + 16)
                    dve.wait_ge(out_done, b * 16)
                    for i in range(2):
                        nc.vector.tensor_tensor(res[:, 2 * i:2 * i + 2], yt[:, 2 * i:2 * i + 2], x2[:, 2 * i:2 * i + 2],
                                                ALU.add).then_inc(res_done, 1)

                over_batches(dve, chunk)

            @block.gpsimd
            def _(pool):
                def batch(b):
                    for n in range(NE * MF):
                        e = n // MF
                        pool.wait_ge(aw_done, b * PAIRS + n + 1)
                        if n % MF == 0:
                            pool.wait_ge(cwb_in[e], b * 16 + 16)
                        pool.wait_ge(yused, b * (PAIRS - 1) + (n - 1 if n >= 2 else 0))
                        nc.gpsimd.tensor_tensor(a[:, n % 2], aw[:, n % 2], cwb[:, e], ALU.mult).then_inc(a_done, 1)

                over_batches(pool, batch)
        s.end()


def decoder_layer(nc, w, out):
    def dram(name, shape, dt=F32):
        return nc.dram_tensor(name, shape, dt).ap()

    scratch = {
        "qkv": dram("scratch_qkv", [B * HEADS * S, 3 * HD]),
        "parts": dram("scratch_parts", [B, 2, 3, D, S], BF16),
        "o": dram("scratch_o", [B * S, D]),
        "x1": dram("scratch_x1", [B * S, D]),
        "v": dram("scratch_v", [B * S, D]),
        "x2": dram("scratch_x2", [B * S, D]),
        "xnT": dram("scratch_xnT", [B, P, DK, S]),
        "cw": dram("scratch_cw", [NE + 1, B * S]),
    }
    k = {}
    with ExitStack() as ctx:
        prepare_weights(nc, ctx, w, k)
        project_self(nc, w, k, scratch)
        split_self(nc, w, k, scratch)
        attention(nc, w, k, scratch, cross=False)
        project_cross(nc, w, k, scratch)
        attention(nc, w, k, scratch, cross=True)
        route(nc, w, k, scratch)
        experts(nc, w, k, scratch, out)


_INS = {
    "x": "x", "ctx_1024": "ctx", "mask_Bx1xSxS2_ik1": "mask",
    "L0_attn_W_qkv": "W_qkv", "L0_attn_b_qkv": "b_qkv", "L0_attn_W_out": "W_out", "L0_attn_b_out": "b_out",
    "L0_xattn_adj": "adj", "L0_xattn_Wq": "Wq", "L0_xattn_bq": "bq", "L0_xattn_Wk": "Wk", "L0_xattn_bk": "bk",
    "L0_xattn_Wv": "Wv", "L0_xattn_bv": "bv", "L0_xattn_Wo": "Wo", "L0_xattn_bo": "bo",
    "L0_ffn_gate_w": "gate_w", "L0_ffn_gate_b": "gate_b", "L0_ffn_w1": "w1", "L0_ffn_b1": "b1", "L0_ffn_w3": "w3",
    "L0_ffn_b3": "b3", "L0_ffn_w2": "w2", "L0_ffn_b2": "b2", "L0_ffn_sw1": "sw1", "L0_ffn_sb1": "sb1",
    "L0_ffn_sw3": "sw3", "L0_ffn_sb3": "sb3", "L0_ffn_sw2": "sw2", "L0_ffn_sb2": "sb2",
}


def kernel(**inputs):
    import numpy as _np
    import concourse.bacc as _bacc
    from concourse import mybir as _mybir
    from concourse.bass_utils import run_bass_kernel_spmd as _run

    nc = _bacc.Bacc("TRN2", target_bir_lowering=False, num_devices=1)
    arrays, w = {}, {}
    for name, short in _INS.items():
        a = _np.ascontiguousarray(inputs[name])
        arrays[f"in_{name}_dram"] = a
        w[short] = nc.dram_tensor(f"in_{name}_dram", a.shape, _mybir.dt.from_np(a.dtype), kind="ExternalInput").ap()
    out = nc.dram_tensor("out_dram", (B, S, D), F32, kind="ExternalOutput").ap()
    decoder_layer(nc, w, out)
    r = _run(nc, [arrays], core_ids=[0])
    return r.results[0]["out_dram"]
```

```python
from contextlib import ExitStack

import concourse.bass as bass
from concourse import mybir

ALU = mybir.AluOpType
ACT = mybir.ActivationFunctionType
F32 = mybir.dt.float32
BF16 = mybir.dt.bfloat16
I32 = mybir.dt.int32
U32 = mybir.dt.uint32
AX_X = mybir.AxisListType.X

P = 128
B, S, D = 8, 512, 256
HEADS, HD = 16, 16
TT = S // P
DK = D // P
NE = 8
TOPK = 2
NX = NE + 1
FF = 256
MF = FF // P
ROUTED = -(-((TOPK * B * S + NE * (P - 1)) // P) // TT) * TT
NTILES = B * TT + ROUTED
ROW = D + 4
QUAD = 4
NQUAD = HEADS // QUAD
UNITS = HEADS * TT
Q_SLOTS = (0, 1, 2, 0, 1, 0)
K_SLOTS = (0, 0, 0, 1, 1, 2)
NS = len(Q_SLOTS)
EPS = 1e-5
FILL = -1e30
HUGE = 3e38


class Scope:

    def __init__(self, nc, ctx, tag):
        self.nc, self.ctx, self.tag = nc, ctx, tag
        self.sems = []

    def sb(self, name, shape, dt=F32):
        return self.ctx.enter_context(self.nc.sbuf_tensor(f"{self.tag}_{name}", shape, dt))

    def ps(self, name, shape, dt=F32):
        return self.ctx.enter_context(self.nc.psum_tensor(f"{self.tag}_{name}", shape, dt))

    def sem(self, name):
        self.sems.append(self.nc.alloc_semaphore(name=f"{self.tag}_{name}"))
        return self.sems[-1]

    def end(self):
        self.nc.clear_and_free_semaphores(self.sems)
        self.nc.all_engine_barrier()


def wait_apart(eng, k, sem, value):
    eng.wait_ge(sem, value)
    eng.sem_inc(k["passed"], 1)


def over_batches(eng, body, n=B):
    body(0)
    with eng.Fori(1, n) as b:
        body(b)


def prepare_weights(nc, ctx, early, w, k):
    keep = Scope(nc, ctx, "k")
    k["passed"] = keep.sem("passed")
    k["ident"] = keep.sb("ident", [P, P])
    k["sel"], k["cw"] = keep.sb("sel", [P, B * TT, NE]), keep.sb("cw", [P, B * TT, NE])
    k["slots"], k["cw2"] = keep.sb("slots", [P, 2, B * TT], U32), keep.sb("cw2", [P, 2, B * TT])
    k["eidx"] = keep.sb("eidx", [P, NTILES + 8], I32)
    keep = Scope(nc, early, "ke")
    k["identb"] = keep.sb("identb", [P, P], BF16)
    k["eps"] = keep.sb("eps", [P, 1])
    k["causal"] = keep.sb("causal", [P, TT, S])
    k["wqkv"] = keep.sb("wqkv", [P, DK, 3 * D])
    k["bqkv"] = keep.sb("bqkv", [P, 3 * D])
    k["wout"] = keep.sb("wout", [P, DK, D])
    k["bout"] = keep.sb("bout", [P, D])
    k["xw"] = keep.sb("xw", [P, 4, DK, D])
    k["bqk"] = keep.sb("bqk", [P, 2, DK])
    k["bv"] = keep.sb("bv", [P, D])
    k["bo"] = keep.sb("bo", [P, D])
    k["gateT"] = keep.sb("gateT", [P, DK, NE])
    k["gateb"] = keep.sb("gateb", [P, NE])
    with ExitStack() as c:
        s = Scope(nc, c, "pw")
        raw = s.sb("raw", [P, 4, DK, D])
        graw = s.sb("graw", [NE, D])
        bq = s.sb("bq", [P, 3 * D])
        tp = s.ps("tp", [P, 4, S])
        tg = s.ps("tg", [P, S])
        loaded, ident_z, ident_1, ident_ok, identb_ok = (s.sem(n) for n in (
            "loaded", "ident_z", "ident_1", "ident_ok", "identb_ok"))
        turned, scaled, kept, causal_0, causal_1 = (s.sem(n) for n in (
            "turned", "scaled", "kept", "causal_0", "causal_1"))
        with nc.Block() as block:
            @block.sync
            def _(sp):
                sp.dma_start(k["wqkv"][:], w["W_qkv"].rearrange("(c p) f -> p c f", p=P)).then_inc(loaded, 16)
                sp.dma_start(k["wout"][:], w["W_out"].rearrange("(c p) f -> p c f", p=P)).then_inc(loaded, 16)
                for n, name in enumerate(("Wq", "Wk", "Wv", "Wo")):
                    sp.dma_start(raw[:, n], w[name].rearrange("(c p) e -> p c e", p=P)).then_inc(loaded, 16)
                sp.dma_start(graw[:], w["gate_w"]).then_inc(loaded, 16)
                for dst, name in ((bq, "b_qkv"), (k["bout"], "b_out"), (k["bv"], "bv"), (k["bo"], "bo"),
                                  (k["gateb"], "gate_b")):
                    n = w[name].shape[0]
                    sp.dma_start(dst[:], w[name].rearrange("(o f) -> o f", o=1).broadcast_to([P, n])).then_inc(loaded, 16)
                for n, name in enumerate(("bq", "bk")):
                    sp.dma_start(k["bqk"][:, n], w[name].rearrange("(c p) -> p c", p=P),
                                 allow_slow_non_contiguous=True).then_inc(loaded, 16)
                sp.wait_ge(loaded, 14 * 16)

            @block.gpsimd
            def _(pool):
                nc.gpsimd.memset(k["ident"][:], 0.0).then_inc(ident_z, 1)
                nc.gpsimd.memset(k["causal"][:], 0.0).then_inc(causal_0, 1)
                pool.wait_ge(ident_z, 1)
                nc.gpsimd.affine_select(out=k["ident"][:], in_=k["ident"][:], compare_op=ALU.not_equal, fill=1.0,
                                        base=0, pattern=[[-1, P]], channel_multiplier=1).then_inc(ident_ok, 1)
                pool.wait_ge(causal_0, 1)
                nc.gpsimd.affine_select(out=k["causal"][:], in_=k["causal"][:], compare_op=ALU.is_ge,
                                        fill=FILL, base=0, pattern=[[P, TT], [-1, S]],
                                        channel_multiplier=1).then_inc(causal_1, 1)
                pool.wait_ge(causal_1, 1)

            @block.tensor
            def _(pe):
                pe.wait_ge(loaded, 14 * 16)
                pe.wait_ge(ident_ok, 1)
                for n in range(4):
                    for ek in range(DK):
                        for fk in range(DK):
                            last = nc.tensor.transpose(tp[:, n, (ek * DK + fk) * P:(ek * DK + fk + 1) * P],
                                                       raw[:, n, fk, ek * P:(ek + 1) * P], k["ident"][:])
                    last.then_inc(turned, 1)
                for ek in range(DK):
                    last = nc.tensor.transpose(tg[:, ek * NE:(ek + 1) * NE], graw[:, ek * P:(ek + 1) * P],
                                               k["ident"][0:NE, 0:NE])
                last.then_inc(turned, 1)

            @block.vector
            def _(dve):
                nc.vector.memset(k["eps"][:], EPS).then_inc(kept, 1)
                dve.wait_ge(ident_ok, 1)
                nc.vector.tensor_copy(k["identb"][:], k["ident"][:]).then_inc(identb_ok, 1)
                dve.wait_ge(loaded, 14 * 16)
                sc = float((2 * D) ** -0.5)
                wq = k["wqkv"][:].rearrange("p c (n f) -> p (c n) f", f=3 * HD)[:, :, 0:HD]
                nc.vector.tensor_scalar(wq, wq, sc, None, ALU.mult).then_inc(scaled, 1)
                nc.vector.tensor_copy(k["bqkv"][:], bq[:]).then_inc(scaled, 1)
                dve.wait_ge(scaled, 2)
                bqs = k["bqkv"][:].rearrange("p (n f) -> p n f", f=3 * HD)[:, :, 0:HD]
                nc.vector.tensor_scalar(bqs, bqs, sc, None, ALU.mult).then_inc(scaled, 1)
                nc.vector.tensor_scalar(k["bqk"][:, 0], k["bqk"][:, 0], float(HD) ** -0.5, None,
                                        ALU.mult).then_inc(scaled, 1)
                for n in range(4):
                    dve.wait_ge(turned, n + 1)
                    nc.vector.tensor_copy(k["xw"][:, n].rearrange("p c f -> p (c f)"), tp[:, n]).then_inc(kept, 1)
                dve.wait_ge(turned, 5)
                nc.vector.tensor_copy(k["gateT"][:].rearrange("p c e -> p (c e)"), tg[:, 0:DK * NE]).then_inc(kept, 1)
                dve.wait_ge(kept, 6)
                dve.wait_ge(scaled, 4)
                dve.wait_ge(identb_ok, 1)
        s.end()


def norm_stats(nc, dve, k, x_of, stats, mv, stats_done, mv_done, b):
    for t in range(TT):
        last = nc.vector.bn_stats(stats[:, t], x_of(t))
    last.then_inc(stats_done, 1)
    wait_apart(dve, k, stats_done, b + 1)
    for t in range(TT):
        last = nc.vector.bn_aggr(mv[:, t], stats[:, t])
    last.then_inc(mv_done, 1)


def norm_sqrt(nc, act, k, mv, sd, mv_done, sd_done, b):
    act.wait_ge(mv_done, b + 1)
    nc.scalar.activation(sd[:], mv[:, :, 1], ACT.Sqrt, bias=k["eps"][:]).then_inc(sd_done, 1)


def norm_apply(nc, dve, x_of, xn_of, mv, sd, rstd, sd_done, rstd_done, xn_done, b):
    dve.wait_ge(sd_done, b + 1)
    nc.vector.reciprocal(rstd[:], sd[:]).then_inc(rstd_done, 1)
    dve.wait_ge(rstd_done, b + 1)
    for t in range(TT):
        nc.vector.tensor_scalar(xn_of(t), x_of(t), mv[:, t, 0:1], rstd[:, t:t + 1],
                                ALU.subtract, ALU.mult).then_inc(xn_done, 1)


def project_self(nc, w, k, scratch):
    with ExitStack() as c:
        s = Scope(nc, c, "ps")
        x = s.sb("x", [P, TT, D])
        xn = s.sb("xn", [P, TT, D])
        xnT = s.sb("xnT", [P, DK, S])
        stats, mv, sd, rstd = s.sb("stats", [P, TT, 6]), s.sb("mv", [P, TT, 2]), s.sb("sd", [P, TT]), s.sb("rstd", [P, TT])
        qkv = s.sb("qkv", [P, TT, 3 * D])
        tp = s.ps("tp", [P, DK, S])
        acc = s.ps("acc", [P, 2, 2 * S])
        x_in = [s.sem(f"x_in{t}") for t in range(TT)]
        stored = [s.sem(f"stored{t}") for t in range(TT)]
        stats_done, mv_done, sd_done, rstd_done, xn_done, turned, xnT_done, acc_done, qkv_done = (s.sem(n) for n in (
            "stats_done", "mv_done", "sd_done", "rstd_done", "xn_done", "turned", "xnT_done", "acc_done", "qkv_done"))
        xr = w["x"].rearrange("b (t p) d -> b t p d", p=P)
        out = scratch["qkv"].rearrange("(b t p r) f -> b t p (r f)", t=TT, p=P, r=HEADS)

        with nc.Block() as block:
            def load(sp, b):
                for t in range(TT):
                    sp.dma_start(x[:, t], xr[bass.ds(b, 1), t].rearrange("o p d -> (o p) d")).then_inc(x_in[t], 16)

            def store(sp, b):
                for t in range(TT):
                    sp.wait_ge(qkv_done, b * TT + t + 1)
                    sp.dma_start(out[bass.ds(b, 1), t].rearrange("o p d -> (o p) d"), qkv[:, t]).then_inc(stored[t], 16)

            @block.sync
            def _(sp):
                load(sp, 0)
                def batch(b):
                    sp.wait_ge(xn_done, b * TT + TT)
                    load(sp, b + 1)
                    store(sp, b)

                over_batches(sp, batch, B - 1)
                store(sp, B - 1)
                for t in range(TT):
                    sp.wait_ge(stored[t], 16 * B)

            def norm(dve, b):
                for t in range(TT):
                    dve.wait_ge(x_in[t], b * 16 + 16)
                norm_stats(nc, dve, k, lambda t: x[:, t], stats, mv, stats_done, mv_done, b)
                dve.wait_ge(turned, b)
                norm_apply(nc, dve, lambda t: x[:, t], lambda t: xn[:, t], mv, sd, rstd, sd_done, rstd_done, xn_done, b)

            def add_bias(dve, b):
                for t in range(TT):
                    dve.wait_ge(acc_done, b * TT + t + 1)
                    dve.wait_ge(stored[t], b * 16)
                    nc.vector.tensor_tensor(qkv[:, t, 0:S], acc[:, t % 2, 0:S], k["bqkv"][:, 0:S], ALU.add)
                    nc.vector.tensor_tensor(qkv[:, t, S:3 * D], acc[:, t % 2, S:3 * D], k["bqkv"][:, S:3 * D],
                                            ALU.add).then_inc(qkv_done, 1)

            @block.vector
            def _(dve):
                norm(dve, 0)
                def batch(b):
                    norm(dve, b + 1)
                    add_bias(dve, b)

                over_batches(dve, batch, B - 1)
                add_bias(dve, B - 1)

            @block.scalar
            def _(act):
                def batch(b):
                    norm_sqrt(nc, act, k, mv, sd, mv_done, sd_done, b)
                    for c_ in range(DK):
                        act.wait_ge(turned, b + 1)
                        if c_ == 0:
                            act.wait_ge(acc_done, b * TT)
                        nc.scalar.copy(xnT[:, c_], tp[:, c_]).then_inc(xnT_done, 1)

                over_batches(act, batch)

            @block.tensor
            def _(pe):
                def batch(b):
                    pe.wait_ge(xnT_done, b * DK)
                    for t in range(TT):
                        pe.wait_ge(xn_done, b * TT + t + 1)
                        for c_ in range(DK):
                            last = nc.tensor.transpose(tp[:, c_, t * P:(t + 1) * P], xn[:, t, c_ * P:(c_ + 1) * P],
                                                       k["ident"][:])
                    last.then_inc(turned, 1)
                    pe.wait_ge(xnT_done, b * DK + DK)
                    for t in range(TT):
                        if t >= 2:
                            pe.wait_ge(qkv_done, b * TT + t - 1)
                        else:
                            pe.wait_ge(qkv_done, b * TT)
                        for lo, hi in ((0, S), (S, 3 * D)):
                            for c_ in range(DK):
                                last = nc.tensor.matmul(acc[:, t % 2, lo:hi], xnT[:, c_, t * P:(t + 1) * P],
                                                        k["wqkv"][:, c_, lo:hi], start=c_ == 0, stop=c_ == DK - 1)
                        last.then_inc(acc_done, 1)

                over_batches(pe, batch)
        s.end()



def split_self(nc, w, k, scratch):
    with ExitStack() as c:
        s = Scope(nc, c, "ss")
        G = 2
        GH = HEADS // G
        src = s.sb("src", [P, G, TT, 2, GH, HD])
        parts = s.sb("parts", [P, 2 * G, 3, S], BF16)
        rest = s.sb("rest", [P, 2 * G, S])
        tp = s.ps("tp", [P, 2 * G, S])
        src_in = [s.sem(f"src_in{g}") for g in range(G)]
        stored = [s.sem(f"stored{u}") for u in range(2 * G)]
        turned, hi_done, rest_done, mid_done, lo_done = (s.sem(n) for n in (
            "turned", "hi_done", "rest_done", "mid_done", "lo_done"))
        rows_of = scratch["qkv"].rearrange("(b g h t p) f -> b g t p h f", b=B, g=G, t=TT, p=P)
        out = scratch["parts"]
        U = 2 * G

        with nc.Block() as block:
            def load(sp, b, g):
                for t in range(TT):
                    for qk in range(2):
                        sp.dma_start(src[:, g, t, qk], rows_of[bass.ds(b, 1), g, t, :, :, qk * HD:(qk + 1) * HD].rearrange(
                            "o p h e -> (o p) h e")).then_inc(src_in[g], 16)

            @block.sync
            def _(sp):
                for g in range(G):
                    load(sp, 0, g)
                def batch(b):
                    for g in range(G):
                        sp.wait_ge(turned, b * U + 2 * g + 2)
                        load(sp, b + 1, g)

                over_batches(sp, batch, B - 1)

            @block.gpsimd
            def _(pool):
                def batch(b):
                    for u in range(U):
                        wait_apart(pool, k, lo_done, b * U + u + 1)
                        pool.dma_start(out[bass.ds(b, 1), u % 2, :, (u // 2) * P:(u // 2 + 1) * P].rearrange("o c p s -> (o p) c s"),
                                       parts[:, u]).then_inc(stored[u], 16)

                over_batches(pool, batch)
                for u in range(U):
                    pool.wait_ge(stored[u], 16 * B)

            @block.tensor
            def _(pe):
                def batch(b):
                    for u in range(U):
                        g, qk = u // 2, u % 2
                        if qk == 0:
                            pe.wait_ge(src_in[g], (b + 1) * 16 * 2 * TT)
                        if u == 0:
                            pe.wait_ge(rest_done, b * U)
                        for t in range(TT):
                            last = nc.tensor.transpose(tp[:, u, t * P:(t + 1) * P], src[:, g, t, qk].rearrange("p h e -> p (h e)"),
                                                       k["ident"][:])
                        last.then_inc(turned, 1)

                over_batches(pe, batch)

            @block.scalar
            def _(act):
                def batch(b):
                    for u in range(U):
                        act.wait_ge(turned, b * U + u + 1)
                        act.wait_ge(stored[u], b * 16)
                        nc.scalar.copy(parts[:, u, 0], tp[:, u]).then_inc(hi_done, 1)
                        act.wait_ge(rest_done, b * U + u + 1)
                        nc.scalar.copy(parts[:, u, 1], rest[:, u]).then_inc(mid_done, 1)

                over_batches(act, batch)

            @block.vector
            def _(dve):
                def batch(b):
                    for u in range(U):
                        dve.wait_ge(hi_done, b * U + u + 1)
                        nc.vector.tensor_tensor(rest[:, u], tp[:, u], parts[:, u, 0], ALU.subtract).then_inc(rest_done, 1)
                        dve.wait_ge(mid_done, b * U + u + 1)
                        nc.vector.tensor_tensor(parts[:, u, 2], rest[:, u], parts[:, u, 1], ALU.subtract).then_inc(lo_done, 1)

                over_batches(dve, batch)
        s.end()


def attention(nc, w, k, scratch, cross):
    with ExitStack() as c:
        s = Scope(nc, c, "xa" if cross else "sa")
        NSC, NPT, NA, NP_, NM = 2, 4, 4, 8, UNITS
        TURN, COPY = 4, 5
        qs = s.sb("qs", [NS * HD, 2, QUAD, S], BF16)
        ks = s.sb("ks", [NS * HD, 2, QUAD, S], BF16)
        v = s.sb("v", [P, 2, QUAD, TT, 32])
        neg = s.sb("neg", [P, NA, S])
        nmax = s.sb("nmax", [P, NM])
        prob = s.sb("prob", [P, NP_, S])
        pT = s.sb("pT", [P, 2, QUAD, TT, TT, P])
        oT = s.sb("oT", [P, S])
        rsum = s.sb("rsum", [P, TT, QUAD])
        o = s.sb("o", [P, 2, TT, QUAD, HD])
        sc = s.ps("sc", [P, NSC, S])
        ptp = s.ps("ptp", [P, NPT, S])
        acc = s.ps("acc", [P, S])
        otp = s.ps("otp", [P, S])
        if cross:
            adj = s.sb("adj", [P, TT, S])
            mask = s.sb("mask", [P, TT, S], I32)
            fill = s.sb("fill", [P, TT, S])
            bias = s.sb("bias", [P, TT, S])
            den, inv = s.sb("den", [P, TT, QUAD]), s.sb("inv", [P, TT, QUAD])
            adj_in, mask_in, fill_done, bias_done, den_done, inv_done = (s.sem(n) for n in (
                "adj_in", "mask_in", "fill_done", "bias_done", "den_done", "inv_done"))
        else:
            bias = k["causal"]
        q_in, k_in, v_in, o_out = ([s.sem(f"{n}{i}") for i in range(2)] for n in ("q_in", "k_in", "v_in", "o_out"))
        (ones_done, sc_done, neg_done, prob_done, turned, copied_d, copied_a, pv_done, oT_done, oturned, rsum_done,
         o_done) = (s.sem(n) for n in ("ones_done", "sc_done", "neg_done", "prob_done", "turned", "copied_d",
                                       "copied_a", "pv_done", "oT_done", "oturned", "rsum_done", "o_done"))
        QU = QUAD * TT

        def width(t):
            return S if cross else (t + 1) * P

        def on_dve(j):
            return j % 2 == 0

        def copied_by(j, dve_side):
            n = j + 1
            return (n + 1) // 2 if dve_side else n // 2

        def wait_copied(eng, b, j):
            eng.wait_ge(copied_d, b * (UNITS // 2) + copied_by(j, True))
            eng.wait_ge(copied_a, b * (UNITS // 2) + copied_by(j, False))

        def steps(emit):
            def run(eng):
                emit(eng, 0, range(UNITS), True)
                with eng.Fori(1, B) as b:
                    emit(eng, b, range(UNITS), False)
                emit(eng, B - 1, range(UNITS, UNITS + 2 * QU), False)
            return run

        parts = scratch["parts"]
        if cross:
            vrows = scratch["v"].rearrange("(b t p) (q h e) -> b q t p h e", b=B, p=P, h=QUAD, e=HD)
        else:
            vrows = scratch["qkv"].rearrange("(b q h t p) f -> b q p h t f", b=B, q=NQUAD, h=QUAD, p=P)

        with nc.Block() as block:
            def load_quad(sp, b, q):
                hs = slice(q * QUAD * HD, (q + 1) * QUAD * HD)
                for which, (dst, slots, sem) in enumerate(((qs, Q_SLOTS, q_in), (ks, K_SLOTS, k_in))):
                    for n, part in enumerate(slots):
                        sp.dma_start(dst[n * HD:(n + 1) * HD, q % 2],
                                     parts[bass.ds(b, 1), which, part, hs].rearrange("o (h e) s -> (o e) h s", e=HD)
                                     ).then_inc(sem[q % 2], 16)

            def load_v(sp, b, q):
                if cross:
                    for t in range(TT):
                        sp.dma_start(v[:, q % 2, :, t, 0:HD], vrows[bass.ds(b, 1), q, t].rearrange("o p h e -> (o p) h e")
                                     ).then_inc(v_in[q % 2], 16)
                else:
                    for h in range(QUAD):
                        sp.dma_start(v[:, q % 2, h, :, 0:HD],
                                     vrows[bass.ds(b, 1), q, :, h, :, 2 * HD:3 * HD].rearrange("o p t e -> (o p) t e")
                                     ).then_inc(v_in[q % 2], 16)

            def loads(sp, b, first):
                if cross:
                    if not first:
                        sp.wait_ge(fill_done, b * TT)
                    sp.dma_start(mask[:], w["mask"][bass.ds(b, 1)].rearrange("o u (t p) s -> (o p) (u t) s", p=P)
                                 ).then_inc(mask_in, 16)
                for q in range(NQUAD):
                    if not (first and q < 2):
                        sp.wait_ge(sc_done, b * UNITS + (q - 1) * QU)
                    load_quad(sp, b, q)
                    if not (first and q < 2):
                        sp.wait_ge(pv_done, b * NQUAD + q - 1)
                    load_v(sp, b, q)

            @block.sync
            def _(sp):
                sp.wait_ge(ones_done, 1)
                if cross:
                    sp.dma_start(adj[:], w["adj"].rearrange("(t p) s -> p t s", p=P)).then_inc(adj_in, 16)
                loads(sp, 0, True)
                with sp.Fori(1, B) as b:
                    loads(sp, b, False)

            @block.gpsimd
            def _(pool):
                nc.gpsimd.memset(v[:].rearrange("p a h t e -> p (a h t e)"), 1.0).then_inc(ones_done, 1)
                def batch(b):
                    for q in range(NQUAD):
                        wait_apart(pool, k, o_done, b * NQUAD + q + 1)
                        if cross:
                            dst = scratch["o"].rearrange("(b t p) (q f) -> b q p t f", b=B, p=P, q=NQUAD)
                            pool.dma_start(dst[bass.ds(b, 1), q].rearrange("o p t f -> (o p) t f"),
                                           o[:, q % 2].rearrange("p t h e -> p t (h e)")).then_inc(o_out[q % 2], 16)
                        else:
                            dst = scratch["o"].rearrange("r (c e) -> (r c) e", e=HD).rearrange(
                                "(b q h t p) e -> b q p t h e", b=B, q=NQUAD, h=QUAD, p=P)
                            for t in range(TT):
                                pool.dma_start(dst[bass.ds(b, 1), q, :, t].rearrange("o p h e -> (o p) h e"),
                                               o[:, q % 2, t]).then_inc(o_out[q % 2], 16)

                over_batches(pool, batch)
                for i in range(2):
                    pool.wait_ge(o_out[i], 16 * (B * NQUAD // 2) * (1 if cross else TT))

            def pe_steps(pe, b, js, first):
                for j in js:
                    q, jj, t = j // QU, j % QU, j % TT
                    if j < UNITS:
                        h, W = jj // TT, width(t)
                        if jj == 0:
                            n = 2 * b + q // 2 + 1
                            pe.wait_ge(q_in[q % 2], n * 16 * NS)
                            pe.wait_ge(k_in[q % 2], n * 16 * NS)
                        if not (first and j < NSC):
                            pe.wait_ge(neg_done, b * UNITS + j - NSC + 1)
                        nc.tensor.matmul(sc[:, j % NSC, 0:W],
                                         qs[:, q % 2, h, t * P:(t + 1) * P], ks[:, q % 2, h, 0:W],
                                         start=True, stop=True).then_inc(sc_done, 1)
                    i = j - TURN
                    if not (first and i < 0) and i < UNITS:
                        it = i % TT
                        pe.wait_ge(prob_done, b * UNITS + i + 1)
                        if not (first and i < NPT):
                            wait_copied(pe, b, i - NPT)
                        for kt in range(width(it) // P):
                            last = nc.tensor.transpose(ptp[:, i % NPT, kt * P:(kt + 1) * P],
                                                       prob[:, i % NP_, kt * P:(kt + 1) * P], k["ident"][:])
                        last.then_inc(turned, 1)
                    if jj in (7, 9, 11, 13) and not (first and q < 1) and q - 1 < NQUAD:
                        pq, kt = q - 1, (jj - 7) // 2
                        if kt == 0:
                            wait_copied(pe, b, pq * QU + QU - 1)
                            pe.wait_ge(v_in[pq % 2], (2 * b + pq // 2 + 1) * 16 * 4)
                            if not (first and pq < 1):
                                pe.wait_ge(oT_done, b * NQUAD + pq)
                        t0 = 0 if cross else kt
                        for h in range(QUAD):
                            last = nc.tensor.matmul(acc[32 * h:32 * h + 32, t0 * P:S], v[:, pq % 2, h, kt, :],
                                                    pT[:, pq % 2, h, t0:TT, kt, :], start=kt == 0, stop=kt == TT - 1,
                                                    tile_position=(0, 32 * h))
                        if kt == TT - 1:
                            last.then_inc(pv_done, 1)
                    if jj == 1 and not (first and q < 2) and q - 2 < NQUAD:
                        pe.wait_ge(oT_done, b * NQUAD + q - 1)
                        if not (first and q < 3):
                            pe.wait_ge(o_done, b * NQUAD + q - 2)
                        for t_ in range(TT):
                            last = nc.tensor.transpose(otp[:, t_ * P:(t_ + 1) * P], oT[:, t_ * P:(t_ + 1) * P], k["ident"][:])
                        last.then_inc(oturned, 1)

            block.tensor(steps(pe_steps))

            def dve_steps(dve, b, js, first):
                for j in js:
                    q, jj, t = j // QU, j % QU, j % TT
                    if j < UNITS:
                        W = width(t)
                        if cross and j == 0:
                            if first:
                                dve.wait_ge(adj_in, 16)
                            dve.wait_ge(mask_in, b * 16 + 16)
                            for t_ in range(TT):
                                nc.vector.tensor_scalar(fill[:, t_], mask[:, t_], 0, FILL, ALU.is_equal,
                                                        ALU.mult).then_inc(fill_done, 1)
                        if cross and j < TT:
                            dve.wait_ge(fill_done, b * TT + j + 1)
                            nc.vector.scalar_tensor_tensor(bias[:, j], fill[:, j], 1.0, adj[:, j], ALU.mult,
                                                           ALU.add).then_inc(bias_done, 1)
                            dve.wait_ge(bias_done, b * TT + j + 1)
                        if not (first and j < NA):
                            dve.wait_ge(prob_done, b * UNITS + j - NA + 1)
                        wait_apart(dve, k, sc_done, b * UNITS + j + 1)
                        nc.vector.tensor_tensor_reduce(out=neg[:, j % NA, 0:W], in0=sc[:, j % NSC, 0:W],
                                                       in1=bias[:, t, 0:W], scale=-1.0, scalar=HUGE, op0=ALU.add,
                                                       op1=ALU.min, accum_out=nmax[:, j % NM:j % NM + 1]
                                                       ).then_inc(neg_done, 1)
                    i = j - COPY
                    if not (first and i < 0) and i < UNITS and on_dve(i):
                        copy_out(dve, nc.vector.tensor_copy, copied_d, b, i, first)
                    if jj == 3 and not (first and q < 2) and q - 2 < NQUAD:
                        pq = q - 2
                        dve.wait_ge(oturned, b * NQUAD + pq + 1)
                        if not (first and pq < 2):
                            dve.wait_ge(o_out[pq % 2], (2 * b + pq // 2) * 16 * (1 if cross else TT))
                        ov = otp[:].rearrange("p (n e) -> p n e", e=32)
                        rs = rsum[:].rearrange("p t h -> p (t h)")
                        if cross:
                            m0 = (pq * QU) % NM
                            nm = nmax[:, m0:m0 + QU].rearrange("p (h t) -> p t h", t=TT)
                            nc.vector.scalar_tensor_tensor(den[:], nm, -FILL / 2, ov[:, :, HD].rearrange(
                                "p (t h) -> p t h", h=QUAD), ALU.is_lt, ALU.mult).then_inc(den_done, 1)
                            dve.wait_ge(den_done, b * NQUAD + pq + 1)
                            nc.vector.reciprocal(inv[:], den[:]).then_inc(inv_done, 1)
                            dve.wait_ge(inv_done, b * NQUAD + pq + 1)
                            nc.vector.scalar_tensor_tensor(rsum[:], nm, -FILL / 2, inv[:], ALU.is_lt,
                                                           ALU.mult).then_inc(rsum_done, 1)
                        else:
                            nc.vector.reciprocal(rs, ov[:, :, HD]).then_inc(rsum_done, 1)
                        dve.wait_ge(rsum_done, b * NQUAD + pq + 1)
                        nc.vector.tensor_tensor(o[:, pq % 2].rearrange("p t h e -> p (t h) e"), ov[:, :, 0:HD],
                                                rsum[:].rearrange("p t (h o) -> p (t h) o", o=1).broadcast_to([P, TT * QUAD, HD]),
                                                ALU.mult).then_inc(o_done, 1)

            def copy_out(eng, copy, sem, b, i, first):
                iq, ih, it = i // QU, (i % QU) // TT, i % TT
                eng.wait_ge(turned, b * UNITS + i + 1)
                if i % QU < 2 and not (first and iq < 2):
                    eng.wait_ge(pv_done, b * NQUAD + iq - 1)
                W = width(it)
                copy(pT[:, iq % 2, ih, it, 0:W // P].rearrange("p a s -> p (a s)"), ptp[:, i % NPT, 0:W]).then_inc(sem, 1)

            block.vector(steps(dve_steps))

            def act_steps(act, b, js, first):
                for j in js:
                    q, jj, t = j // QU, j % QU, j % TT
                    if j < UNITS:
                        W = width(t)
                        act.wait_ge(neg_done, b * UNITS + j + 1)
                        if not (first and j < NP_):
                            act.wait_ge(turned, b * UNITS + j - NP_ + 1)
                        nc.scalar.activation(prob[:, j % NP_, 0:W], neg[:, j % NA, 0:W], ACT.Exp,
                                             bias=nmax[:, j % NM:j % NM + 1], scale=-1.0).then_inc(prob_done, 1)
                    i = j - COPY
                    if not (first and i < 0) and i < UNITS and not on_dve(i):
                        copy_out(act, nc.scalar.copy, copied_a, b, i, first)
                    if jj == 15 and not (first and q < 1) and q - 1 < NQUAD:
                        act.wait_ge(pv_done, b * NQUAD + q)
                        if not (first and q < 2):
                            act.wait_ge(oturned, b * NQUAD + q - 1)
                        nc.scalar.copy(oT[:], acc[:]).then_inc(oT_done, 1)

            block.scalar(steps(act_steps))
        s.end()




def batch_rows(ap, b, n=B):
    return ap.rearrange("(b t p) f -> b p t f", b=n, p=P)[bass.ds(b, 1)].rearrange("o p t f -> (o p) t f")


def turn_batch(nc, pe, k, dst, src, ready, ready_base, done):
    for t in range(TT):
        if ready is not None:
            pe.wait_ge(ready, ready_base + t + 1)
        for c_ in range(DK):
            last = nc.tensor.transpose(dst[:, c_, t * P:(t + 1) * P], src[:, t, c_ * P:(c_ + 1) * P], k["ident"][:])
    last.then_inc(done, 1)


def project_cross(nc, w, k, scratch):
    with ExitStack() as c:
        s = Scope(nc, c, "pc")
        U = 4
        UNIT = ((1, 0), (1, 1), (0, 0), (0, 1))
        x, o, cx, xn, x1 = (s.sb(n, [P, TT, D]) for n in ("x", "o", "cx", "xn", "x1"))
        oT, cT, xnT = (s.sb(n, [P, DK, S]) for n in ("oT", "cT", "xnT"))
        vv = s.sb("v", [P, TT, D])
        full, rest = s.sb("full", [P, U, S]), s.sb("rest", [P, U, S])
        parts = s.sb("parts", [P, U, 3, S], BF16)
        stats, mv, sd, rstd = (s.sb("stats", [P, TT, 6]), s.sb("mv", [P, TT, 2]), s.sb("sd", [P, TT]),
                               s.sb("rstd", [P, TT]))
        tp, at, qk = s.ps("tp", [P, DK, S]), s.ps("at", [P, TT, D]), s.ps("qk", [P, 2, S])
        vp = s.ps("vp", [P, TT, D])
        (x_in, o_in, cx_in, x1_out, v_out, xb_done, turned, tp_free, at_done, x1_done, stats_done, mv_done, sd_done,
         rstd_done, xn_done, qk_done, full_done, hi_done, rest_done, mid_done, lo_done, vp_done, v_done) = (
            s.sem(n) for n in (
                "x_in", "o_in", "cx_in", "x1_out", "v_out", "xb_done", "turned", "tp_free", "at_done", "x1_done",
                "stats_done", "mv_done", "sd_done", "rstd_done", "xn_done", "qk_done", "full_done", "hi_done",
                "rest_done", "mid_done", "lo_done", "vp_done", "v_done"))
        parts_out = [s.sem(f"parts_out{u}") for u in range(U)]
        xrows = w["x"].rearrange("b s d -> (b s) d")
        crows = w["ctx"].rearrange("b s d -> (b s) d")

        with nc.Block() as block:
            def load(sp, b):
                sp.dma_start(o[:], batch_rows(scratch["o"], b)).then_inc(o_in, 16)
                sp.dma_start(x[:], batch_rows(xrows, b)).then_inc(x_in, 16)
                sp.dma_start(cx[:], batch_rows(crows, b)).then_inc(cx_in, 16)

            @block.sync
            def _(sp):
                load(sp, 0)
                with sp.Fori(1, B) as b:
                    wait_apart(sp, k, turned, b * 3 - 1)
                    sp.wait_ge(x1_done, b * TT)
                    load(sp, b)

            def store_parts(pool, b, u):
                which, g = UNIT[u]
                wait_apart(pool, k, lo_done, b * U + u + 1)
                pool.dma_start(scratch["parts"][bass.ds(b, 1), which, :, g * P:(g + 1) * P].rearrange("o c p s -> (o p) c s"),
                               parts[:, u]).then_inc(parts_out[u], 16)

            @block.gpsimd
            def _(pool):
                def batch(b):
                    pool.wait_ge(x_in, b * 16 + 16)
                    for t in range(TT):
                        nc.gpsimd.tensor_tensor(x[:, t], x[:, t], k["bout"][:], ALU.add).then_inc(xb_done, 1)
                    wait_apart(pool, k, x1_done, b * TT + TT)
                    pool.dma_start(batch_rows(scratch["x1"], b), x1[:]).then_inc(x1_out, 16)
                    for u in range(2):
                        store_parts(pool, b, u)
                    wait_apart(pool, k, v_done, b * TT + TT)
                    pool.dma_start(batch_rows(scratch["v"], b), vv[:]).then_inc(v_out, 16)
                    for u in range(2, U):
                        store_parts(pool, b, u)

                over_batches(pool, batch)
                pool.wait_ge(x1_out, 16 * B)
                pool.wait_ge(v_out, 16 * B)
                for u in range(U):
                    pool.wait_ge(parts_out[u], 16 * B)

            def project_heads(pe, b, u0, srcT):
                for u in (u0, u0 + 1):
                    which, g = UNIT[u]
                    pe.wait_ge(full_done, b * U + u0)
                    for c_ in range(DK):
                        last = nc.tensor.matmul(qk[:, u % 2], k["xw"][:, which, c_, g * P:(g + 1) * P], srcT[:, c_],
                                                start=c_ == 0, stop=c_ == DK - 1)
                    last.then_inc(qk_done, 1)

            @block.tensor
            def _(pe):
                def batch(b):
                    pe.wait_ge(o_in, b * 16 + 16)
                    pe.wait_ge(tp_free, b * 3 * DK)
                    turn_batch(nc, pe, k, tp, o, None, 0, turned)
                    pe.wait_ge(tp_free, b * 3 * DK + DK)
                    pe.wait_ge(x1_done, b * TT)
                    for t in range(TT):
                        for c_ in range(DK):
                            last = nc.tensor.matmul(at[:, t], oT[:, c_, t * P:(t + 1) * P], k["wout"][:, c_],
                                                    start=c_ == 0, stop=c_ == DK - 1)
                        last.then_inc(at_done, 1)
                    pe.wait_ge(cx_in, b * 16 + 16)
                    turn_batch(nc, pe, k, tp, cx, None, 0, turned)
                    pe.wait_ge(tp_free, b * 3 * DK + 2 * DK)
                    project_heads(pe, b, 0, cT)
                    pe.wait_ge(v_done, b * TT)
                    for t in range(TT):
                        for c_ in range(DK):
                            last = nc.tensor.matmul(vp[:, t], cT[:, c_, t * P:(t + 1) * P], k["xw"][:, 2, c_],
                                                    start=c_ == 0, stop=c_ == DK - 1)
                        last.then_inc(vp_done, 1)
                    turn_batch(nc, pe, k, tp, xn, xn_done, b * TT, turned)
                    pe.wait_ge(tp_free, b * 3 * DK + 3 * DK)
                    project_heads(pe, b, 2, xnT)

                over_batches(pe, batch)

            @block.scalar
            def _(act):
                def keep_turned(b, n, dst):
                    act.wait_ge(turned, b * 3 + n + 1)
                    for c_ in range(DK):
                        nc.scalar.copy(dst[:, c_], tp[:, c_]).then_inc(tp_free, 1)

                def full_and_hi(b, u):
                    which, g = UNIT[u]
                    act.wait_ge(qk_done, b * U + u + 1)
                    nc.scalar.activation(full[:, u], qk[:, u % 2], ACT.Identity, bias=k["bqk"][:, which, g:g + 1],
                                         scale=1.0 if which else float(HD) ** -0.5).then_inc(full_done, 1)
                    act.wait_ge(full_done, b * U + u + 1)
                    act.wait_ge(parts_out[u], b * 16)
                    nc.scalar.copy(parts[:, u, 0], full[:, u]).then_inc(hi_done, 1)

                def mid(b, u):
                    act.wait_ge(rest_done, b * U + u + 1)
                    nc.scalar.copy(parts[:, u, 1], rest[:, u]).then_inc(mid_done, 1)

                def batch(b):
                    act.wait_ge(at_done, b * TT)
                    keep_turned(b, 0, oT)
                    act.wait_ge(vp_done, b * TT)
                    keep_turned(b, 1, cT)
                    norm_sqrt(nc, act, k, mv, sd, mv_done, sd_done, b)
                    full_and_hi(b, 0)
                    full_and_hi(b, 1)
                    mid(b, 0)
                    act.wait_ge(qk_done, b * U)
                    keep_turned(b, 2, xnT)
                    mid(b, 1)
                    full_and_hi(b, 2)
                    full_and_hi(b, 3)
                    mid(b, 2)
                    mid(b, 3)

                over_batches(act, batch)

            @block.vector
            def _(dve):
                def split_rest(b, u):
                    dve.wait_ge(hi_done, b * U + u + 1)
                    nc.vector.tensor_tensor(rest[:, u], full[:, u], parts[:, u, 0], ALU.subtract).then_inc(rest_done, 1)

                def split_lo(b, u):
                    dve.wait_ge(mid_done, b * U + u + 1)
                    nc.vector.tensor_tensor(parts[:, u, 2], rest[:, u], parts[:, u, 1], ALU.subtract).then_inc(lo_done, 1)

                def batch(b):
                    for t in range(TT):
                        dve.wait_ge(at_done, b * TT + (t | 1) + 1)
                        dve.wait_ge(xb_done, b * TT + t + 1)
                        dve.wait_ge(x1_out, b * 16)
                        nc.vector.tensor_tensor(x1[:, t], at[:, t], x[:, t], ALU.add).then_inc(x1_done, 1)
                    dve.wait_ge(x1_done, b * TT + TT)
                    norm_stats(nc, dve, k, lambda t: x1[:, t], stats, mv, stats_done, mv_done, b)
                    dve.wait_ge(turned, b * 3)
                    norm_apply(nc, dve, lambda t: x1[:, t], lambda t: xn[:, t], mv, sd, rstd, sd_done, rstd_done,
                               xn_done, b)
                    split_rest(b, 0)
                    split_rest(b, 1)
                    split_lo(b, 0)
                    dve.wait_ge(v_out, b * 16)
                    for t in range(TT):
                        dve.wait_ge(vp_done, b * TT + (t | 1) + 1)
                        nc.vector.tensor_tensor(vv[:, t], vp[:, t], k["bv"][:], ALU.add).then_inc(v_done, 1)
                    split_lo(b, 1)
                    split_rest(b, 2)
                    split_rest(b, 3)
                    split_lo(b, 2)
                    split_lo(b, 3)

                over_batches(dve, batch)
        s.end()


def route(nc, w, k, scratch):
    with ExitStack() as c:
        s = Scope(nc, c, "rt")
        x, o, x2 = (s.sb(n, [P, TT, D]) for n in ("x", "o", "x2"))
        xn = s.sb("xn", [P, TT, ROW])
        zeros = s.sb("zeros", [P, TT, ROW])
        oT, xnT = (s.sb(n, [P, DK, S]) for n in ("oT", "xnT"))
        stats, mv, sd, rstd = (s.sb("stats", [P, TT, 6]), s.sb("mv", [P, TT, 2]), s.sb("sd", [P, TT]),
                               s.sb("rstd", [P, TT]))
        top, zero1, expg, shift, score, biased, above, equal, s2_, s4_, pick, sel = (
            s.sb(n, [P, TT, NE]) for n in ("top", "zero1", "expg", "shift", "score", "biased", "above", "equal",
                                           "s2", "s4", "pick", "sel"))
        c0, c1, c2 = (s.sb(n, [P, TT, 2 * NE]) for n in ("c0", "c1", "c2"))
        gmax, gsum, ginv, nabove, need = (s.sb(n, [P, TT]) for n in ("gmax", "gsum", "ginv", "nabove", "need"))
        tp, at, gp = s.ps("tp", [P, DK, S]), s.ps("at", [P, TT, D]), s.ps("gp", [P, S])
        (x_in, o_in, x2_out, xn_out, zeros_out, ones_done, xb_done, turned, tp_free, at_done, x2_done,
         stats_done, mv_done, sd_done, rstd_done, xn_done, gate_done, exp_done, g_step, cw_done, zeroed) = (
            s.sem(n) for n in (
                "x_in", "o_in", "x2_out", "xn_out", "zeros_out", "ones_done", "xb_done", "turned", "tp_free",
                "at_done", "x2_done", "stats_done", "mv_done", "sd_done", "rstd_done", "xn_done", "gate_done",
                "exp_done", "g_step", "cw_done", "zeroed"))
        GATE_STEPS = 16
        xs = scratch["xs"]

        with nc.Block() as block:
            def load(sp, b):
                sp.dma_start(o[:], batch_rows(scratch["o"], b)).then_inc(o_in, 16)
                sp.dma_start(x[:], batch_rows(scratch["x1"], b)).then_inc(x_in, 16)

            @block.sync
            def _(sp):
                load(sp, 0)
                sp.wait_ge(ones_done, 2)
                for i in range(ROUTED // TT):
                    sp.dma_start(batch_rows(xs[B * S:NTILES * P], i, ROUTED // TT), zeros[:]).then_inc(zeros_out, 16)
                with sp.Fori(1, B) as b:
                    wait_apart(sp, k, turned, b * 2 - 1)
                    sp.wait_ge(x2_done, b * TT)
                    load(sp, b)
                sp.wait_ge(zeros_out, 16 * (ROUTED // TT))

            @block.gpsimd
            def _(pool):
                nc.gpsimd.memset(zeros[:], 0.0).then_inc(ones_done, 1)
                nc.gpsimd.memset(xn[:], 1.0).then_inc(ones_done, 1)
                def batch(b):
                    pool.wait_ge(x_in, b * 16 + 16)
                    for t in range(TT):
                        nc.gpsimd.tensor_tensor(x[:, t], x[:, t], k["bo"][:], ALU.add).then_inc(xb_done, 1)
                    wait_apart(pool, k, x2_done, b * TT + TT)
                    pool.dma_start(batch_rows(scratch["x2"], b), x2[:]).then_inc(x2_out, 16)
                    wait_apart(pool, k, xn_done, b * TT + TT)
                    pool.dma_start(batch_rows(xs[0:B * S], b), xn[:]).then_inc(xn_out, 16)

                over_batches(pool, batch)
                for q in (x2_out, xn_out):
                    pool.wait_ge(q, 16 * B)

            @block.tensor
            def _(pe):
                def batch(b):
                    pe.wait_ge(o_in, b * 16 + 16)
                    pe.wait_ge(tp_free, b * 2 * DK)
                    turn_batch(nc, pe, k, tp, o, None, 0, turned)
                    pe.wait_ge(tp_free, b * 2 * DK + DK)
                    pe.wait_ge(x2_done, b * TT)
                    for t in range(TT):
                        for c_ in range(DK):
                            last = nc.tensor.matmul(at[:, t], oT[:, c_, t * P:(t + 1) * P], k["xw"][:, 3, c_],
                                                    start=c_ == 0, stop=c_ == DK - 1)
                        last.then_inc(at_done, 1)
                    turn_batch(nc, pe, k, tp, xn, xn_done, b * TT, turned)
                    pe.wait_ge(tp_free, b * 2 * DK + 2 * DK)
                    for t in range(TT):
                        for c_ in range(DK):
                            last = nc.tensor.matmul(gp[:, t * NE:(t + 1) * NE], xnT[:, c_, t * P:(t + 1) * P],
                                                    k["gateT"][:, c_], start=c_ == 0, stop=c_ == DK - 1)
                    last.then_inc(gate_done, 1)

                over_batches(pe, batch)

            @block.scalar
            def _(act):
                def batch(b):
                    act.wait_ge(turned, b * 2 + 1)
                    for c_ in range(DK):
                        nc.scalar.copy(oT[:, c_], tp[:, c_]).then_inc(tp_free, 1)
                    norm_sqrt(nc, act, k, mv, sd, mv_done, sd_done, b)
                    act.wait_ge(turned, b * 2 + 2)
                    act.wait_ge(gate_done, b)
                    for c_ in range(DK):
                        nc.scalar.copy(xnT[:, c_], tp[:, c_]).then_inc(tp_free, 1)
                    act.wait_ge(g_step, b * GATE_STEPS + 2)
                    nc.scalar.activation(expg[:], shift[:], ACT.Exp).then_inc(exp_done, 1)

                over_batches(act, batch)

            @block.vector
            def _(dve):
                dve.wait_ge(ones_done, 2)
                for z in (c0, c1, c2):
                    nc.vector.memset(z[:], 0.0).then_inc(zeroed, 1)
                dve.wait_ge(zeroed, 3)

                def batch(b):
                    for t in range(TT):
                        dve.wait_ge(at_done, b * TT + (t | 1) + 1)
                        dve.wait_ge(xb_done, b * TT + t + 1)
                        dve.wait_ge(x2_out, b * 16)
                        nc.vector.tensor_tensor(x2[:, t], at[:, t], x[:, t], ALU.add).then_inc(x2_done, 1)
                    dve.wait_ge(x2_done, b * TT + TT)
                    norm_stats(nc, dve, k, lambda t: x2[:, t], stats, mv, stats_done, mv_done, b)
                    dve.wait_ge(xn_out, b * 16)
                    norm_apply(nc, dve, lambda t: x2[:, t], lambda t: xn[:, t, 0:D], mv, sd, rstd, sd_done, rstd_done,
                               xn_done, b)
                    steps = [0]

                    def then(ins):
                        steps[0] += 1
                        ins.then_inc(g_step, 1)
                        wait_apart(dve, k, g_step, b * GATE_STEPS + steps[0])

                    def wide(a):
                        return a.rearrange("p (t o) -> p t o", o=1).broadcast_to([P, TT, NE])

                    dve.wait_ge(gate_done, b + 1)
                    logits = gp[:, 0:TT * NE].rearrange("p (t e) -> p t e", e=NE)
                    then(nc.vector.tensor_reduce(gmax[:], logits, AX_X, ALU.max))
                    then(nc.vector.tensor_tensor(shift[:], logits, wide(gmax[:]), ALU.subtract))
                    dve.wait_ge(exp_done, b + 1)
                    then(nc.vector.tensor_reduce(gsum[:], expg[:], AX_X, ALU.add))
                    then(nc.vector.reciprocal(ginv[:], gsum[:]))
                    then(nc.vector.tensor_tensor(score[:], expg[:], wide(ginv[:]), ALU.mult))
                    then(nc.vector.tensor_tensor(biased[:], score[:], k["gateb"][:].rearrange(
                        "p (o e) -> p o e", o=1).broadcast_to([P, TT, NE]), ALU.add))
                    for t in range(TT):
                        last = nc.vector.max(top[:, t], biased[:, t])
                    then(last)
                    second = top[:, :, 1:2].broadcast_to([P, TT, NE])
                    then(nc.vector.tensor_tensor(above[:], biased[:], second, ALU.is_gt))
                    then(nc.vector.tensor_tensor(c0[:, :, NE:], biased[:], second, ALU.is_equal))
                    then(nc.vector.tensor_reduce(nabove[:], above[:], AX_X, ALU.add))
                    then(nc.vector.tensor_tensor(c1[:, :, NE:], c0[:, :, NE:], c0[:, :, NE - 1:2 * NE - 1], ALU.add))
                    then(nc.vector.tensor_tensor(c2[:, :, NE:], c1[:, :, NE:], c1[:, :, NE - 2:2 * NE - 2], ALU.add))
                    then(nc.vector.tensor_tensor(s4_[:], c2[:, :, NE:], c2[:, :, NE - 4:2 * NE - 4], ALU.add))
                    then(nc.vector.tensor_tensor(s2_[:], s4_[:], wide(nabove[:]), ALU.add))
                    then(nc.vector.scalar_tensor_tensor(pick[:], s2_[:], 2.0, c0[:, :, NE:], ALU.is_le, ALU.mult))
                    mine = bass.ds(b * TT, TT)
                    then(nc.vector.tensor_tensor(sel[:], above[:], pick[:], ALU.add))
                    nc.vector.tensor_copy(k["sel"][:, mine], sel[:])
                    nc.vector.tensor_tensor(k["cw"][:, mine], sel[:], score[:], ALU.mult).then_inc(cw_done, 1)
                    assert steps[0] == GATE_STEPS

                over_batches(dve, batch)
        s.end()


def experts_of(nc, engine, k, j):
    return nc.values_load_multi_w_load_instructions(
        k["eidx"][0:1, bass.ds(j * 4, 8)], engines=[engine], min_val=0, max_val=NE,
        skip_runtime_bounds_check_because="assign clamps each to 0..NE")[1]


def of_expert(a, e):
    n = len(a.shape)
    x = a[:, bass.ds(e, 1)]
    return x.rearrange({3: "p o f -> p (o f)", 4: "p o n f -> p (o n) f", 5: "p o n c f -> p (o n) c f"}[n])


def load_experts(nc, w, k, ctx):
    keep = Scope(nc, ctx, "xk")
    k["w13"] = keep.sb("w13", [P, NX, 2, DK, 2 * FF])
    k["w2"] = keep.sb("w2", [P, NX, MF, D])
    k["b13"] = keep.sb("b13", [P, NX, 2, 2 * FF])
    k["b2"] = keep.sb("b2", [P, NX, D])
    with ExitStack() as c:
        s = Scope(nc, c, "ew")
        FO = 2 * FF // P
        raw13 = s.sb("raw13", [P, 2, 2, FO, D])
        raw2 = s.sb("raw2", [P, 2, DK, FF])
        tp = s.ps("tp", [P, 8, S])
        raw_in = [s.sem(f"raw_in{i}") for i in range(2)]
        small_in, turned, copied_a, copied_d = (s.sem(n) for n in ("small_in", "turned", "copied_a", "copied_d"))
        G = 2 * DK + MF

        def src(name, e):
            return w[name][e] if e < NE else w["s" + name]

        with nc.Block() as block:
            @block.sync
            def _(sp):
                for e in range(NX):
                    for dst, name in ((k["b13"][:, e, 0], "b1"), (k["b13"][:, e, 1], "b3"), (k["b2"][:, e], "b2")):
                        n = dst.shape[1]
                        sp.dma_start(dst, src(name, e).rearrange("(o f) -> o f", o=1).broadcast_to([P, n])).then_inc(small_in, 16)
                sp.wait_ge(small_in, 16 * 3 * NX)

            @block.gpsimd
            def _(pool):
                for e in range(NX):
                    if e >= 2:
                        pool.wait_ge(turned, G * (e - 1))
                    for n, name in enumerate(("w1", "w3")):
                        pool.dma_start(raw13[:, e % 2, n], src(name, e).rearrange("(c p) d -> p c d", p=P)
                                       ).then_inc(raw_in[e % 2], 16)
                    pool.dma_start(raw2[:, e % 2], src("w2", e).rearrange("(c p) f -> p c f", p=P)
                                   ).then_inc(raw_in[e % 2], 16)

            @block.tensor
            def _(pe):
                for e in range(NX):
                    pe.wait_ge(raw_in[e % 2], 48 * (e // 2 + 1))
                    for g in range(G):
                        n = e * G + g
                        if n >= 8:
                            pe.wait_ge(copied_d if n % 2 == 0 else copied_a, (n - 8) // 2 + 1)
                        if g < 2 * DK:
                            blocks = [raw13[:, e % 2, g // DK, i, (g % DK) * P:(g % DK + 1) * P] for i in range(FO)]
                        else:
                            fk = g - 2 * DK
                            blocks = [raw2[:, e % 2, i, fk * P:(fk + 1) * P] for i in range(DK)]
                        for i, a in enumerate(blocks):
                            last = nc.tensor.transpose(tp[:, n % 8, i * P:(i + 1) * P], a, k["ident"][:])
                        last.then_inc(turned, 1)

            def copies(eng, copy, side, sem):
                for n in range(side, NX * G, 2):
                    e, g = n // G, n % G
                    eng.wait_ge(turned, n + 1)
                    if g < 2 * DK:
                        copy(k["w13"][:, e, g // DK, g % DK], tp[:, n % 8]).then_inc(sem, 1)
                    else:
                        copy(k["w2"][:, e, g - 2 * DK], tp[:, n % 8, 0:D]).then_inc(sem, 1)

            @block.vector
            def _(dve):
                copies(dve, nc.vector.tensor_copy, 0, copied_d)

            @block.scalar
            def _(act):
                copies(act, nc.scalar.copy, 1, copied_a)
        s.end()


def assign(nc, k):
    with ExitStack() as c:
        s = Scope(nc, c, "as")
        TB = B * TT
        tri, ones = s.sb("tri", [P, P]), s.sb("ones", [P, P])
        iota_i = s.sb("iota_i", [P, ROUTED], I32)
        iota, starts = s.sb("iota", [P, ROUTED]), s.sb("starts", [P, TB])
        ca, cb = s.sb("ca", [P, NE, 2 * TB]), s.sb("cb", [P, NE, 2 * TB])
        more, ntiles = s.sb("more", [P, NE, TB]), s.sb("ntiles", [P, NE])
        na, nb = s.sb("na", [P, 2 * NE]), s.sb("nb", [P, 2 * NE])
        base, slot, slotm, hit, hitw = (s.sb(n, [P, TB, NE]) for n in ("base", "slot", "slotm", "hit", "hitw"))
        two, total = s.sb("two", [P, 2, TB]), s.sb("total", [P, TB])
        ended, ef = s.sb("ended", [P, ROUTED, NE]), s.sb("ef", [P, NTILES + 8])
        pre, tot = s.ps("pre", [P, S]), s.ps("tot", [P, S])
        made, tri_done, counted, step = (s.sem(n) for n in ("made", "tri_done", "counted", "step"))
        with nc.Block() as block:
            @block.gpsimd
            def _(pool):
                nc.gpsimd.memset(tri[:], 1.0).then_inc(made, 1)
                pool.wait_ge(made, 1)
                nc.gpsimd.affine_select(out=tri[:], in_=tri[:], compare_op=ALU.is_gt, fill=0.0, base=0,
                                        pattern=[[1, P]], channel_multiplier=-1).then_inc(tri_done, 1)
                nc.gpsimd.memset(ones[:], 1.0).then_inc(tri_done, 1)
                nc.gpsimd.iota(iota_i[:], pattern=[[1, ROUTED]], base=0, channel_multiplier=0).then_inc(tri_done, 1)

            @block.tensor
            def _(pe):
                pe.wait_ge(tri_done, 2)
                sel = k["sel"][:].rearrange("p t e -> p (t e)")
                nc.tensor.matmul(pre[:, 0:TB * NE], tri[:], sel, start=True, stop=True)
                nc.tensor.matmul(tot[:, 0:TB * NE], ones[:], sel, start=True, stop=True).then_inc(counted, 1)

            @block.vector
            def _(dve):
                n = [0]

                def then(ins):
                    n[0] += 1
                    ins.then_inc(step, 1)
                    dve.wait_ge(step, n[0])

                def over_t(a):
                    return a.rearrange("p (o e) -> p o e", o=1).broadcast_to([P, TB, NE])

                for z in (ca, cb, na, nb):
                    then(nc.vector.memset(z[:], 0.0))
                dve.wait_ge(tri_done, 3)
                then(nc.vector.tensor_copy(iota[:], iota_i[:]))
                then(nc.vector.tensor_scalar(starts[:], iota[:, 0:TB], float(P), None, ALU.mult))
                dve.wait_ge(counted, 1)
                then(nc.vector.tensor_copy(ca[:, :, TB:], tot[:, 0:TB * NE].rearrange("p (t e) -> p e t", e=NE)))
                a, b_, d = ca, cb, 1
                while d < TB:
                    then(nc.vector.tensor_tensor(b_[:, :, TB:], a[:, :, TB:], a[:, :, TB - d:2 * TB - d], ALU.add))
                    a, b_, d = b_, a, 2 * d
                count = a[:, :, 2 * TB - 1:2 * TB].broadcast_to([P, NE, TB])
                then(nc.vector.tensor_tensor(more[:], count, starts[:].rearrange("p (o t) -> p o t", o=1).broadcast_to(
                    [P, NE, TB]), ALU.is_gt))
                then(nc.vector.tensor_reduce(ntiles[:], more[:], AX_X, ALU.add))
                then(nc.vector.tensor_copy(na[:, NE:], ntiles[:]))
                f, g_, d = na, nb, 1
                while d < NE:
                    then(nc.vector.tensor_tensor(g_[:, NE:], f[:, NE:], f[:, NE - d:2 * NE - d], ALU.add))
                    f, g_, d = g_, f, 2 * d
                before = a[:, :, TB - 1:2 * TB - 1].rearrange("p e t -> p t e")
                then(nc.vector.scalar_tensor_tensor(base[:], over_t(f[:, NE - 1:2 * NE - 1]), float(P), before,
                                                    ALU.mult, ALU.add))
                then(nc.vector.tensor_tensor(slot[:], pre[:, 0:TB * NE].rearrange("p (t e) -> p t e", e=NE), base[:], ALU.add))
                then(nc.vector.scalar_tensor_tensor(slotm[:], slot[:], float(B * S), k["sel"][:], ALU.add, ALU.mult))
                then(nc.vector.tensor_reduce(two[:, 1], slotm[:], AX_X, ALU.max))
                then(nc.vector.tensor_reduce(total[:], slotm[:], AX_X, ALU.add))
                then(nc.vector.tensor_tensor(two[:, 0], total[:], two[:, 1], ALU.subtract))
                then(nc.vector.tensor_copy(k["slots"][:], two[:]))
                for i in range(2):
                    then(nc.vector.tensor_tensor(hit[:], slotm[:], two[:, i].rearrange("p (t o) -> p t o", o=1).broadcast_to(
                        [P, TB, NE]), ALU.is_equal))
                    then(nc.vector.tensor_tensor(hitw[:], hit[:], k["cw"][:], ALU.mult))
                    then(nc.vector.tensor_reduce(k["cw2"][:, i], hitw[:], AX_X, ALU.add))
                then(nc.vector.tensor_tensor(ended[:], iota[:].rearrange("p (i o) -> p i o", o=1).broadcast_to([P, ROUTED, NE]),
                                             f[:, NE:].rearrange("p (o e) -> p o e", o=1).broadcast_to([P, ROUTED, NE]),
                                             ALU.is_ge))
                then(nc.vector.memset(ef[:], float(NE)))
                mine = slice(4 + TB, 4 + NTILES)
                then(nc.vector.tensor_reduce(ef[:, mine], ended[:], AX_X, ALU.add))
                then(nc.vector.tensor_scalar(ef[:, mine], ef[:, mine], float(NE - 1), None, ALU.min))
                then(nc.vector.tensor_copy(k["eidx"][:], ef[:]))
        s.end()


def experts(nc, k, scratch):
    ALPHA, LIMIT = 1.702, 7.0
    R = 4
    UP, GATE, DOWN, STORE = 1, 2, 4, 9
    with ExitStack() as c:
        s = Scope(nc, c, "ex")
        xg = s.sb("xg", [P, R, ROW])
        xgT = s.sb("xgT", [P, R, DK, P])
        t1, t3, hh = s.sb("t1", [P, 2 * FF]), s.sb("t3", [P, 2 * FF]), s.sb("hh", [P, 2 * FF])
        g, sg, l = (s.sb(n, [P, 2, FF]) for n in ("g", "sg", "l"))
        gs = s.sb("gs", [P, FF])
        a = s.sb("a", [P, R, FF])
        cwc = s.sb("cwc", [P, R])
        aT = s.sb("aT", [P, R, MF, P])
        ysb = s.sb("ysb", [P, R, D])
        xr = s.sb("xr", [P, 2, TT, ROW])
        idx = s.sb("idx", [P, 2, TT], U32)
        xtp, hp, atp, yp = s.ps("xtp", [P, S]), s.ps("hp", [P, 2, 2, S]), s.ps("atp", [P, S]), s.ps("yp", [P, 2, S])
        x_in, y_out = ([s.sem(f"{n}{i}") for i in range(R)] for n in ("x_in", "y_out"))
        (xturned, xgT_done, cwc_done, h_done, t_done, hh_done, g_done, sg_done, gs_done, l_done, a_done, aturned,
         aT_done, y_done, ysb_done, xr_in, filled, scattered) = (s.sem(n) for n in (
            "xturned", "xgT_done", "cwc_done", "h_done", "t_done", "hh_done", "g_done", "sg_done", "gs_done",
            "l_done", "a_done", "aturned", "aT_done", "y_done", "ysb_done", "xr_in", "filled", "scattered"))
        xs, ys = scratch["xs"], scratch["ys"]
        xs_t = xs.rearrange("(i q p) f -> i q p f", q=R, p=P)
        ys_t = ys.rearrange("(i q p) f -> i q p f", q=R, p=P)
        GROUPS = NTILES // R
        SHARED = B * TT // R

        def back(j, q, n):
            jj, qq = j + (q - n) // R, (q - n) % R
            if isinstance(j, int) and not 0 <= jj < GROUPS:
                return None
            return jj, qq, jj * R + qq

        def groups(eng, step, engine):
            def group(j):
                es = experts_of(nc, engine, k, j) if engine is not None else None
                for q in range(R):
                    step(j, q, es)

            group(0)
            group(1)
            with eng.Fori(2, GROUPS) as j:
                group(j)
            group(GROUPS)

        def wait_if(eng, sem, value):
            if not isinstance(value, int) or value > 0:
                eng.wait_ge(sem, value)

        with nc.Block() as block:
            def load(sp, j, q):
                wait_if(sp, xturned, R * (j - 1) + q + 1)
                wait_if(sp, cwc_done, R * (j - 1) + q + 1)
                sp.dma_start(xg[:, q], xs_t[bass.ds(j, 1), q].rearrange("o p f -> (o p) f")).then_inc(x_in[q], 16)

            @block.sync
            def _(sp):
                def group(j):
                    for q in range(R):
                        store = back(j, q, STORE)
                        if store:
                            jj, qq, i = store
                            sp.wait_ge(ysb_done, i + 1)
                            sp.dma_start(ys_t[bass.ds(jj, 1), qq].rearrange("o p f -> (o p) f"), ysb[:, qq]
                                         ).then_inc(y_out[qq], 16)
                        if not isinstance(j, int) or j < GROUPS:
                            load(sp, j, q)

                for j in range(3):
                    group(j)
                with sp.Fori(3, SHARED) as j:
                    group(j)
                sp.wait_ge(scattered, 16 * 2 * TT * B)
                with sp.Fori(SHARED, GROUPS) as j:
                    group(j)
                for j in range(GROUPS, GROUPS + 3):
                    group(j)
                for q in range(R):
                    sp.wait_ge(y_out[q], 16 * GROUPS)

            @block.gpsimd
            def _(pool):
                def batch(b):
                    wait_if(pool, scattered, b * (16 * 2 * TT))
                    for n in range(2):
                        pool.dma_start(xr[:, n], batch_rows(xs[0:B * S], b)).then_inc(xr_in, 16)
                    pool.wait_ge(xr_in, b * 32 + 32)
                    for n in range(2):
                        nc.gpsimd.tensor_copy(xr[:, n, :, D:D + 1], k["cw2"][:, n, bass.ds(b * TT, TT)].rearrange(
                            "p (t o) -> p t o", o=1)).then_inc(filled, 1)
                        nc.gpsimd.tensor_copy(idx[:, n], k["slots"][:, n, bass.ds(b * TT, TT)]).then_inc(filled, 1)
                    wait_apart(pool, k, filled, b * 4 + 4)
                    for n in range(2):
                        for t in range(TT):
                            pool.indirect_dma_start(xs, bass.IndirectOffsetOnAxis(ap=idx[:, n, t:t + 1], axis=0),
                                                    xr[:, n, t], None).then_inc(scattered, 16)

                over_batches(pool, batch)

            @block.tensor
            def _(pe):
                def step(j, q, es):
                    here, up, down = back(j, q, 0), back(j, q, UP), back(j, q, DOWN)
                    if here:
                        jj, qq, i = here
                        pe.wait_ge(x_in[qq], 16 * jj + 16)
                        wait_if(pe, xgT_done, i)
                        for c_ in range(DK):
                            last = nc.tensor.transpose(xtp[:, c_ * P:(c_ + 1) * P], xg[:, qq, c_ * P:(c_ + 1) * P],
                                                       k["ident"][:])
                        last.then_inc(xturned, 1)
                    if down:
                        jj, qq, i = down
                        pe.wait_ge(a_done, i + 1)
                        wait_if(pe, aT_done, i)
                        for m in range(MF):
                            last = nc.tensor.transpose(atp[:, m * P:(m + 1) * P], a[:, qq, m * P:(m + 1) * P],
                                                       k["ident"][:])
                        last.then_inc(aturned, 1)
                    if up:
                        jj, qq, i = up
                        e = es[q - UP + DOWN]
                        pe.wait_ge(xgT_done, i + 1)
                        wait_if(pe, t_done, 2 * i - 2)
                        for n in range(2):
                            for c_ in range(DK):
                                last = nc.tensor.matmul(hp[:, qq % 2, n], xgT[:, qq, c_], of_expert(k["w13"], e)[:, n, c_],
                                                        start=c_ == 0, stop=c_ == DK - 1)
                        last.then_inc(h_done, 1)
                    if down:
                        jj, qq, i = down
                        e = es[q]
                        pe.wait_ge(aT_done, i + 1)
                        wait_if(pe, ysb_done, i - 1)
                        for m in range(MF):
                            last = nc.tensor.matmul(yp[:, qq % 2, 0:D], aT[:, qq, m], of_expert(k["w2"], e)[:, m],
                                                    start=m == 0, stop=m == MF - 1)
                        last.then_inc(y_done, 1)

                groups(pe, step, mybir.EngineType.PE)

            @block.scalar
            def _(act):
                def step(j, q, es):
                    here, gate, down = (back(j, q, n) for n in (0, GATE, DOWN))
                    if here:
                        jj, qq, i = here
                        act.wait_ge(xturned, i + 1)
                        wait_if(act, h_done, i - R + 1)
                        nc.scalar.copy(xgT[:, qq].rearrange("p c s -> p (c s)"), xtp[:, 0:D]).then_inc(xgT_done, 1)
                    if down:
                        jj, qq, i = down
                        act.wait_ge(aturned, i + 1)
                        wait_if(act, y_done, i - R + 1)
                        nc.scalar.copy(aT[:, qq].rearrange("p c s -> p (c s)"), atp[:, 0:FF]).then_inc(aT_done, 1)
                    if gate:
                        jj, qq, i = gate
                        act.wait_ge(g_done, i + 1)
                        wait_if(act, gs_done, i - 1)
                        nc.scalar.activation(sg[:, qq % 2], g[:, qq % 2], ACT.Sigmoid, scale=ALPHA).then_inc(sg_done, 1)

                groups(act, step, None)

            @block.vector
            def _(dve):
                def step(j, q, es):
                    up, gate, down = back(j, q, UP), back(j, q, GATE), back(j, q, DOWN)
                    if gate:
                        jj, qq, i = gate
                        dve.wait_ge(cwc_done, i + 1)
                        dve.wait_ge(sg_done, i + 1)
                        nc.vector.scalar_tensor_tensor(gs[:], g[:, qq % 2], cwc[:, qq:qq + 1], sg[:, qq % 2], ALU.mult,
                                                       ALU.mult).then_inc(gs_done, 1)
                        dve.wait_ge(l_done, i + 1)
                        dve.wait_ge(gs_done, i + 1)
                        wait_if(dve, aturned, i - R + 1)
                        nc.vector.scalar_tensor_tensor(a[:, qq], l[:, qq % 2], 1.0, gs[:], ALU.add, ALU.mult).then_inc(a_done, 1)
                    if up:
                        jj, qq, i = up
                        e = es[q - UP + DOWN]
                        dve.wait_ge(x_in[qq], 16 * jj + 16)
                        nc.vector.tensor_copy(cwc[:, qq:qq + 1], xg[:, qq, D:D + 1]).then_inc(cwc_done, 1)
                        dve.wait_ge(h_done, i + 1)
                        for n, h in enumerate((t1, t3)):
                            nc.vector.tensor_tensor(h[:], hp[:, qq % 2, n], of_expert(k["b13"], e)[:, n],
                                                    ALU.add).then_inc(t_done, 1)
                        dve.wait_ge(t_done, 2 * i + 2)
                        nc.vector.tensor_tensor(hh[:], t1[:], t3[:], ALU.mult).then_inc(hh_done, 1)
                        dve.wait_ge(hh_done, i + 1)
                        pair = hh[:].rearrange("p (f two) -> p two f", two=2)
                        nc.vector.tensor_scalar(g[:, qq % 2], pair[:, 0], LIMIT, None, ALU.min).then_inc(g_done, 1)
                        nc.vector.tensor_scalar(l[:, qq % 2], pair[:, 1], LIMIT, -LIMIT, ALU.min, ALU.max).then_inc(l_done, 1)
                    if down:
                        jj, qq, i = down
                        e = es[q]
                        wait_if(dve, y_out[qq], 16 * jj)
                        dve.wait_ge(y_done, i + 1)
                        nc.vector.scalar_tensor_tensor(ysb[:, qq], of_expert(k["b2"], e), cwc[:, qq:qq + 1],
                                                       yp[:, qq % 2, 0:D], ALU.mult, ALU.add).then_inc(ysb_done, 1)

                groups(dve, step, mybir.EngineType.DVE)
        s.end()


def combine(nc, k, scratch, out):
    with ExitStack() as c:
        s = Scope(nc, c, "cb")
        x2, sh, ab = s.sb("x2", [P, 2, TT, D]), s.sb("sh", [P, 2, TT, D]), s.sb("ab", [P, 2, 2, TT, D])
        res = s.sb("res", [P, 2, TT, D])
        idx = s.sb("idx", [P, 2, 2, TT], U32)
        x_in, ab_in, r_out = ([s.sem(f"{n}{i}") for i in range(2)] for n in ("x_in", "ab_in", "r_out"))
        filled, added, step1, step2 = (s.sem(n) for n in ("filled", "added", "step1", "step2"))
        ys = scratch["ys"]
        orow = out.rearrange("b s d -> (b s) d")

        def pairs(eng, body):
            for h in range(2):
                body(0, h, h)
            with eng.Fori(1, B // 2) as j:
                for h in range(2):
                    body(j, h, j * 2 + h)

        def wait_if(eng, sem, value):
            if not isinstance(value, int) or value > 0:
                eng.wait_ge(sem, value)

        with nc.Block() as block:
            @block.sync
            def _(sp):
                def body(j, h, b):
                    wait_if(sp, added, 2 * j + h - 1)
                    sp.dma_start(x2[:, h], batch_rows(scratch["x2"], b)).then_inc(x_in[h], 16)
                    sp.dma_start(sh[:, h], batch_rows(ys[0:B * S], b)).then_inc(x_in[h], 16)

                pairs(sp, body)

            @block.gpsimd
            def _(pool):
                def body(j, h, b):
                    wait_if(pool, ab_in[h], j * (16 * 2 * TT))
                    nc.gpsimd.tensor_copy(idx[:, h], k["slots"][:, :, bass.ds(b * TT, TT)]).then_inc(filled, 1)
                    wait_if(pool, added, 2 * j + h - 1)
                    wait_apart(pool, k, filled, 2 * j + h + 1)
                    for n in range(2):
                        for t in range(TT):
                            pool.indirect_dma_start(ab[:, h, n, t], None, ys,
                                                    bass.IndirectOffsetOnAxis(ap=idx[:, h, n, t:t + 1], axis=0)
                                                    ).then_inc(ab_in[h], 16)

                pairs(pool, body)

            @block.vector
            def _(dve):
                def body(j, h, b):
                    n = 2 * j + h
                    flat = "p t d -> p (t d)"
                    dve.wait_ge(x_in[h], 32 * j + 32)
                    wait_if(dve, r_out[h], 16 * j)
                    nc.vector.tensor_tensor(res[:, h].rearrange(flat), x2[:, h].rearrange(flat), sh[:, h].rearrange(flat),
                                            ALU.add).then_inc(step1, 1)
                    dve.wait_ge(ab_in[h], j * (16 * 2 * TT) + 16 * 2 * TT)
                    dve.wait_ge(step1, n * 2 + 1)
                    nc.vector.tensor_tensor(res[:, h].rearrange(flat), res[:, h].rearrange(flat),
                                            ab[:, h, 0].rearrange(flat), ALU.add).then_inc(step1, 1)
                    dve.wait_ge(step1, n * 2 + 2)
                    nc.vector.tensor_tensor(res[:, h].rearrange(flat), res[:, h].rearrange(flat),
                                            ab[:, h, 1].rearrange(flat), ALU.add).then_inc(added, 1)

                pairs(dve, body)

            @block.scalar
            def _(act):
                def body(j, h, b):
                    act.wait_ge(added, 2 * j + h + 1)
                    act.dma_start(batch_rows(orow, b), res[:, h]).then_inc(r_out[h], 16)

                pairs(act, body)
                for h in range(2):
                    act.wait_ge(r_out[h], 16 * B // 2)
        s.end()


def decoder_layer(nc, w, out):
    def dram(name, shape, dt=F32):
        return nc.dram_tensor(name, shape, dt).ap()

    scratch = {
        "qkv": dram("scratch_qkv", [B * HEADS * S, 3 * HD]),
        "parts": dram("scratch_parts", [B, 2, 3, D, S], BF16),
        "o": dram("scratch_o", [B * S, D]),
        "x1": dram("scratch_x1", [B * S, D]),
        "v": dram("scratch_v", [B * S, D]),
        "x2": dram("scratch_x2", [B * S, D]),
        "xs": dram("scratch_xs", [NTILES * P, ROW]),
        "ys": dram("scratch_ys", [NTILES * P, D]),
    }
    k = {}
    with ExitStack() as ctx:
        with ExitStack() as early:
            prepare_weights(nc, ctx, early, w, k)
            project_self(nc, w, k, scratch)
            split_self(nc, w, k, scratch)
            attention(nc, w, k, scratch, cross=False)
            project_cross(nc, w, k, scratch)
            attention(nc, w, k, scratch, cross=True)
            route(nc, w, k, scratch)
            assign(nc, k)
        with ExitStack() as weights:
            load_experts(nc, w, k, weights)
            experts(nc, k, scratch)
        combine(nc, k, scratch, out)


_INS = {
    "x": "x", "ctx_1024": "ctx", "mask_Bx1xSxS2_ik1": "mask",
    "L0_attn_W_qkv": "W_qkv", "L0_attn_b_qkv": "b_qkv", "L0_attn_W_out": "W_out", "L0_attn_b_out": "b_out",
    "L0_xattn_adj": "adj", "L0_xattn_Wq": "Wq", "L0_xattn_bq": "bq", "L0_xattn_Wk": "Wk", "L0_xattn_bk": "bk",
    "L0_xattn_Wv": "Wv", "L0_xattn_bv": "bv", "L0_xattn_Wo": "Wo", "L0_xattn_bo": "bo",
    "L0_ffn_gate_w": "gate_w", "L0_ffn_gate_b": "gate_b", "L0_ffn_w1": "w1", "L0_ffn_b1": "b1", "L0_ffn_w3": "w3",
    "L0_ffn_b3": "b3", "L0_ffn_w2": "w2", "L0_ffn_b2": "b2", "L0_ffn_sw1": "sw1", "L0_ffn_sb1": "sb1",
    "L0_ffn_sw3": "sw3", "L0_ffn_sb3": "sb3", "L0_ffn_sw2": "sw2", "L0_ffn_sb2": "sb2",
}


def kernel(**inputs):
    import numpy as _np
    import concourse.bacc as _bacc
    from concourse import mybir as _mybir
    from concourse.bass_utils import run_bass_kernel_spmd as _run

    nc = _bacc.Bacc("TRN2", target_bir_lowering=False, num_devices=1)
    arrays, w = {}, {}
    for name, short in _INS.items():
        a = _np.ascontiguousarray(inputs[name])
        arrays[f"in_{name}_dram"] = a
        w[short] = nc.dram_tensor(f"in_{name}_dram", a.shape, _mybir.dt.from_np(a.dtype), kind="ExternalInput").ap()
    out = nc.dram_tensor("out_dram", (B, S, D), F32, kind="ExternalOutput").ap()
    decoder_layer(nc, w, out)
    r = _run(nc, [arrays], core_ids=[0])
    return r.results[0]["out_dram"]
```

```python
from contextlib import ExitStack

import concourse.bass as bass
from concourse import mybir

ALU = mybir.AluOpType
ACT = mybir.ActivationFunctionType
F32 = mybir.dt.float32
BF16 = mybir.dt.bfloat16
I32 = mybir.dt.int32
U32 = mybir.dt.uint32
AX_X = mybir.AxisListType.X

P = 128
B, S, D = 8, 512, 256
HEADS, HD = 16, 16
TT = S // P
DK = D // P
NE = 8
TOPK = 2
NX = NE + 1
FF = 256
MF = FF // P
ROUTED = -(-((TOPK * B * S + NE * (P - 1)) // P) // TT) * TT
NTILES = B * TT + ROUTED
ROW = D + 4
QUAD = 4
NQUAD = HEADS // QUAD
UNITS = HEADS * TT
NPART = 3
Q_SLOTS = (0, 1, 2, 0, 0, 1)
K_SLOTS = (2, 1, 0, 0, 1, 0)
NS = len(Q_SLOTS)
STACK_DMAS = 1 + NS - NPART
EPS = 1e-5
FILL = -1e30
HUGE = 3e38


class Scope:

    def __init__(self, nc, ctx, tag):
        self.nc, self.ctx, self.tag = nc, ctx, tag
        self.sems = []

    def sb(self, name, shape, dt=F32):
        return self.ctx.enter_context(self.nc.sbuf_tensor(f"{self.tag}_{name}", shape, dt))

    def ps(self, name, shape, dt=F32):
        return self.ctx.enter_context(self.nc.psum_tensor(f"{self.tag}_{name}", shape, dt))

    def sem(self, name):
        self.sems.append(self.nc.alloc_semaphore(name=f"{self.tag}_{name}"))
        return self.sems[-1]

    def end(self):
        self.nc.clear_and_free_semaphores(self.sems)
        self.nc.all_engine_barrier()


def place(which, part):
    return NPART - 1 - part if which else part


def wait_apart(eng, k, sem, value):
    eng.wait_ge(sem, value)
    eng.sem_inc(k["passed"], 1)


def over_batches(eng, body, n=B):
    body(0)
    with eng.Fori(1, n) as b:
        body(b)


def prepare_weights(nc, ctx, early, first, w, k):
    keep = Scope(nc, ctx, "k")
    k["passed"] = keep.sem("passed")
    k["ident"] = keep.sb("ident", [P, P])
    k["sel"], k["cw"] = keep.sb("sel", [P, B * TT, NE]), keep.sb("cw", [P, B * TT, NE])
    k["slots"], k["cw2"] = keep.sb("slots", [P, 2, B * TT], U32), keep.sb("cw2", [P, 2, B * TT])
    k["eidx"] = keep.sb("eidx", [P, NTILES + 8], I32)
    keep = Scope(nc, early, "ke")
    k["identb"] = keep.sb("identb", [P, P], BF16)
    k["eps"] = keep.sb("eps", [P, 1])
    k["wout"] = keep.sb("wout", [P, DK, D])
    k["bout"] = keep.sb("bout", [P, D])
    k["xw"] = keep.sb("xw", [P, 4, DK, D])
    k["bqk"] = keep.sb("bqk", [P, 2, DK])
    k["bv"] = keep.sb("bv", [P, D])
    k["bo"] = keep.sb("bo", [P, D])
    k["gateT"] = keep.sb("gateT", [P, DK, NE])
    k["gateb"] = keep.sb("gateb", [P, NE])
    keep = Scope(nc, first, "kf")
    k["causal"] = keep.sb("causal", [P, TT, S])
    k["wqkv"] = keep.sb("wqkv", [P, DK, 3 * D])
    k["bqkv"] = keep.sb("bqkv", [P, 3 * D])
    with ExitStack() as c:
        s = Scope(nc, c, "pw")
        raw = s.sb("raw", [P, 4, DK, D])
        graw = s.sb("graw", [NE, D])
        bq = s.sb("bq", [P, 3 * D])
        tp = s.ps("tp", [P, 4, S])
        tg = s.ps("tg", [P, S])
        loaded, ident_z, ident_1, ident_ok, identb_ok = (s.sem(n) for n in (
            "loaded", "ident_z", "ident_1", "ident_ok", "identb_ok"))
        turned, scaled, kept, causal_0, causal_1 = (s.sem(n) for n in (
            "turned", "scaled", "kept", "causal_0", "causal_1"))
        with nc.Block() as block:
            @block.sync
            def _(sp):
                sp.dma_start(k["wqkv"][:], w["W_qkv"].rearrange("(c p) f -> p c f", p=P)).then_inc(loaded, 16)
                sp.dma_start(k["wout"][:], w["W_out"].rearrange("(c p) f -> p c f", p=P)).then_inc(loaded, 16)
                for n, name in enumerate(("Wq", "Wk", "Wv", "Wo")):
                    sp.dma_start(raw[:, n], w[name].rearrange("(c p) e -> p c e", p=P)).then_inc(loaded, 16)
                sp.dma_start(graw[:], w["gate_w"]).then_inc(loaded, 16)
                for dst, name in ((bq, "b_qkv"), (k["bout"], "b_out"), (k["bv"], "bv"), (k["bo"], "bo"),
                                  (k["gateb"], "gate_b")):
                    n = w[name].shape[0]
                    sp.dma_start(dst[:], w[name].rearrange("(o f) -> o f", o=1).broadcast_to([P, n])).then_inc(loaded, 16)
                for n, name in enumerate(("bq", "bk")):
                    sp.dma_start(k["bqk"][:, n], w[name].rearrange("(c p) -> p c", p=P),
                                 allow_slow_non_contiguous=True).then_inc(loaded, 16)
                sp.wait_ge(loaded, 14 * 16)

            @block.gpsimd
            def _(pool):
                nc.gpsimd.memset(k["ident"][:], 0.0).then_inc(ident_z, 1)
                nc.gpsimd.memset(k["causal"][:], 0.0).then_inc(causal_0, 1)
                pool.wait_ge(ident_z, 1)
                nc.gpsimd.affine_select(out=k["ident"][:], in_=k["ident"][:], compare_op=ALU.not_equal, fill=1.0,
                                        base=0, pattern=[[-1, P]], channel_multiplier=1).then_inc(ident_ok, 1)
                pool.wait_ge(causal_0, 1)
                nc.gpsimd.affine_select(out=k["causal"][:], in_=k["causal"][:], compare_op=ALU.is_ge,
                                        fill=FILL, base=0, pattern=[[P, TT], [-1, S]],
                                        channel_multiplier=1).then_inc(causal_1, 1)
                pool.wait_ge(causal_1, 1)

            @block.tensor
            def _(pe):
                pe.wait_ge(loaded, 14 * 16)
                pe.wait_ge(ident_ok, 1)
                for n in range(4):
                    for ek in range(DK):
                        for fk in range(DK):
                            last = nc.tensor.transpose(tp[:, n, (ek * DK + fk) * P:(ek * DK + fk + 1) * P],
                                                       raw[:, n, fk, ek * P:(ek + 1) * P], k["ident"][:])
                    last.then_inc(turned, 1)
                for ek in range(DK):
                    last = nc.tensor.transpose(tg[:, ek * NE:(ek + 1) * NE], graw[:, ek * P:(ek + 1) * P],
                                               k["ident"][0:NE, 0:NE])
                last.then_inc(turned, 1)

            @block.vector
            def _(dve):
                nc.vector.memset(k["eps"][:], EPS).then_inc(kept, 1)
                dve.wait_ge(ident_ok, 1)
                nc.vector.tensor_copy(k["identb"][:], k["ident"][:]).then_inc(identb_ok, 1)
                dve.wait_ge(loaded, 14 * 16)
                sc = float((2 * D) ** -0.5)
                wq = k["wqkv"][:].rearrange("p c (n f) -> p (c n) f", f=3 * HD)[:, :, 0:HD]
                nc.vector.tensor_scalar(wq, wq, sc, None, ALU.mult).then_inc(scaled, 1)
                nc.vector.tensor_copy(k["bqkv"][:], bq[:]).then_inc(scaled, 1)
                dve.wait_ge(scaled, 2)
                bqs = k["bqkv"][:].rearrange("p (n f) -> p n f", f=3 * HD)[:, :, 0:HD]
                nc.vector.tensor_scalar(bqs, bqs, sc, None, ALU.mult).then_inc(scaled, 1)
                nc.vector.tensor_scalar(k["bqk"][:, 0], k["bqk"][:, 0], float(HD) ** -0.5, None,
                                        ALU.mult).then_inc(scaled, 1)
                for n in range(4):
                    dve.wait_ge(turned, n + 1)
                    nc.vector.tensor_copy(k["xw"][:, n].rearrange("p c f -> p (c f)"), tp[:, n]).then_inc(kept, 1)
                dve.wait_ge(turned, 5)
                nc.vector.tensor_copy(k["gateT"][:].rearrange("p c e -> p (c e)"), tg[:, 0:DK * NE]).then_inc(kept, 1)
                dve.wait_ge(kept, 6)
                dve.wait_ge(scaled, 4)
                dve.wait_ge(identb_ok, 1)
        s.end()


def norm_stats(nc, dve, k, x_of, stats, mv, stats_done, mv_done, b):
    for t in range(TT):
        last = nc.vector.bn_stats(stats[:, t], x_of(t))
    last.then_inc(stats_done, 1)
    wait_apart(dve, k, stats_done, b + 1)
    for t in range(TT):
        last = nc.vector.bn_aggr(mv[:, t], stats[:, t])
    last.then_inc(mv_done, 1)


def norm_sqrt(nc, act, k, mv, sd, mv_done, sd_done, b):
    act.wait_ge(mv_done, b + 1)
    nc.scalar.activation(sd[:], mv[:, :, 1], ACT.Sqrt, bias=k["eps"][:]).then_inc(sd_done, 1)


def norm_apply(nc, dve, x_of, xn_of, mv, sd, rstd, sd_done, rstd_done, xn_done, b):
    dve.wait_ge(sd_done, b + 1)
    nc.vector.reciprocal(rstd[:], sd[:]).then_inc(rstd_done, 1)
    dve.wait_ge(rstd_done, b + 1)
    for t in range(TT):
        nc.vector.tensor_scalar(xn_of(t), x_of(t), mv[:, t, 0:1], rstd[:, t:t + 1],
                                ALU.subtract, ALU.mult).then_inc(xn_done, 1)


def batch_rows(ap, b, n=B):
    return ap.rearrange("(b t p) f -> b p t f", b=n, p=P)[bass.ds(b, 1)].rearrange("o p t f -> (o p) t f")


def turn_batch(nc, pe, k, dst, src, ready, ready_base, done):
    for t in range(TT):
        if ready is not None:
            pe.wait_ge(ready, ready_base + t + 1)
        for c_ in range(DK):
            last = nc.tensor.transpose(dst[:, c_, t * P:(t + 1) * P], src[:, t, c_ * P:(c_ + 1) * P], k["ident"][:])
    last.then_inc(done, 1)


def project_self(nc, w, k, scratch):
    with ExitStack() as c:
        s = Scope(nc, c, "ps")
        x = s.sb("x", [P, TT, D])
        xn = s.sb("xn", [P, TT, D])
        xnT = s.sb("xnT", [P, DK, S])
        stats, mv, sd, rstd = s.sb("stats", [P, TT, 6]), s.sb("mv", [P, TT, 2]), s.sb("sd", [P, TT]), s.sb("rstd", [P, TT])
        qkv = s.sb("qkv", [P, TT, 3 * D])
        G = 2
        GH = HEADS // G
        U = 2 * G
        src = s.sb("src", [P, G, TT, 2, GH, HD])
        parts = s.sb("parts", [P, U, NPART, S], BF16)
        rest = s.sb("rest", [P, U, S])
        tp = s.ps("tp", [P, DK, S])
        acc = s.ps("acc", [P, 2, 2 * S])
        up = s.ps("up", [P, 2, S])
        x_in, stored = ([s.sem(f"{n}{t}") for t in range(TT)] for n in ("x_in", "stored"))
        src_in = [s.sem(f"src_in{g}") for g in range(G)]
        parts_out = [s.sem(f"parts_out{u}") for u in range(U)]
        (stats_done, mv_done, sd_done, rstd_done, xn_done, turned, xnT_done, acc_done, qkv_done, u_turned, hi_done,
         rest_done, mid_done, lo_done) = (s.sem(n) for n in (
            "stats_done", "mv_done", "sd_done", "rstd_done", "xn_done", "turned", "xnT_done", "acc_done", "qkv_done",
            "u_turned", "hi_done", "rest_done", "mid_done", "lo_done"))
        xr = w["x"].rearrange("b (t p) d -> b t p d", p=P)
        rows = scratch["qkv"].rearrange("(b t p r) f -> b t p (r f)", t=TT, p=P, r=HEADS)
        rows_of = scratch["qkv"].rearrange("(b g h t p) f -> b g t p h f", b=B, g=G, t=TT, p=P)

        def steps(step):
            def run(eng):
                step(eng, 0, True, False, True)
                step(eng, 1, True, False, True)
                step(eng, 2, True, True, True)
                with eng.Fori(3, B - 1) as b:
                    step(eng, b, True, True, True)
                step(eng, B - 1, True, True, False)
                step(eng, B, False, True, False)
                step(eng, B + 1, False, True, False)
            return run

        with nc.Block() as block:
            def load(sp, b):
                for t in range(TT):
                    sp.dma_start(x[:, t], xr[bass.ds(b, 1), t].rearrange("o p d -> (o p) d")).then_inc(x_in[t], 16)

            def sp_step(sp, b, project, split, ahead):
                if ahead:
                    sp.wait_ge(xn_done, b * TT + TT)
                    load(sp, b + 1)
                back = not isinstance(b, int) or 1 <= b <= B
                if back:
                    for t in range(TT):
                        wait_apart(sp, k, stored[t], b * 16)
                for g in range(G):
                    if project:
                        for t in (2 * g, 2 * g + 1):
                            sp.wait_ge(qkv_done, b * TT + t + 1)
                            sp.dma_start(rows[bass.ds(b, 1), t].rearrange("o p d -> (o p) d"), qkv[:, t]
                                         ).then_inc(stored[t], 16)
                    if back:
                        if split:
                            sp.wait_ge(u_turned, (b - 2) * U + 2 * g + 2)
                        for t in range(TT):
                            for qk in range(2):
                                sp.dma_start(src[:, g, t, qk], rows_of[bass.ds(b - 1, 1), g, t, :, :, qk * HD:(qk + 1) * HD
                                                                       ].rearrange("o p h e -> (o p) h e")
                                             ).then_inc(src_in[g], 16)

            @block.sync
            def _(sp):
                load(sp, 0)
                steps(sp_step)(sp)

            @block.gpsimd
            def _(pool):
                def batch(b):
                    for u in range(U):
                        wait_apart(pool, k, lo_done, b * U + u + 1)
                        pool.dma_start(scratch["parts"][bass.ds(b, 1), u % 2, (u // 2) * P:(u // 2 + 1) * P].rearrange(
                            "o p c s -> (o p) c s"), parts[:, u]).then_inc(parts_out[u], 16)

                over_batches(pool, batch)
                for u in range(U):
                    pool.wait_ge(parts_out[u], 16 * B)

            def turn_xn(pe, b):
                pe.wait_ge(xnT_done, b * DK)
                turn_batch(nc, pe, k, tp, xn, xn_done, b * TT, turned)

            def pe_step(pe, b, project, split, ahead):
                if project:
                    pe.wait_ge(xnT_done, b * DK + DK)
                for t in range(TT):
                    if project:
                        if not (isinstance(b, int) and b == 0 and t < 2):
                            pe.wait_ge(qkv_done, b * TT + t - 1)
                        for lo, hi in ((0, S), (S, 3 * D)):
                            for c_ in range(DK):
                                last = nc.tensor.matmul(acc[:, t % 2, lo:hi], xnT[:, c_, t * P:(t + 1) * P],
                                                        k["wqkv"][:, c_, lo:hi], start=c_ == 0, stop=c_ == DK - 1)
                        last.then_inc(acc_done, 1)
                    if ahead and t == TT - 1:
                        turn_xn(pe, b + 1)
                    if split:
                        u, n = t, (b - 2) * U + t
                        g, qk = u // 2, u % 2
                        if qk == 0:
                            pe.wait_ge(src_in[g], (b - 1) * (16 * 2 * TT))
                        if not (isinstance(n, int) and n < 2):
                            pe.wait_ge(rest_done, n - 1)
                        for t_ in range(TT):
                            last = nc.tensor.transpose(up[:, u % 2, t_ * P:(t_ + 1) * P],
                                                       src[:, g, t_, qk].rearrange("p h e -> p (h e)"), k["ident"][:])
                        last.then_inc(u_turned, 1)

            @block.tensor
            def _(pe):
                turn_xn(pe, 0)
                steps(pe_step)(pe)

            def keep_xnT(act, b):
                act.wait_ge(turned, b + 1)
                act.wait_ge(acc_done, b * TT)
                for c_ in range(DK):
                    nc.scalar.copy(xnT[:, c_], tp[:, c_]).then_inc(xnT_done, 1)

            def act_step(act, b, project, split, ahead):
                for u in range(U):
                    if ahead and u == U // 2:
                        norm_sqrt(nc, act, k, mv, sd, mv_done, sd_done, b + 1)
                    if ahead and u == U - 1:
                        keep_xnT(act, b + 1)
                    if split:
                        n = (b - 2) * U + u
                        act.wait_ge(u_turned, n + 1)
                        if not (isinstance(b, int) and b == 2):
                            act.wait_ge(parts_out[u], (b - 2) * 16)
                        nc.scalar.copy(parts[:, u, place(u % 2, 0)], up[:, u % 2]).then_inc(hi_done, 1)
                        act.wait_ge(rest_done, n + 1)
                        nc.scalar.copy(parts[:, u, place(u % 2, 1)], rest[:, u]).then_inc(mid_done, 1)

            @block.scalar
            def _(act):
                norm_sqrt(nc, act, k, mv, sd, mv_done, sd_done, 0)
                keep_xnT(act, 0)
                steps(act_step)(act)

            def take_stats(dve, b):
                for t in range(TT):
                    dve.wait_ge(x_in[t], b * 16 + 16)
                norm_stats(nc, dve, k, lambda t: x[:, t], stats, mv, stats_done, mv_done, b)

            def apply_norm(dve, b):
                dve.wait_ge(turned, b)
                norm_apply(nc, dve, lambda t: x[:, t], lambda t: xn[:, t], mv, sd, rstd, sd_done, rstd_done, xn_done, b)

            def dve_step(dve, b, project, split, ahead):
                def split_rest(u):
                    dve.wait_ge(hi_done, (b - 2) * U + u + 1)
                    nc.vector.tensor_tensor(rest[:, u], up[:, u % 2], parts[:, u, place(u % 2, 0)],
                                            ALU.subtract).then_inc(rest_done, 1)

                def split_lo(u):
                    dve.wait_ge(mid_done, (b - 2) * U + u + 1)
                    nc.vector.tensor_tensor(parts[:, u, place(u % 2, 2)], rest[:, u], parts[:, u, place(u % 2, 1)],
                                            ALU.subtract).then_inc(lo_done, 1)

                for t in range(TT):
                    if ahead and t == TT - 2:
                        take_stats(dve, b + 1)
                    if ahead and t == TT - 1:
                        apply_norm(dve, b + 1)
                    if project:
                        dve.wait_ge(acc_done, b * TT + t + 1)
                        dve.wait_ge(stored[t], b * 16)
                        nc.vector.tensor_tensor(qkv[:, t, 0:S], acc[:, t % 2, 0:S], k["bqkv"][:, 0:S], ALU.add)
                        nc.vector.tensor_tensor(qkv[:, t, S:3 * D], acc[:, t % 2, S:3 * D], k["bqkv"][:, S:3 * D],
                                                ALU.add).then_inc(qkv_done, 1)
                    if split:
                        if t > 0:
                            split_lo(t - 1)
                        split_rest(t)
                if split:
                    split_lo(TT - 1)

            @block.vector
            def _(dve):
                take_stats(dve, 0)
                apply_norm(dve, 0)
                steps(dve_step)(dve)
        s.end()



def load_stacks(sp, parts, b, q, slot, stacks):
    hs = slice(q * QUAD * HD, (q + 1) * QUAD * HD)
    for which, (dst, slots, sem) in enumerate(stacks):
        sp.dma_start(dst[0:NPART * HD, slot],
                     parts[bass.ds(b, 1), which, hs].rearrange("o (h e) c s -> (o e c) h s", e=HD)
                     ).then_inc(sem[slot], 16)
        for n in range(NPART, NS):
            sp.dma_start(dst[n * HD:(n + 1) * HD, slot],
                         parts[bass.ds(b, 1), which, hs, place(which, slots[n])].rearrange(
                             "o (h e) s -> (o e) h s", e=HD)).then_inc(sem[slot], 16)


def attention_cross(nc, w, k, scratch):
    with ExitStack() as c:
        s = Scope(nc, c, "xa")
        NSC, NPT, NA, NP_, NM = 2, 4, 4, 8, UNITS
        TURN, COPY = 3, 4
        PV_AT = (7, 11, 15, 3)
        qs = s.sb("qs", [NS * HD, 2, QUAD, S], BF16)
        ks = s.sb("ks", [NS * HD, 2, QUAD, S], BF16)
        v = s.sb("v", [P, 2, QUAD, TT, 32])
        neg = s.sb("neg", [P, NA, S])
        nmax = s.sb("nmax", [P, NM])
        prob = s.sb("prob", [P, NP_, S])
        pT = s.sb("pT", [P, 2, QUAD, TT, TT, P])
        oT = s.sb("oT", [P, S])
        rsum = s.sb("rsum", [P, TT, QUAD])
        o = s.sb("o", [P, 2, TT * QUAD, HD])
        sc = s.ps("sc", [P, NSC, S])
        ptp = s.ps("ptp", [P, NPT, S])
        acc = s.ps("acc", [P, S])
        otp = s.ps("otp", [P, S])
        adj = s.sb("adj", [P, TT, S])
        mask = s.sb("mask", [P, TT, S], I32)
        fill = s.sb("fill", [P, TT, S])
        bias = s.sb("bias", [P, TT, S])
        den, inv = s.sb("den", [P, TT, QUAD]), s.sb("inv", [P, TT, QUAD])
        adj_in, mask_in, fill_done, bias_done, den_done, inv_done = (s.sem(n) for n in (
            "adj_in", "mask_in", "fill_done", "bias_done", "den_done", "inv_done"))
        q_in, k_in, v_in, o_out = ([s.sem(f"{n}{i}") for i in range(2)] for n in ("q_in", "k_in", "v_in", "o_out"))
        (ones_done, sc_done, neg_done, prob_done, turned, copied_d, copied_a, pv_done, oT_done, oturned, rsum_done,
         o_done) = (s.sem(n) for n in ("ones_done", "sc_done", "neg_done", "prob_done", "turned", "copied_d",
                                       "copied_a", "pv_done", "oT_done", "oturned", "rsum_done", "o_done"))
        QU = QUAD * TT

        ON_DVE = (0, 3, 6)

        def on_dve(j):
            return j % 8 in ON_DVE

        def copied_by(j, dve_side):
            n = (j + 1) // 8 * len(ON_DVE) + sum(i < (j + 1) % 8 for i in ON_DVE)
            return n if dve_side else j + 1 - n

        def wait_copied(eng, b, j):
            for sem, dve_side in ((copied_d, True), (copied_a, False)):
                value = b * copied_by(UNITS - 1, dve_side) + copied_by(j, dve_side)
                if not isinstance(value, int) or value > 0:
                    eng.wait_ge(sem, value)

        def steps(emit):
            def run(eng):
                emit(eng, 0, range(UNITS), True)
                with eng.Fori(1, B) as b:
                    emit(eng, b, range(UNITS), False)
                emit(eng, B - 1, range(UNITS, UNITS + 2 * QU), False)
            return run

        parts = scratch["parts"]
        vrows = scratch["v"].rearrange("(b t p) (q h e) -> b q t p h e", b=B, p=P, h=QUAD, e=HD)
        orows = scratch["o"].rearrange("(b t p) (q f) -> b q p t f", b=B, p=P, q=NQUAD)

        with nc.Block() as block:
            def load_quad(sp, b, q):
                load_stacks(sp, parts, b, q, q % 2, ((qs, Q_SLOTS, q_in), (ks, K_SLOTS, k_in)))

            def load_v(sp, b, q):
                for t in range(TT):
                    sp.dma_start(v[:, q % 2, :, t, 0:HD], vrows[bass.ds(b, 1), q, t].rearrange("o p h e -> (o p) h e")
                                 ).then_inc(v_in[q % 2], 16)

            def loads(sp, b, first):
                if not first:
                    sp.wait_ge(fill_done, b * TT)
                sp.dma_start(mask[:], w["mask"][bass.ds(b, 1)].rearrange("o u (t p) s -> (o p) (u t) s", p=P)
                             ).then_inc(mask_in, 16)
                for q in range(NQUAD):
                    if not (first and q < 2):
                        sp.wait_ge(sc_done, b * UNITS + (q - 1) * QU)
                    load_quad(sp, b, q)
                    if not (first and q < 2):
                        sp.wait_ge(pv_done, b * NQUAD + q - 1)
                    load_v(sp, b, q)

            @block.sync
            def _(sp):
                sp.wait_ge(ones_done, 1)
                sp.dma_start(adj[:], w["adj"].rearrange("(t p) s -> p t s", p=P)).then_inc(adj_in, 16)
                loads(sp, 0, True)
                with sp.Fori(1, B) as b:
                    loads(sp, b, False)

            @block.gpsimd
            def _(pool):
                nc.gpsimd.memset(v[:].rearrange("p a h t e -> p (a h t e)"), 1.0).then_inc(ones_done, 1)
                def fill_masked(b):
                    pool.wait_ge(mask_in, b * 16 + 16)
                    if not isinstance(b, int) or b > 0:
                        wait_apart(pool, k, bias_done, b * TT)
                    for t in range(TT):
                        nc.gpsimd.tensor_scalar(fill[:, t], mask[:, t], 0, FILL, ALU.is_equal,
                                                ALU.mult).then_inc(fill_done, 1)

                def batch(b, last=False):
                    for q in range(NQUAD):
                        if q == 2 and not last:
                            fill_masked(b + 1)
                        wait_apart(pool, k, o_done, b * NQUAD + q + 1)
                        pool.dma_start(orows[bass.ds(b, 1), q].rearrange("o p t f -> (o p) t f"),
                                       o[:, q % 2].rearrange("p (t h) e -> p t (h e)", t=TT)).then_inc(o_out[q % 2], 16)

                fill_masked(0)
                over_batches(pool, batch, B - 1)
                batch(B - 1, last=True)
                for i in range(2):
                    pool.wait_ge(o_out[i], 16 * (B * NQUAD // 2))

            def pe_steps(pe, b, js, first):
                for j in js:
                    q, jj, t = j // QU, j % QU, j % TT
                    if j < UNITS:
                        h = jj // TT
                        if jj == 0:
                            n = 2 * b + q // 2 + 1
                            pe.wait_ge(q_in[q % 2], n * 16 * STACK_DMAS)
                            pe.wait_ge(k_in[q % 2], n * 16 * STACK_DMAS)
                        if not (first and j < NSC):
                            pe.wait_ge(neg_done, b * UNITS + j - NSC + 1)
                        nc.tensor.matmul(sc[:, j % NSC],
                                         qs[:, q % 2, h, t * P:(t + 1) * P], ks[:, q % 2, h],
                                         start=True, stop=True).then_inc(sc_done, 1)
                    i = j - TURN
                    if not (first and i < 0) and i < UNITS:
                        it = i % TT
                        pe.wait_ge(prob_done, b * UNITS + i + 1)
                        if not (first and i < NPT):
                            wait_copied(pe, b, i - NPT)
                        for kt in range(S // P):
                            last = nc.tensor.transpose(ptp[:, i % NPT, kt * P:(kt + 1) * P],
                                                       prob[:, i % NP_, kt * P:(kt + 1) * P], k["ident"][:])
                        last.then_inc(turned, 1)
                    back = 1 if jj >= PV_AT[0] else 2
                    if jj in PV_AT and not (first and q < back) and q - back < NQUAD:
                        pq, kt = q - back, PV_AT.index(jj)
                        if kt == 0:
                            wait_copied(pe, b, pq * QU + QU - 1)
                            pe.wait_ge(v_in[pq % 2], (2 * b + pq // 2 + 1) * 16 * TT)
                            if not (first and pq < 1):
                                pe.wait_ge(oT_done, b * NQUAD + pq)
                        for h in range(QUAD):
                            last = nc.tensor.matmul(acc[32 * h:32 * h + 32], v[:, pq % 2, h, kt, :],
                                                    pT[:, pq % 2, h, :, kt, :], start=kt == 0, stop=kt == TT - 1,
                                                    tile_position=(0, 32 * h))
                        if kt == TT - 1:
                            last.then_inc(pv_done, 1)
                    if jj == 6 and not (first and q < 2) and q - 2 < NQUAD:
                        pe.wait_ge(oT_done, b * NQUAD + q - 1)
                        if not (first and q < 3):
                            pe.wait_ge(o_done, b * NQUAD + q - 2)
                        for t_ in range(TT):
                            last = nc.tensor.transpose(otp[:, t_ * P:(t_ + 1) * P], oT[:, t_ * P:(t_ + 1) * P], k["ident"][:])
                        last.then_inc(oturned, 1)

            block.tensor(steps(pe_steps))

            def dve_steps(dve, b, js, first):
                for j in js:
                    q, jj, t = j // QU, j % QU, j % TT
                    if j < UNITS:
                        if j == 0 and first:
                            dve.wait_ge(adj_in, 16)
                        if j < TT:
                            dve.wait_ge(fill_done, b * TT + j + 1)
                            nc.vector.scalar_tensor_tensor(bias[:, j], fill[:, j], 1.0, adj[:, j], ALU.mult,
                                                           ALU.add).then_inc(bias_done, 1)
                            dve.wait_ge(bias_done, b * TT + j + 1)
                        if not (first and j < NA):
                            dve.wait_ge(prob_done, b * UNITS + j - NA + 1)
                        wait_apart(dve, k, sc_done, b * UNITS + j + 1)
                        nc.vector.tensor_tensor_reduce(out=neg[:, j % NA], in0=sc[:, j % NSC],
                                                       in1=bias[:, t], scale=-1.0, scalar=HUGE, op0=ALU.add,
                                                       op1=ALU.min, accum_out=nmax[:, j % NM:j % NM + 1]
                                                       ).then_inc(neg_done, 1)
                    i = j - COPY
                    if not (first and i < 0) and i < UNITS and on_dve(i):
                        copy_out(dve, nc.vector.tensor_copy, copied_d, b, i, first)
                    if jj == 8 and not (first and q < 2) and q - 2 < NQUAD:
                        pq = q - 2
                        dve.wait_ge(oturned, b * NQUAD + pq + 1)
                        if not (first and pq < 2):
                            dve.wait_ge(o_out[pq % 2], (2 * b + pq // 2) * 16)
                        ov = otp[:].rearrange("p (n e) -> p n e", e=32)
                        m0 = (pq * QU) % NM
                        nm = nmax[:, m0:m0 + QU].rearrange("p (h t) -> p t h", t=TT)
                        nc.vector.scalar_tensor_tensor(den[:], nm, -FILL / 2, ov[:, :, HD].rearrange(
                            "p (t h) -> p t h", h=QUAD), ALU.is_lt, ALU.mult).then_inc(den_done, 1)
                        dve.wait_ge(den_done, b * NQUAD + pq + 1)
                        nc.vector.reciprocal(inv[:], den[:]).then_inc(inv_done, 1)
                        dve.wait_ge(inv_done, b * NQUAD + pq + 1)
                        nc.vector.scalar_tensor_tensor(rsum[:], nm, -FILL / 2, inv[:], ALU.is_lt,
                                                       ALU.mult).then_inc(rsum_done, 1)
                        dve.wait_ge(rsum_done, b * NQUAD + pq + 1)
                        nc.vector.tensor_tensor(o[:, pq % 2], ov[:, :, 0:HD], rsum[:].rearrange(
                            "p t (h o) -> p (t h) o", o=1).broadcast_to([P, TT * QUAD, HD]), ALU.mult).then_inc(o_done, 1)

            def copy_out(eng, copy, sem, b, i, first):
                iq, ih, it = i // QU, (i % QU) // TT, i % TT
                eng.wait_ge(turned, b * UNITS + i + 1)
                if i % QU < 2 and not (first and iq < 2):
                    eng.wait_ge(pv_done, b * NQUAD + iq - 1)
                copy(pT[:, iq % 2, ih, it].rearrange("p a s -> p (a s)"), ptp[:, i % NPT]).then_inc(sem, 1)

            block.vector(steps(dve_steps))

            def act_steps(act, b, js, first):
                for j in js:
                    q, jj, t = j // QU, j % QU, j % TT
                    i = j - COPY
                    if not (first and i < 0) and i < UNITS and not on_dve(i):
                        copy_out(act, nc.scalar.copy, copied_a, b, i, first)
                    if j < UNITS:
                        act.wait_ge(neg_done, b * UNITS + j + 1)
                        if not (first and j < NP_):
                            act.wait_ge(turned, b * UNITS + j - NP_ + 1)
                        nc.scalar.activation(prob[:, j % NP_], neg[:, j % NA], ACT.Exp,
                                             bias=nmax[:, j % NM:j % NM + 1], scale=-1.0).then_inc(prob_done, 1)
                    if jj == 4 and not (first and q < 2) and q - 2 < NQUAD:
                        act.wait_ge(pv_done, b * NQUAD + q - 1)
                        if not (first and q < 3):
                            act.wait_ge(oturned, b * NQUAD + q - 2)
                        nc.scalar.copy(oT[:], acc[:]).then_inc(oT_done, 1)

            block.scalar(steps(act_steps))
        s.end()


def attention_causal(nc, w, k, scratch):
    with ExitStack() as c:
        s = Scope(nc, c, "sa")
        NSC, NST, DEPTH = 4, 2, NS * HD
        QU = QUAD * TT
        PV_AT, LAST = (2, 5, 8, 11), 4
        NC = 3
        qs = s.sb("qs", [DEPTH + NC, NQUAD, QUAD, S], BF16)
        ks = s.sb("ks", [DEPTH + NC, NQUAD, QUAD, S], BF16)
        v = s.sb("v", [P, NQUAD, QUAD * TT, 32])
        neg = s.sb("neg", [P, NSC, S])
        nmax = s.sb("nmax", [P, NQUAD, TT * QUAD])
        mrest, mrest2 = s.sb("mrest", [P, TT * QUAD]), s.sb("mrest2", [P, TT * QUAD])
        mparts = s.sb("mparts", [P, TT, NC, QUAD], BF16)
        mrow = s.sb("mrow", [NC * QUAD, S], BF16)
        later = s.sb("later", [P, P], BF16)
        pT = s.sb("pT", [P, 2, QUAD, TT, S])
        oT = s.sb("oT", [P, S])
        rsum = s.sb("rsum", [P, TT, QUAD])
        o = s.sb("o", [P, 2, QUAD * TT, HD])
        sc = s.ps("sc", [P, NSC, S])
        st = s.ps("st", [P, NST, S])
        acc = s.ps("acc", [P, S])
        misc = s.ps("misc", [P, S])
        q_in, k_in, v_in = ([s.sem(f"{n}{i}") for i in range(NQUAD)] for n in ("q_in", "k_in", "v_in"))
        o_out = [s.sem(f"o_out{i}") for i in range(2)]
        (ones_done, later_0, later_done, sc_done, neg_done, m_step, mparts_done, mp_done, mrow_done, m_in, st_done,
         exp_done, pv_done, oT_done, oturned, rsum_done, o_done) = (s.sem(n) for n in (
            "ones_done", "later_0", "later_done", "sc_done", "neg_done", "m_step", "mparts_done", "mp_done",
            "mrow_done", "m_in", "st_done", "exp_done", "pv_done", "oT_done", "oturned", "rsum_done", "o_done"))
        o_free = s.sem("o_free")
        parts = scratch["parts"]
        vrows = scratch["qkv"].rearrange("(b q n p) f -> b q p n f", b=B, q=NQUAD, p=P)
        orows = scratch["o"].rearrange("r (c e) -> (r c) e", e=HD).rearrange("(b q n p) e -> b q p n e", b=B, q=NQUAD, p=P)

        def steps(emit):
            def run(eng):
                emit(eng, 0, range(UNITS), True)
                with eng.Fori(1, B) as b:
                    emit(eng, b, range(UNITS), False)
                emit(eng, B - 1, range(UNITS, UNITS + LAST * QU), False)
            return run

        def lagging(q, n, first):
            return q - n if q - n < NQUAD and not (first and q < n) else None

        with nc.Block() as block:
            def load(sp, b, q):
                load_stacks(sp, parts, b, q, q, ((qs, Q_SLOTS, q_in), (ks, K_SLOTS, k_in)))

            def load_v(sp, b, q):
                sp.dma_start(v[:, q, :, 0:HD], vrows[bass.ds(b, 1), q, :, :, 2 * HD:3 * HD].rearrange(
                    "o p n e -> (o p) n e")).then_inc(v_in[q], 16)

            def put_rows(sp, b, q):
                slot = (q - 1) % NQUAD
                sp.wait_ge(mrow_done, b * NQUAD + q)
                for part in range(NC):
                    sp.dma_start(qs[DEPTH + part:DEPTH + part + 1, slot].rearrange("o h s -> o (h s)"),
                                 mrow[part * QUAD:(part + 1) * QUAD]).then_inc(m_in, 16)

            @block.sync
            def _(sp):
                def ahead(b, q):
                    first = isinstance(b, int) and b == 0
                    if not (first and q == 0):
                        put_rows(sp, b, q)
                    if not (first and q < 3):
                        sp.wait_ge(pv_done, b * NQUAD + q - 2)
                        load_v(sp, b if q < 3 else b + 1, (q + 1) % NQUAD)
                    if not (first and q < 2):
                        sp.wait_ge(st_done, b * UNITS + (q - 1) * QU)
                        load(sp, b if q < 2 else b + 1, (q + 2) % NQUAD)

                def turn(b):
                    ahead(b - 1, 2)
                    ahead(b - 1, 3)
                    ahead(b, 0)
                    ahead(b, 1)

                for q in range(2):
                    load(sp, 0, q)
                sp.wait_ge(ones_done, 1)
                for q in range(NQUAD):
                    if q >= 2:
                        load(sp, 0, q)
                    load_v(sp, 0, q)
                ahead(0, 1)
                turn(1)
                with sp.Fori(2, B) as b:
                    turn(b)
                put_rows(sp, B - 1, 2)
                sp.wait_ge(pv_done, B * NQUAD - NQUAD)
                load_v(sp, B - 1, 3)
                put_rows(sp, B - 1, 3)
                put_rows(sp, B - 1, 4)

            @block.gpsimd
            def _(pool):
                pool.sem_inc(o_free, 2)
                nc.gpsimd.memset(v[:].rearrange("p q n e -> p (q n e)"), 1.0).then_inc(ones_done, 1)
                pool.wait_ge(ones_done, 1)
                nc.gpsimd.memset(ks[DEPTH:DEPTH + NC].rearrange("p q h s -> p (q h s)"), 1.0).then_inc(later_done, 1)
                pool.wait_ge(later_done, 1)
                nc.gpsimd.memset(later[:], 0.0).then_inc(later_0, 1)
                pool.wait_ge(later_0, 1)
                nc.gpsimd.affine_select(out=later[:], in_=later[:], compare_op=ALU.is_ge, fill=FILL, base=0,
                                        pattern=[[1, P]], channel_multiplier=-1).then_inc(later_done, 1)

                def store(b, q):
                    wait_apart(pool, k, o_done, b * NQUAD + q + 1)
                    pool.dma_start(orows[bass.ds(b, 1), q].rearrange("o p n e -> (o p) n e"),
                                   o[:, q % 2]).then_inc(o_out[q % 2], 16)
                    if not (isinstance(b, int) and b == 0 and q == 0):
                        pool.wait_ge(o_out[(q - 1) % 2], (b * 2 + (q - 1) // 2 + 1) * 16)
                        pool.sem_inc(o_free, 1)

                def split_max(b, q):
                    first = isinstance(b, int) and b == 0
                    n = [0]

                    def then(ins):
                        n[0] += 1
                        ins.then_inc(m_step, 1)
                        wait_apart(pool, k, m_step, (b * NQUAD + q) * 4 + n[0])

                    def mp(part):
                        return mparts[:, :, part]

                    def wide(a):
                        return a.rearrange("p (t h) -> p t h", h=QUAD)

                    wait_apart(pool, k, neg_done, b * UNITS + (q + 1) * QU)
                    if not (first and q == 0):
                        wait_apart(pool, k, mp_done, b * NQUAD + q)
                    then(nc.gpsimd.tensor_copy(mp(0), wide(nmax[:, q])))
                    then(nc.gpsimd.tensor_tensor(wide(mrest[:]), wide(nmax[:, q]), mp(0), ALU.subtract))
                    then(nc.gpsimd.tensor_copy(mp(1), wide(mrest[:])))
                    then(nc.gpsimd.tensor_tensor(wide(mrest2[:]), wide(mrest[:]), mp(1), ALU.subtract))
                    nc.gpsimd.tensor_copy(mp(2), wide(mrest2[:])).then_inc(mparts_done, 1)

                for q in range(NQUAD):
                    split_max(0, q)
                def turn(b):
                    for q in range(NQUAD):
                        split_max(b, q)
                        store(b - 1, q)

                turn(1)
                with pool.Fori(2, B) as b:
                    turn(b)
                for q in range(NQUAD):
                    store(B - 1, q)
                for i in range(2):
                    pool.wait_ge(o_out[i], 16 * (B * NQUAD // 2))

            def pe_steps(pe, b, js, first):
                for j in js:
                    q, jj, t = j // QU, j % QU, j % TT
                    if j < UNITS:
                        h, W = jj // TT, (t + 1) * P
                        if jj == 0:
                            pe.wait_ge(q_in[q], b * (16 * STACK_DMAS) + 16 * STACK_DMAS)
                            pe.wait_ge(k_in[q], b * (16 * STACK_DMAS) + 16 * STACK_DMAS)
                        if not (first and j < NSC):
                            pe.wait_ge(neg_done, b * UNITS + j - NSC + 1)
                        nc.tensor.matmul(sc[:, j % NSC, 0:W], qs[0:DEPTH, q, h, t * P:(t + 1) * P],
                                         ks[0:DEPTH, q, h, 0:W], start=True, stop=True).then_inc(sc_done, 1)
                    mq = lagging(q, 1, first)
                    if jj == 6 and mq is not None:
                        pe.wait_ge(mparts_done, b * NQUAD + mq + 1)
                        if not (first and q < LAST):
                            pe.wait_ge(o_done, b * NQUAD + q - LAST + 1)
                        for t_ in range(TT):
                            last = nc.tensor.matmul(misc[0:NC * QUAD, t_ * P:(t_ + 1) * P],
                                                    mparts[:, t_].rearrange("p c h -> p (c h)"), k["identb"][:],
                                                    start=True, stop=True)
                        last.then_inc(mp_done, 1)
                    i = j - 2 * QU
                    if not (first and i < 0) and i < UNITS:
                        iq, h, kt = i // QU, i % QU // TT, i % TT
                        if i % QU == 0:
                            if first and i == 0:
                                pe.wait_ge(later_done, 2)
                            pe.wait_ge(m_in, (b * NQUAD + iq + 1) * (16 * NC))
                        if not (first and i < NST):
                            pe.wait_ge(exp_done, b * UNITS + i - NST + 1)
                        keys = ks[:, iq % NQUAD, h, kt * P:(kt + 1) * P]
                        diag, rest = slice(kt * P, (kt + 1) * P), slice((kt + 1) * P, S)
                        nc.tensor.matmul(st[:, i % NST, diag], k["identb"][:], later[:], start=True, stop=False)
                        last = nc.tensor.matmul(st[:, i % NST, diag], keys, qs[:, iq % NQUAD, h, diag],
                                                start=False, stop=True)
                        if kt < TT - 1:
                            last = nc.tensor.matmul(st[:, i % NST, rest], keys, qs[:, iq % NQUAD, h, rest],
                                                    start=True, stop=True)
                        last.then_inc(st_done, 1)
                    pq = lagging(q, 3, first)
                    if jj in PV_AT and pq is not None:
                        kt = PV_AT.index(jj)
                        if kt == 0:
                            pe.wait_ge(exp_done, b * UNITS + (pq + 1) * QU)
                            pe.wait_ge(v_in[pq % NQUAD], (b + pq // NQUAD + 1) * 16)
                            if not (first and pq == 0):
                                pe.wait_ge(oT_done, b * NQUAD + pq)
                        for h in range(QUAD):
                            last = nc.tensor.matmul(acc[32 * h:32 * h + 32, kt * P:S], v[:, pq % NQUAD, h * TT + kt],
                                                    pT[:, pq % 2, h, kt, kt * P:S], start=kt == 0,
                                                    stop=kt == TT - 1, tile_position=(0, 32 * h))
                        if kt == TT - 1:
                            last.then_inc(pv_done, 1)
                    if jj == 15 and pq is not None:
                        pe.wait_ge(oT_done, b * NQUAD + pq + 1)
                        pe.wait_ge(mrow_done, b * NQUAD + min(q, NQUAD))
                        if not (first and pq == 0):
                            pe.wait_ge(o_done, b * NQUAD + pq)
                        for t_ in range(TT):
                            last = nc.tensor.transpose(misc[:, t_ * P:(t_ + 1) * P], oT[:, t_ * P:(t_ + 1) * P],
                                                       k["ident"][:])
                        last.then_inc(oturned, 1)

            block.tensor(steps(pe_steps))

            def dve_steps(dve, b, js, first):
                for j in js:
                    q, jj, t = j // QU, j % QU, j % TT
                    if j < UNITS:
                        h, W = jj // TT, (t + 1) * P
                        if jj == 0 and not first:
                            dve.wait_ge(mparts_done, b * NQUAD + q - NQUAD + 1)
                        wait_apart(dve, k, sc_done, b * UNITS + j + 1)
                        m = t * QUAD + h
                        nc.vector.tensor_tensor_reduce(out=neg[:, j % NSC, 0:W], in0=sc[:, j % NSC, 0:W],
                                                       in1=k["causal"][:, t, 0:W], scale=-1.0, scalar=HUGE,
                                                       op0=ALU.add, op1=ALU.min, accum_out=nmax[:, q, m:m + 1]
                                                       ).then_inc(neg_done, 1)
                    pq = lagging(q, LAST, first)
                    if jj == 1 and pq is not None:
                        dve.wait_ge(oturned, b * NQUAD + pq + 1)
                        dve.wait_ge(o_free, b * NQUAD + pq + 1)
                        ov = misc[:].rearrange("p (n e) -> p n e", e=32)
                        nc.vector.reciprocal(rsum[:].rearrange("p t h -> p (t h)"), ov[:, :, HD]).then_inc(rsum_done, 1)
                        dve.wait_ge(rsum_done, b * NQUAD + pq + 1)
                        by = rsum[:].rearrange("p t (h o) -> p (t h) o", o=1).broadcast_to([P, TT * QUAD, HD])
                        nc.vector.tensor_tensor(o[:, pq % 2].rearrange("p (h t) e -> p t h e", t=TT),
                                                ov[:, :, 0:HD].rearrange("p (t h) e -> p t h e", t=TT),
                                                by.rearrange("p (t h) e -> p t h e", t=TT), ALU.mult).then_inc(o_done, 1)

            block.vector(steps(dve_steps))

            def act_steps(act, b, js, first):
                for j in js:
                    q, jj = j // QU, j % QU
                    mq = lagging(q, 1, first)
                    if jj == 7 and mq is not None:
                        act.wait_ge(mp_done, b * NQUAD + mq + 1)
                        if not (first and mq == 0):
                            act.wait_ge(m_in, (b * NQUAD + mq) * (16 * NC))
                        nc.scalar.copy(mrow[:], misc[0:NC * QUAD]).then_inc(mrow_done, 1)
                    i = j - 2 * QU
                    if not (first and i < 0) and i < UNITS:
                        iq, h, kt = i // QU, i % QU // TT, i % TT
                        if i % QU == 0 and not (first and iq < 2):
                            act.wait_ge(pv_done, b * NQUAD + iq - 1)
                        act.wait_ge(st_done, b * UNITS + i + 1)
                        nc.scalar.activation(pT[:, iq % 2, h, kt, kt * P:S], st[:, i % NST, kt * P:S],
                                             ACT.Exp).then_inc(exp_done, 1)
                    pq = lagging(q, 3, first)
                    if jj == 13 and pq is not None:
                        act.wait_ge(pv_done, b * NQUAD + pq + 1)
                        if not (first and pq == 0):
                            act.wait_ge(oturned, b * NQUAD + pq)
                        nc.scalar.copy(oT[:], acc[:]).then_inc(oT_done, 1)

            block.scalar(steps(act_steps))
        s.end()




def project_cross(nc, w, k, scratch):
    with ExitStack() as c:
        s = Scope(nc, c, "pc")
        U = 4
        UNIT = ((1, 0), (1, 1), (0, 0), (0, 1))
        x, o, cx, xn, x1 = (s.sb(n, [P, TT, D]) for n in ("x", "o", "cx", "xn", "x1"))
        oT, cT, xnT = (s.sb(n, [P, DK, S]) for n in ("oT", "cT", "xnT"))
        vv = s.sb("v", [P, TT, D])
        full, rest = s.sb("full", [P, U, S]), s.sb("rest", [P, U, S])
        parts = s.sb("parts", [P, U, 3, S], BF16)
        stats, mv, sd, rstd = (s.sb("stats", [P, TT, 6]), s.sb("mv", [P, TT, 2]), s.sb("sd", [P, TT]),
                               s.sb("rstd", [P, TT]))
        tp, at, qk = s.ps("tp", [P, DK, S]), s.ps("at", [P, TT, D]), s.ps("qk", [P, 2, S])
        vp = s.ps("vp", [P, TT, D])
        (x_in, o_in, cx_in, x1_out, v_out, xb_done, turned, tp_free, at_done, x1_done, stats_done, mv_done, sd_done,
         rstd_done, xn_done, qk_done, full_done, hi_done, rest_done, mid_done, lo_done, vp_done, v_done) = (
            s.sem(n) for n in (
                "x_in", "o_in", "cx_in", "x1_out", "v_out", "xb_done", "turned", "tp_free", "at_done", "x1_done",
                "stats_done", "mv_done", "sd_done", "rstd_done", "xn_done", "qk_done", "full_done", "hi_done",
                "rest_done", "mid_done", "lo_done", "vp_done", "v_done"))
        parts_out = [s.sem(f"parts_out{u}") for u in range(U)]
        xrows = w["x"].rearrange("b s d -> (b s) d")
        crows = w["ctx"].rearrange("b s d -> (b s) d")

        with nc.Block() as block:
            @block.sync
            def _(sp):
                def load(b, first=False):
                    if not first:
                        wait_apart(sp, k, turned, b * 3 - 2)
                    sp.dma_start(o[:], batch_rows(scratch["o"], b)).then_inc(o_in, 16)
                    if not first:
                        wait_apart(sp, k, x1_done, b * TT)
                    sp.dma_start(x[:], batch_rows(xrows, b)).then_inc(x_in, 16)
                    if not first:
                        wait_apart(sp, k, turned, b * 3 - 1)
                    sp.dma_start(cx[:], batch_rows(crows, b)).then_inc(cx_in, 16)

                load(0, first=True)
                with sp.Fori(1, B) as b:
                    load(b)

            def store_parts(pool, b, u):
                which, g = UNIT[u]
                wait_apart(pool, k, lo_done, b * U + u + 1)
                pool.dma_start(scratch["parts"][bass.ds(b, 1), which, g * P:(g + 1) * P].rearrange("o p c s -> (o p) c s"),
                               parts[:, u]).then_inc(parts_out[u], 16)

            @block.gpsimd
            def _(pool):
                def batch(b):
                    pool.wait_ge(x_in, b * 16 + 16)
                    for t in range(TT):
                        nc.gpsimd.tensor_tensor(x[:, t], x[:, t], k["bout"][:], ALU.add).then_inc(xb_done, 1)
                    wait_apart(pool, k, x1_done, b * TT + TT)
                    pool.dma_start(batch_rows(scratch["x1"], b), x1[:]).then_inc(x1_out, 16)
                    for u in range(2):
                        store_parts(pool, b, u)
                    wait_apart(pool, k, v_done, b * TT + TT)
                    pool.dma_start(batch_rows(scratch["v"], b), vv[:]).then_inc(v_out, 16)
                    for u in range(2, U):
                        store_parts(pool, b, u)

                over_batches(pool, batch)
                pool.wait_ge(x1_out, 16 * B)
                pool.wait_ge(v_out, 16 * B)
                for u in range(U):
                    pool.wait_ge(parts_out[u], 16 * B)

            def each_batch(eng, batch):
                batch(0, True)
                with eng.Fori(1, B - 1) as b:
                    batch(b, True)
                batch(B - 1, False)

            def project_heads(pe, b, u, srcT):
                which, g = UNIT[u]
                pe.wait_ge(full_done, b * U + u // 2 * 2)
                for c_ in range(DK):
                    last = nc.tensor.matmul(qk[:, u % 2], k["xw"][:, which, c_, g * P:(g + 1) * P], srcT[:, c_],
                                            start=c_ == 0, stop=c_ == DK - 1)
                last.then_inc(qk_done, 1)

            @block.tensor
            def _(pe):
                def turn_o(b):
                    pe.wait_ge(o_in, b * 16 + 16)
                    pe.wait_ge(tp_free, b * 3 * DK)
                    turn_batch(nc, pe, k, tp, o, None, 0, turned)

                def batch(b, more):
                    pe.wait_ge(cx_in, b * 16 + 16)
                    pe.wait_ge(tp_free, b * 3 * DK + DK)
                    turn_batch(nc, pe, k, tp, cx, None, 0, turned)
                    pe.wait_ge(x1_done, b * TT)
                    for t in range(TT):
                        for c_ in range(DK):
                            last = nc.tensor.matmul(at[:, t], oT[:, c_, t * P:(t + 1) * P], k["wout"][:, c_],
                                                    start=c_ == 0, stop=c_ == DK - 1)
                        last.then_inc(at_done, 1)
                    pe.wait_ge(tp_free, b * 3 * DK + 2 * DK)
                    for u in (0, 1):
                        project_heads(pe, b, u, cT)
                    pe.wait_ge(v_done, b * TT)
                    for t in range(TT):
                        for c_ in range(DK):
                            last = nc.tensor.matmul(vp[:, t], cT[:, c_, t * P:(t + 1) * P], k["xw"][:, 2, c_],
                                                    start=c_ == 0, stop=c_ == DK - 1)
                        last.then_inc(vp_done, 1)
                    turn_batch(nc, pe, k, tp, xn, xn_done, b * TT, turned)
                    pe.wait_ge(tp_free, b * 3 * DK + 3 * DK)
                    project_heads(pe, b, 2, xnT)
                    if more:
                        turn_o(b + 1)
                    project_heads(pe, b, 3, xnT)

                turn_o(0)
                each_batch(pe, batch)

            @block.scalar
            def _(act):
                def keep_turned(b, n, dst):
                    act.wait_ge(turned, b * 3 + n + 1)
                    for c_ in range(DK):
                        nc.scalar.copy(dst[:, c_], tp[:, c_]).then_inc(tp_free, 1)

                def full_and_hi(b, u):
                    which, g = UNIT[u]
                    act.wait_ge(qk_done, b * U + u + 1)
                    nc.scalar.activation(full[:, u], qk[:, u % 2], ACT.Identity, bias=k["bqk"][:, which, g:g + 1],
                                         scale=1.0 if which else float(HD) ** -0.5).then_inc(full_done, 1)
                    act.wait_ge(full_done, b * U + u + 1)
                    act.wait_ge(parts_out[u], b * 16)
                    nc.scalar.copy(parts[:, u, place(which, 0)], full[:, u]).then_inc(hi_done, 1)

                def mid(b, u):
                    act.wait_ge(rest_done, b * U + u + 1)
                    nc.scalar.copy(parts[:, u, place(UNIT[u][0], 1)], rest[:, u]).then_inc(mid_done, 1)

                def batch(b, more):
                    act.wait_ge(vp_done, b * TT)
                    keep_turned(b, 1, cT)
                    norm_sqrt(nc, act, k, mv, sd, mv_done, sd_done, b)
                    full_and_hi(b, 0)
                    full_and_hi(b, 1)
                    mid(b, 0)
                    act.wait_ge(qk_done, b * U)
                    keep_turned(b, 2, xnT)
                    mid(b, 1)
                    full_and_hi(b, 2)
                    if more:
                        act.wait_ge(at_done, b * TT + TT)
                        keep_turned(b + 1, 0, oT)
                    full_and_hi(b, 3)
                    mid(b, 2)
                    mid(b, 3)

                keep_turned(0, 0, oT)
                each_batch(act, batch)

            @block.vector
            def _(dve):
                def split_rest(b, u):
                    dve.wait_ge(hi_done, b * U + u + 1)
                    nc.vector.tensor_tensor(rest[:, u], full[:, u], parts[:, u, place(UNIT[u][0], 0)],
                                            ALU.subtract).then_inc(rest_done, 1)

                def split_lo(b, u):
                    dve.wait_ge(mid_done, b * U + u + 1)
                    which = UNIT[u][0]
                    nc.vector.tensor_tensor(parts[:, u, place(which, 2)], rest[:, u], parts[:, u, place(which, 1)],
                                            ALU.subtract).then_inc(lo_done, 1)

                def batch(b):
                    for t in range(TT):
                        dve.wait_ge(at_done, b * TT + (t | 1) + 1)
                        dve.wait_ge(xb_done, b * TT + t + 1)
                        dve.wait_ge(x1_out, b * 16)
                        nc.vector.tensor_tensor(x1[:, t], at[:, t], x[:, t], ALU.add).then_inc(x1_done, 1)
                    dve.wait_ge(x1_done, b * TT + TT)
                    norm_stats(nc, dve, k, lambda t: x1[:, t], stats, mv, stats_done, mv_done, b)
                    dve.wait_ge(turned, b * 3)
                    norm_apply(nc, dve, lambda t: x1[:, t], lambda t: xn[:, t], mv, sd, rstd, sd_done, rstd_done,
                               xn_done, b)
                    split_rest(b, 0)
                    split_rest(b, 1)
                    split_lo(b, 0)
                    dve.wait_ge(v_out, b * 16)
                    for t in range(TT):
                        dve.wait_ge(vp_done, b * TT + (t | 1) + 1)
                        nc.vector.tensor_tensor(vv[:, t], vp[:, t], k["bv"][:], ALU.add).then_inc(v_done, 1)
                    split_lo(b, 1)
                    split_rest(b, 2)
                    split_rest(b, 3)
                    split_lo(b, 2)
                    split_lo(b, 3)

                over_batches(dve, batch)
        s.end()


def of_expert(a, e):
    n = len(a.shape)
    x = a[:, bass.ds(e, 1)]
    return x.rearrange({3: "p o f -> p (o f)", 4: "p o n f -> p (o n) f", 5: "p o n c f -> p (o n) c f"}[n])


def route(nc, w, k, scratch):
    with ExitStack() as c:
        s = Scope(nc, c, "rt")
        x, o, x2 = (s.sb(n, [P, TT, D]) for n in ("x", "o", "x2"))
        xn = s.sb("xn", [P, TT, ROW])
        zeros = s.sb("zeros", [P, TT, ROW])
        oT, xnT = (s.sb(n, [P, DK, S]) for n in ("oT", "xnT"))
        stats, mv, sd, rstd = (s.sb("stats", [P, TT, 6]), s.sb("mv", [P, TT, 2]), s.sb("sd", [P, TT]),
                               s.sb("rstd", [P, TT]))
        top, expg, shift, score, biased, above, s2_, s4_, pick, sel = (
            s.sb(n, [P, TT, NE]) for n in ("top", "expg", "shift", "score", "biased", "above", "s2", "s4", "pick",
                                           "sel"))
        c0, c1, c2 = (s.sb(n, [P, TT, 2 * NE]) for n in ("c0", "c1", "c2"))
        gmax, gsum, ginv, nabove = (s.sb(n, [P, TT]) for n in ("gmax", "gsum", "ginv", "nabove"))
        FO = 2 * FF // P
        raw13 = s.sb("raw13", [P, 2, FO, D])
        raw2 = s.sb("raw2", [P, DK, FF])
        tp, at, gp = s.ps("tp", [P, DK, S]), s.ps("at", [P, TT, D]), s.ps("gp", [P, S])
        NXP = 3
        xp = s.ps("xp", [P, NXP, S])
        G = 2 * DK + MF
        (x_in, o_in, x2_out, xn_out, zeros_out, ones_done, xb_done, o_turned, xn_turned, oT_done, xnT_done, at_done,
         x2_done, stats_done, mv_done, sd_done, rstd_done, xn_done, gate_done, exp_done, g_step, cw_done, zeroed,
         raw_in, small_in, w_turned, w_kept) = (
            s.sem(n) for n in (
                "x_in", "o_in", "x2_out", "xn_out", "zeros_out", "ones_done", "xb_done", "o_turned", "xn_turned",
                "oT_done", "xnT_done", "at_done", "x2_done", "stats_done", "mv_done", "sd_done", "rstd_done",
                "xn_done", "gate_done", "exp_done", "g_step", "cw_done", "zeroed", "raw_in", "small_in",
                "w_turned", "w_kept"))
        GATE_STEPS = 16
        xs = scratch["xs"]

        def each_step(eng, step):
            step(0, True)
            with eng.Fori(1, B - 1) as b:
                step(b, True)
            step(B - 1, False)

        with nc.Block() as block:
            def load_weights(sp, e):
                def src(name):
                    if isinstance(e, int) and e == NE:
                        return w["s" + name].rearrange("(o a) -> o a", o=1) if len(w["s" + name].shape) == 1 else (
                            w["s" + name].rearrange("(o a) d -> o a d", o=1))
                    return w[name][bass.ds(e, 1)]

                for n, name in enumerate(("w1", "w3")):
                    sp.dma_start(raw13[:, n], src(name).rearrange("o (c p) d -> p (o c) d", p=P)).then_inc(raw_in, 16)
                sp.dma_start(raw2[:], src("w2").rearrange("o (c p) f -> p (o c) f", p=P)).then_inc(raw_in, 16)
                for dst, name in ((of_expert(k["b13"], e)[:, 0], "b1"), (of_expert(k["b13"], e)[:, 1], "b3"),
                                  (of_expert(k["b2"], e), "b2")):
                    sp.dma_start(dst, src(name).broadcast_to([P, dst.shape[1]])).then_inc(small_in, 16)

            @block.sync
            def _(sp):
                sp.dma_start(o[:], batch_rows(scratch["o"], 0)).then_inc(o_in, 16)
                sp.dma_start(x[:], batch_rows(scratch["x1"], 0)).then_inc(x_in, 16)
                load_weights(sp, NE)
                sp.wait_ge(ones_done, 2)
                for i in range(ROUTED // TT):
                    sp.dma_start(batch_rows(xs[B * S:NTILES * P], i, ROUTED // TT), zeros[:]).then_inc(zeros_out, 16)

                def step(b, more):
                    if more:
                        wait_apart(sp, k, o_turned, b + 1)
                        sp.dma_start(o[:], batch_rows(scratch["o"], b + 1)).then_inc(o_in, 16)
                        wait_apart(sp, k, x2_done, b * TT + TT)
                        sp.dma_start(x[:], batch_rows(scratch["x1"], b + 1)).then_inc(x_in, 16)
                    wait_apart(sp, k, w_turned, b * G + G)
                    load_weights(sp, b)

                each_step(sp, step)
                sp.wait_ge(zeros_out, 16 * (ROUTED // TT))
                sp.wait_ge(small_in, 16 * 3 * NX)

            @block.gpsimd
            def _(pool):
                nc.gpsimd.memset(zeros[:], 0.0).then_inc(ones_done, 1)
                nc.gpsimd.memset(xn[:], 1.0).then_inc(ones_done, 1)

                def add_bias(b):
                    pool.wait_ge(x_in, b * 16 + 16)
                    for t in range(TT):
                        nc.gpsimd.tensor_tensor(x[:, t], x[:, t], k["bo"][:], ALU.add).then_inc(xb_done, 1)

                def store_x2(b):
                    wait_apart(pool, k, x2_done, b * TT + TT)
                    pool.dma_start(batch_rows(scratch["x2"], b), x2[:]).then_inc(x2_out, 16)

                def step(b, more):
                    if more:
                        add_bias(b + 1)
                    wait_apart(pool, k, xn_done, b * TT + TT)
                    pool.dma_start(batch_rows(xs[0:B * S], b), xn[:]).then_inc(xn_out, 16)
                    if more:
                        store_x2(b + 1)

                add_bias(0)
                store_x2(0)
                each_step(pool, step)
                for q in (x2_out, xn_out):
                    pool.wait_ge(q, 16 * B)

            @block.tensor
            def _(pe):
                def sum_rows(b, first=False):
                    pe.wait_ge(o_in, b * 16 + 16)
                    if not first:
                        pe.wait_ge(oT_done, b * DK)
                        pe.wait_ge(x2_done, b * TT)
                    turn_batch(nc, pe, k, tp, o, None, 0, o_turned)
                    pe.wait_ge(oT_done, b * DK + DK)
                    for t in range(TT):
                        for c_ in range(DK):
                            last = nc.tensor.matmul(at[:, t], oT[:, c_, t * P:(t + 1) * P], k["xw"][:, 3, c_],
                                                    start=c_ == 0, stop=c_ == DK - 1)
                        last.then_inc(at_done, 1)

                def turn_expert(m, groups):
                    pe.wait_ge(raw_in, m * 48 + 48)
                    for g in groups:
                        if not (isinstance(m, int) and m == 0 and g < NXP):
                            pe.wait_ge(w_kept, m * G + g - NXP + 1)
                        if g < 2 * DK:
                            blocks = [raw13[:, g // DK, i, (g % DK) * P:(g % DK + 1) * P] for i in range(FO)]
                        else:
                            blocks = [raw2[:, i, (g - 2 * DK) * P:(g - 2 * DK + 1) * P] for i in range(DK)]
                        for i, a in enumerate(blocks):
                            last = nc.tensor.transpose(xp[:, g % NXP, i * P:(i + 1) * P], a, k["ident"][:])
                        last.then_inc(w_turned, 1)

                def step(b, more):
                    if not (isinstance(b, int) and b == 0):
                        pe.wait_ge(xnT_done, b * DK)
                    if more:
                        sum_rows(b + 1)
                    for t in range(TT):
                        pe.wait_ge(xn_done, b * TT + t + 1)
                        if t == 0:
                            pe.wait_ge(oT_done, (b + 2) * DK if more else B * DK)
                        for c_ in range(DK):
                            last = nc.tensor.transpose(tp[:, c_, t * P:(t + 1) * P], xn[:, t, c_ * P:(c_ + 1) * P],
                                                       k["ident"][:])
                    last.then_inc(xn_turned, 1)
                    turn_expert(b + 1, range(NXP))
                    pe.wait_ge(xnT_done, b * DK + DK)
                    if not (isinstance(b, int) and b == 0):
                        pe.wait_ge(g_step, b * GATE_STEPS)
                    for t in range(TT):
                        for c_ in range(DK):
                            last = nc.tensor.matmul(gp[:, t * NE:(t + 1) * NE], xnT[:, c_, t * P:(t + 1) * P],
                                                    k["gateT"][:, c_], start=c_ == 0, stop=c_ == DK - 1)
                    last.then_inc(gate_done, 1)
                    turn_expert(b + 1, range(NXP, G))

                sum_rows(0, first=True)
                turn_expert(0, range(G))
                each_step(pe, step)

            def keep_weights(act, m, e, groups):
                for g in groups:
                    act.wait_ge(w_turned, m * G + g + 1)
                    if g < 2 * DK:
                        nc.scalar.copy(of_expert(k["w13"], e)[:, g // DK, g % DK], xp[:, g % NXP]).then_inc(w_kept, 1)
                    else:
                        nc.scalar.copy(of_expert(k["w2"], e)[:, g - 2 * DK], xp[:, g % NXP, 0:D]).then_inc(w_kept, 1)

            @block.scalar
            def _(act):
                def keep_o(b, first=False):
                    act.wait_ge(o_turned, b + 1)
                    if not first:
                        act.wait_ge(at_done, b * TT)
                    for c_ in range(DK):
                        nc.scalar.copy(oT[:, c_], tp[:, c_]).then_inc(oT_done, 1)

                def step(b, more):
                    if more:
                        keep_o(b + 1)
                    norm_sqrt(nc, act, k, mv, sd, mv_done, sd_done, b)
                    act.wait_ge(xn_turned, b + 1)
                    if not (isinstance(b, int) and b == 0):
                        act.wait_ge(gate_done, b)
                    for c_ in range(DK):
                        nc.scalar.copy(xnT[:, c_], tp[:, c_]).then_inc(xnT_done, 1)
                    keep_weights(act, b + 1, b, range(NXP))
                    act.wait_ge(g_step, b * GATE_STEPS + 2)
                    nc.scalar.activation(expg[:], shift[:], ACT.Exp).then_inc(exp_done, 1)
                    keep_weights(act, b + 1, b, range(NXP, G))

                keep_o(0, first=True)
                keep_weights(act, 0, NE, range(G))
                each_step(act, step)

            @block.vector
            def _(dve):
                dve.wait_ge(ones_done, 2)
                for z in (c0, c1, c2):
                    nc.vector.memset(z[:], 0.0).then_inc(zeroed, 1)
                dve.wait_ge(zeroed, 3)

                def sum_rows(b, first=False):
                    for t in range(TT):
                        dve.wait_ge(at_done, b * TT + (t | 1) + 1)
                        dve.wait_ge(xb_done, b * TT + t + 1)
                        if not first and t == 0:
                            dve.wait_ge(x2_out, b * 16)
                            dve.wait_ge(xn_done, b * TT)
                        nc.vector.tensor_tensor(x2[:, t], at[:, t], x[:, t], ALU.add).then_inc(x2_done, 1)

                def norm(b):
                    dve.wait_ge(x2_done, b * TT + TT)
                    norm_stats(nc, dve, k, lambda t: x2[:, t], stats, mv, stats_done, mv_done, b)
                    if not (isinstance(b, int) and b == 0):
                        dve.wait_ge(xn_out, b * 16)
                        dve.wait_ge(xn_turned, b)
                    norm_apply(nc, dve, lambda t: x2[:, t], lambda t: xn[:, t, 0:D], mv, sd, rstd, sd_done, rstd_done,
                               xn_done, b)

                def gate(b):
                    steps = [0]

                    def then(ins):
                        steps[0] += 1
                        ins.then_inc(g_step, 1)
                        wait_apart(dve, k, g_step, b * GATE_STEPS + steps[0])

                    def wide(a):
                        return a.rearrange("p (t o) -> p t o", o=1).broadcast_to([P, TT, NE])

                    dve.wait_ge(gate_done, b + 1)
                    logits = gp[:, 0:TT * NE].rearrange("p (t e) -> p t e", e=NE)
                    then(nc.vector.tensor_reduce(gmax[:], logits, AX_X, ALU.max))
                    then(nc.vector.tensor_tensor(shift[:], logits, wide(gmax[:]), ALU.subtract))
                    dve.wait_ge(exp_done, b + 1)
                    then(nc.vector.tensor_reduce(gsum[:], expg[:], AX_X, ALU.add))
                    then(nc.vector.reciprocal(ginv[:], gsum[:]))
                    then(nc.vector.tensor_tensor(score[:], expg[:], wide(ginv[:]), ALU.mult))
                    then(nc.vector.tensor_tensor(biased[:], score[:], k["gateb"][:].rearrange(
                        "p (o e) -> p o e", o=1).broadcast_to([P, TT, NE]), ALU.add))
                    for t in range(TT):
                        last = nc.vector.max(top[:, t], biased[:, t])
                    then(last)
                    second = top[:, :, 1:2].broadcast_to([P, TT, NE])
                    then(nc.vector.tensor_tensor(above[:], biased[:], second, ALU.is_gt))
                    then(nc.vector.tensor_tensor(c0[:, :, NE:], biased[:], second, ALU.is_equal))
                    then(nc.vector.tensor_reduce(nabove[:], above[:], AX_X, ALU.add))
                    then(nc.vector.tensor_tensor(c1[:, :, NE:], c0[:, :, NE:], c0[:, :, NE - 1:2 * NE - 1], ALU.add))
                    then(nc.vector.tensor_tensor(c2[:, :, NE:], c1[:, :, NE:], c1[:, :, NE - 2:2 * NE - 2], ALU.add))
                    then(nc.vector.tensor_tensor(s4_[:], c2[:, :, NE:], c2[:, :, NE - 4:2 * NE - 4], ALU.add))
                    then(nc.vector.tensor_tensor(s2_[:], s4_[:], wide(nabove[:]), ALU.add))
                    then(nc.vector.scalar_tensor_tensor(pick[:], s2_[:], 2.0, c0[:, :, NE:], ALU.is_le, ALU.mult))
                    mine = bass.ds(b * TT, TT)
                    then(nc.vector.tensor_tensor(sel[:], above[:], pick[:], ALU.add))
                    nc.vector.tensor_copy(k["sel"][:, mine], sel[:])
                    nc.vector.tensor_tensor(k["cw"][:, mine], sel[:], score[:], ALU.mult).then_inc(cw_done, 1)
                    assert steps[0] == GATE_STEPS

                def step(b, more):
                    norm(b)
                    if more:
                        sum_rows(b + 1)
                    gate(b)

                sum_rows(0, first=True)
                each_step(dve, step)
        s.end()


def experts_of(nc, engine, k, j):
    return nc.values_load_multi_w_load_instructions(
        k["eidx"][0:1, bass.ds(j * 4, 8)], engines=[engine], min_val=0, max_val=NE,
        skip_runtime_bounds_check_because="assign clamps each to 0..NE")[1]


def assign(nc, k):
    with ExitStack() as c:
        s = Scope(nc, c, "as")
        TB = B * TT
        tri, ones = s.sb("tri", [P, P]), s.sb("ones", [P, P])
        iota_i = s.sb("iota_i", [P, ROUTED], I32)
        iota, starts = s.sb("iota", [P, ROUTED]), s.sb("starts", [P, TB])
        ca, cb = s.sb("ca", [P, NE, 2 * TB]), s.sb("cb", [P, NE, 2 * TB])
        more, ntiles = s.sb("more", [P, NE, TB]), s.sb("ntiles", [P, NE])
        na, nb = s.sb("na", [P, 2 * NE]), s.sb("nb", [P, 2 * NE])
        base, slot, slotm, hit, hitw = (s.sb(n, [P, TB, NE]) for n in ("base", "slot", "slotm", "hit", "hitw"))
        two, total = s.sb("two", [P, 2, TB]), s.sb("total", [P, TB])
        ended, ef = s.sb("ended", [P, ROUTED, NE]), s.sb("ef", [P, NTILES + 8])
        pre, tot = s.ps("pre", [P, S]), s.ps("tot", [P, S])
        made, tri_done, counted, step = (s.sem(n) for n in ("made", "tri_done", "counted", "step"))
        with nc.Block() as block:
            @block.gpsimd
            def _(pool):
                nc.gpsimd.memset(tri[:], 1.0).then_inc(made, 1)
                pool.wait_ge(made, 1)
                nc.gpsimd.affine_select(out=tri[:], in_=tri[:], compare_op=ALU.is_gt, fill=0.0, base=0,
                                        pattern=[[1, P]], channel_multiplier=-1).then_inc(tri_done, 1)
                nc.gpsimd.memset(ones[:], 1.0).then_inc(tri_done, 1)
                nc.gpsimd.iota(iota_i[:], pattern=[[1, ROUTED]], base=0, channel_multiplier=0).then_inc(tri_done, 1)

            @block.tensor
            def _(pe):
                pe.wait_ge(tri_done, 2)
                sel = k["sel"][:].rearrange("p t e -> p (t e)")
                nc.tensor.matmul(pre[:, 0:TB * NE], tri[:], sel, start=True, stop=True)
                nc.tensor.matmul(tot[:, 0:TB * NE], ones[:], sel, start=True, stop=True).then_inc(counted, 1)

            @block.vector
            def _(dve):
                n = [0]

                def then(ins):
                    n[0] += 1
                    ins.then_inc(step, 1)
                    dve.wait_ge(step, n[0])

                def over_t(a):
                    return a.rearrange("p (o e) -> p o e", o=1).broadcast_to([P, TB, NE])

                for z in (ca, cb, na, nb):
                    then(nc.vector.memset(z[:], 0.0))
                dve.wait_ge(tri_done, 3)
                then(nc.vector.tensor_copy(iota[:], iota_i[:]))
                then(nc.vector.tensor_scalar(starts[:], iota[:, 0:TB], float(P), None, ALU.mult))
                dve.wait_ge(counted, 1)
                then(nc.vector.tensor_copy(ca[:, :, TB:], tot[:, 0:TB * NE].rearrange("p (t e) -> p e t", e=NE)))
                a, b_, d = ca, cb, 1
                while d < TB:
                    then(nc.vector.tensor_tensor(b_[:, :, TB:], a[:, :, TB:], a[:, :, TB - d:2 * TB - d], ALU.add))
                    a, b_, d = b_, a, 2 * d
                count = a[:, :, 2 * TB - 1:2 * TB].broadcast_to([P, NE, TB])
                then(nc.vector.tensor_tensor(more[:], count, starts[:].rearrange("p (o t) -> p o t", o=1).broadcast_to(
                    [P, NE, TB]), ALU.is_gt))
                then(nc.vector.tensor_reduce(ntiles[:], more[:], AX_X, ALU.add))
                then(nc.vector.tensor_copy(na[:, NE:], ntiles[:]))
                f, g_, d = na, nb, 1
                while d < NE:
                    then(nc.vector.tensor_tensor(g_[:, NE:], f[:, NE:], f[:, NE - d:2 * NE - d], ALU.add))
                    f, g_, d = g_, f, 2 * d
                before = a[:, :, TB - 1:2 * TB - 1].rearrange("p e t -> p t e")
                then(nc.vector.scalar_tensor_tensor(base[:], over_t(f[:, NE - 1:2 * NE - 1]), float(P), before,
                                                    ALU.mult, ALU.add))
                then(nc.vector.tensor_tensor(slot[:], pre[:, 0:TB * NE].rearrange("p (t e) -> p t e", e=NE), base[:], ALU.add))
                then(nc.vector.scalar_tensor_tensor(slotm[:], slot[:], float(B * S), k["sel"][:], ALU.add, ALU.mult))
                then(nc.vector.tensor_reduce(two[:, 1], slotm[:], AX_X, ALU.max))
                then(nc.vector.tensor_reduce(total[:], slotm[:], AX_X, ALU.add))
                then(nc.vector.tensor_tensor(two[:, 0], total[:], two[:, 1], ALU.subtract))
                then(nc.vector.tensor_copy(k["slots"][:], two[:]))
                for i in range(2):
                    then(nc.vector.tensor_tensor(hit[:], slotm[:], two[:, i].rearrange("p (t o) -> p t o", o=1).broadcast_to(
                        [P, TB, NE]), ALU.is_equal))
                    then(nc.vector.tensor_tensor(hitw[:], hit[:], k["cw"][:], ALU.mult))
                    then(nc.vector.tensor_reduce(k["cw2"][:, i], hitw[:], AX_X, ALU.add))
                then(nc.vector.tensor_tensor(ended[:], iota[:].rearrange("p (i o) -> p i o", o=1).broadcast_to([P, ROUTED, NE]),
                                             f[:, NE:].rearrange("p (o e) -> p o e", o=1).broadcast_to([P, ROUTED, NE]),
                                             ALU.is_ge))
                then(nc.vector.memset(ef[:], float(NE)))
                mine = slice(4 + TB, 4 + NTILES)
                then(nc.vector.tensor_reduce(ef[:, mine], ended[:], AX_X, ALU.add))
                then(nc.vector.tensor_scalar(ef[:, mine], ef[:, mine], float(NE - 1), None, ALU.min))
                then(nc.vector.tensor_copy(k["eidx"][:], ef[:]))
        s.end()


def experts(nc, k, scratch):
    ALPHA, LIMIT = 1.702, 7.0
    R = 4
    UP, GATE, DOWN, STORE = 1, 2, 4, 9
    with ExitStack() as c:
        s = Scope(nc, c, "ex")
        xg = s.sb("xg", [P, R, ROW])
        xgT = s.sb("xgT", [P, R, DK, P])
        t1, t3, hh = s.sb("t1", [P, 2 * FF]), s.sb("t3", [P, 2 * FF]), s.sb("hh", [P, 2 * FF])
        g, sg, l = (s.sb(n, [P, 2, FF]) for n in ("g", "sg", "l"))
        gs = s.sb("gs", [P, FF])
        a = s.sb("a", [P, R, FF])
        cwc = s.sb("cwc", [P, R])
        aT = s.sb("aT", [P, R, MF, P])
        ysb = s.sb("ysb", [P, R, D])
        xr = s.sb("xr", [P, 2, TT, ROW])
        idx = s.sb("idx", [P, 2, TT], U32)
        xtp, hp, atp, yp = s.ps("xtp", [P, S]), s.ps("hp", [P, 2, 2, S]), s.ps("atp", [P, S]), s.ps("yp", [P, 2, S])
        x_in, y_out = ([s.sem(f"{n}{i}") for i in range(R)] for n in ("x_in", "y_out"))
        (xturned, xgT_done, cwc_done, h_done, t_done, hh_done, g_done, sg_done, gs_done, l_done, a_done, aturned,
         aT_done, y_done, ysb_done, xr_in, filled, scattered) = (s.sem(n) for n in (
            "xturned", "xgT_done", "cwc_done", "h_done", "t_done", "hh_done", "g_done", "sg_done", "gs_done",
            "l_done", "a_done", "aturned", "aT_done", "y_done", "ysb_done", "xr_in", "filled", "scattered"))
        xs, ys = scratch["xs"], scratch["ys"]
        xs_t = xs.rearrange("(i q p) f -> i q p f", q=R, p=P)
        ys_t = ys.rearrange("(i q p) f -> i q p f", q=R, p=P)
        GROUPS = NTILES // R
        SHARED = B * TT // R

        def back(j, q, n):
            jj, qq = j + (q - n) // R, (q - n) % R
            if isinstance(j, int) and not 0 <= jj < GROUPS:
                return None
            return jj, qq, jj * R + qq

        def groups(eng, step, engine):
            def group(j):
                es = experts_of(nc, engine, k, j) if engine is not None else None
                for q in range(R):
                    step(j, q, es)

            group(0)
            group(1)
            with eng.Fori(2, GROUPS) as j:
                group(j)
            group(GROUPS)

        def wait_if(eng, sem, value):
            if not isinstance(value, int) or value > 0:
                eng.wait_ge(sem, value)

        with nc.Block() as block:
            def load(sp, j, q):
                wait_if(sp, xturned, R * (j - 1) + q + 1)
                wait_if(sp, cwc_done, R * (j - 1) + q + 1)
                sp.dma_start(xg[:, q], xs_t[bass.ds(j, 1), q].rearrange("o p f -> (o p) f")).then_inc(x_in[q], 16)

            @block.sync
            def _(sp):
                def group(j):
                    for q in range(R):
                        store = back(j, q, STORE)
                        if store:
                            jj, qq, i = store
                            sp.wait_ge(ysb_done, i + 1)
                            sp.dma_start(ys_t[bass.ds(jj, 1), qq].rearrange("o p f -> (o p) f"), ysb[:, qq]
                                         ).then_inc(y_out[qq], 16)
                        if not isinstance(j, int) or j < GROUPS:
                            load(sp, j, q)

                for j in range(3):
                    group(j)
                with sp.Fori(3, SHARED) as j:
                    group(j)
                sp.wait_ge(scattered, 16 * 2 * TT * B)
                with sp.Fori(SHARED, GROUPS) as j:
                    group(j)
                for j in range(GROUPS, GROUPS + 3):
                    group(j)
                for q in range(R):
                    sp.wait_ge(y_out[q], 16 * GROUPS)

            @block.gpsimd
            def _(pool):
                def batch(b):
                    wait_if(pool, scattered, b * (16 * 2 * TT))
                    for n in range(2):
                        pool.dma_start(xr[:, n], batch_rows(xs[0:B * S], b)).then_inc(xr_in, 16)
                    pool.wait_ge(xr_in, b * 32 + 32)
                    for n in range(2):
                        nc.gpsimd.tensor_copy(xr[:, n, :, D:D + 1], k["cw2"][:, n, bass.ds(b * TT, TT)].rearrange(
                            "p (t o) -> p t o", o=1)).then_inc(filled, 1)
                        nc.gpsimd.tensor_copy(idx[:, n], k["slots"][:, n, bass.ds(b * TT, TT)]).then_inc(filled, 1)
                    wait_apart(pool, k, filled, b * 4 + 4)
                    for n in range(2):
                        for t in range(TT):
                            pool.indirect_dma_start(xs, bass.IndirectOffsetOnAxis(ap=idx[:, n, t:t + 1], axis=0),
                                                    xr[:, n, t], None).then_inc(scattered, 16)

                over_batches(pool, batch)

            @block.tensor
            def _(pe):
                def step(j, q, es):
                    here, up, down = back(j, q, 0), back(j, q, UP), back(j, q, DOWN)
                    if here:
                        jj, qq, i = here
                        pe.wait_ge(x_in[qq], 16 * jj + 16)
                        wait_if(pe, xgT_done, i)
                        for c_ in range(DK):
                            last = nc.tensor.transpose(xtp[:, c_ * P:(c_ + 1) * P], xg[:, qq, c_ * P:(c_ + 1) * P],
                                                       k["ident"][:])
                        last.then_inc(xturned, 1)
                    if down:
                        jj, qq, i = down
                        pe.wait_ge(a_done, i + 1)
                        wait_if(pe, aT_done, i)
                        for m in range(MF):
                            last = nc.tensor.transpose(atp[:, m * P:(m + 1) * P], a[:, qq, m * P:(m + 1) * P],
                                                       k["ident"][:])
                        last.then_inc(aturned, 1)
                    if up:
                        jj, qq, i = up
                        e = es[q - UP + DOWN]
                        pe.wait_ge(xgT_done, i + 1)
                        wait_if(pe, t_done, 2 * i - 2)
                        for n in range(2):
                            for c_ in range(DK):
                                last = nc.tensor.matmul(hp[:, qq % 2, n], xgT[:, qq, c_], of_expert(k["w13"], e)[:, n, c_],
                                                        start=c_ == 0, stop=c_ == DK - 1)
                        last.then_inc(h_done, 1)
                    if down:
                        jj, qq, i = down
                        e = es[q]
                        pe.wait_ge(aT_done, i + 1)
                        wait_if(pe, ysb_done, i - 1)
                        for m in range(MF):
                            last = nc.tensor.matmul(yp[:, qq % 2, 0:D], aT[:, qq, m], of_expert(k["w2"], e)[:, m],
                                                    start=m == 0, stop=m == MF - 1)
                        last.then_inc(y_done, 1)

                groups(pe, step, mybir.EngineType.PE)

            @block.scalar
            def _(act):
                def step(j, q, es):
                    here, gate, down = (back(j, q, n) for n in (0, GATE, DOWN))
                    if here:
                        jj, qq, i = here
                        act.wait_ge(xturned, i + 1)
                        wait_if(act, h_done, i - R + 1)
                        nc.scalar.copy(xgT[:, qq].rearrange("p c s -> p (c s)"), xtp[:, 0:D]).then_inc(xgT_done, 1)
                    if down:
                        jj, qq, i = down
                        act.wait_ge(aturned, i + 1)
                        wait_if(act, y_done, i - R + 1)
                        nc.scalar.copy(aT[:, qq].rearrange("p c s -> p (c s)"), atp[:, 0:FF]).then_inc(aT_done, 1)
                    if gate:
                        jj, qq, i = gate
                        act.wait_ge(g_done, i + 1)
                        wait_if(act, gs_done, i - 1)
                        nc.scalar.activation(sg[:, qq % 2], g[:, qq % 2], ACT.Sigmoid, scale=ALPHA).then_inc(sg_done, 1)

                groups(act, step, None)

            @block.vector
            def _(dve):
                def step(j, q, es):
                    up, gate, down = back(j, q, UP), back(j, q, GATE), back(j, q, DOWN)
                    if gate:
                        jj, qq, i = gate
                        dve.wait_ge(cwc_done, i + 1)
                        dve.wait_ge(sg_done, i + 1)
                        nc.vector.scalar_tensor_tensor(gs[:], g[:, qq % 2], cwc[:, qq:qq + 1], sg[:, qq % 2], ALU.mult,
                                                       ALU.mult).then_inc(gs_done, 1)
                        dve.wait_ge(l_done, i + 1)
                        dve.wait_ge(gs_done, i + 1)
                        wait_if(dve, aturned, i - R + 1)
                        nc.vector.scalar_tensor_tensor(a[:, qq], l[:, qq % 2], 1.0, gs[:], ALU.add, ALU.mult).then_inc(a_done, 1)
                    if up:
                        jj, qq, i = up
                        e = es[q - UP + DOWN]
                        dve.wait_ge(x_in[qq], 16 * jj + 16)
                        nc.vector.tensor_copy(cwc[:, qq:qq + 1], xg[:, qq, D:D + 1]).then_inc(cwc_done, 1)
                        dve.wait_ge(h_done, i + 1)
                        for n, h in enumerate((t1, t3)):
                            nc.vector.tensor_tensor(h[:], hp[:, qq % 2, n], of_expert(k["b13"], e)[:, n],
                                                    ALU.add).then_inc(t_done, 1)
                        dve.wait_ge(t_done, 2 * i + 2)
                        nc.vector.tensor_tensor(hh[:], t1[:], t3[:], ALU.mult).then_inc(hh_done, 1)
                        dve.wait_ge(hh_done, i + 1)
                        pair = hh[:].rearrange("p (f two) -> p two f", two=2)
                        nc.vector.tensor_scalar(g[:, qq % 2], pair[:, 0], LIMIT, None, ALU.min).then_inc(g_done, 1)
                        nc.vector.tensor_scalar(l[:, qq % 2], pair[:, 1], LIMIT, -LIMIT, ALU.min, ALU.max).then_inc(l_done, 1)
                    if down:
                        jj, qq, i = down
                        e = es[q]
                        wait_if(dve, y_out[qq], 16 * jj)
                        dve.wait_ge(y_done, i + 1)
                        nc.vector.scalar_tensor_tensor(ysb[:, qq], of_expert(k["b2"], e), cwc[:, qq:qq + 1],
                                                       yp[:, qq % 2, 0:D], ALU.mult, ALU.add).then_inc(ysb_done, 1)

                groups(dve, step, mybir.EngineType.DVE)
        s.end()


def combine(nc, k, scratch, out):
    with ExitStack() as c:
        s = Scope(nc, c, "cb")
        x2, sh, ab = s.sb("x2", [P, 2, TT, D]), s.sb("sh", [P, 2, TT, D]), s.sb("ab", [P, 2, 2, TT, D])
        res = s.sb("res", [P, 2, TT, D])
        idx = s.sb("idx", [P, 2, 2, TT], U32)
        x_in, ab_in, r_out = ([s.sem(f"{n}{i}") for i in range(2)] for n in ("x_in", "ab_in", "r_out"))
        filled, added, step1, step2 = (s.sem(n) for n in ("filled", "added", "step1", "step2"))
        ys = scratch["ys"]
        orow = out.rearrange("b s d -> (b s) d")

        def pairs(eng, body):
            for h in range(2):
                body(0, h, h)
            with eng.Fori(1, B // 2) as j:
                for h in range(2):
                    body(j, h, j * 2 + h)

        def wait_if(eng, sem, value):
            if not isinstance(value, int) or value > 0:
                eng.wait_ge(sem, value)

        with nc.Block() as block:
            @block.sync
            def _(sp):
                def body(j, h, b):
                    wait_if(sp, added, 2 * j + h - 1)
                    sp.dma_start(x2[:, h], batch_rows(scratch["x2"], b)).then_inc(x_in[h], 16)
                    sp.dma_start(sh[:, h], batch_rows(ys[0:B * S], b)).then_inc(x_in[h], 16)

                pairs(sp, body)

            @block.gpsimd
            def _(pool):
                def body(j, h, b):
                    wait_if(pool, ab_in[h], j * (16 * 2 * TT))
                    nc.gpsimd.tensor_copy(idx[:, h], k["slots"][:, :, bass.ds(b * TT, TT)]).then_inc(filled, 1)
                    wait_if(pool, added, 2 * j + h - 1)
                    wait_apart(pool, k, filled, 2 * j + h + 1)
                    for n in range(2):
                        for t in range(TT):
                            pool.indirect_dma_start(ab[:, h, n, t], None, ys,
                                                    bass.IndirectOffsetOnAxis(ap=idx[:, h, n, t:t + 1], axis=0)
                                                    ).then_inc(ab_in[h], 16)

                pairs(pool, body)

            @block.vector
            def _(dve):
                def body(j, h, b):
                    n = 2 * j + h
                    flat = "p t d -> p (t d)"
                    dve.wait_ge(x_in[h], 32 * j + 32)
                    wait_if(dve, r_out[h], 16 * j)
                    nc.vector.tensor_tensor(res[:, h].rearrange(flat), x2[:, h].rearrange(flat), sh[:, h].rearrange(flat),
                                            ALU.add).then_inc(step1, 1)
                    dve.wait_ge(ab_in[h], j * (16 * 2 * TT) + 16 * 2 * TT)
                    dve.wait_ge(step1, n * 2 + 1)
                    nc.vector.tensor_tensor(res[:, h].rearrange(flat), res[:, h].rearrange(flat),
                                            ab[:, h, 0].rearrange(flat), ALU.add).then_inc(step1, 1)
                    dve.wait_ge(step1, n * 2 + 2)
                    nc.vector.tensor_tensor(res[:, h].rearrange(flat), res[:, h].rearrange(flat),
                                            ab[:, h, 1].rearrange(flat), ALU.add).then_inc(added, 1)

                pairs(dve, body)

            @block.scalar
            def _(act):
                def body(j, h, b):
                    act.wait_ge(added, 2 * j + h + 1)
                    act.dma_start(batch_rows(orow, b), res[:, h]).then_inc(r_out[h], 16)

                pairs(act, body)
                for h in range(2):
                    act.wait_ge(r_out[h], 16 * B // 2)
        s.end()


def decoder_layer(nc, w, out):
    def dram(name, shape, dt=F32):
        return nc.dram_tensor(name, shape, dt).ap()

    scratch = {
        "qkv": dram("scratch_qkv", [B * HEADS * S, 3 * HD]),
        "parts": dram("scratch_parts", [B, 2, D, NPART, S], BF16),
        "o": dram("scratch_o", [B * S, D]),
        "x1": dram("scratch_x1", [B * S, D]),
        "v": dram("scratch_v", [B * S, D]),
        "x2": dram("scratch_x2", [B * S, D]),
        "xs": dram("scratch_xs", [NTILES * P, ROW]),
        "ys": dram("scratch_ys", [NTILES * P, D]),
    }
    k = {}
    with ExitStack() as ctx:
        with ExitStack() as early:
            with ExitStack() as first:
                prepare_weights(nc, ctx, early, first, w, k)
                project_self(nc, w, k, scratch)
                attention_causal(nc, w, k, scratch)
            project_cross(nc, w, k, scratch)
            attention_cross(nc, w, k, scratch)
            keep = Scope(nc, early, "xk")
            k["w13"] = keep.sb("w13", [P, NX, 2, DK, 2 * FF])
            k["w2"] = keep.sb("w2", [P, NX, MF, D])
            k["b13"] = keep.sb("b13", [P, NX, 2, 2 * FF])
            k["b2"] = keep.sb("b2", [P, NX, D])
            route(nc, w, k, scratch)
            assign(nc, k)
            experts(nc, k, scratch)
        combine(nc, k, scratch, out)


_INS = {
    "x": "x", "ctx_1024": "ctx", "mask_Bx1xSxS2_ik1": "mask",
    "L0_attn_W_qkv": "W_qkv", "L0_attn_b_qkv": "b_qkv", "L0_attn_W_out": "W_out", "L0_attn_b_out": "b_out",
    "L0_xattn_adj": "adj", "L0_xattn_Wq": "Wq", "L0_xattn_bq": "bq", "L0_xattn_Wk": "Wk", "L0_xattn_bk": "bk",
    "L0_xattn_Wv": "Wv", "L0_xattn_bv": "bv", "L0_xattn_Wo": "Wo", "L0_xattn_bo": "bo",
    "L0_ffn_gate_w": "gate_w", "L0_ffn_gate_b": "gate_b", "L0_ffn_w1": "w1", "L0_ffn_b1": "b1", "L0_ffn_w3": "w3",
    "L0_ffn_b3": "b3", "L0_ffn_w2": "w2", "L0_ffn_b2": "b2", "L0_ffn_sw1": "sw1", "L0_ffn_sb1": "sb1",
    "L0_ffn_sw3": "sw3", "L0_ffn_sb3": "sb3", "L0_ffn_sw2": "sw2", "L0_ffn_sb2": "sb2",
}


def kernel(**inputs):
    import numpy as _np
    import concourse.bacc as _bacc
    from concourse import mybir as _mybir
    from concourse.bass_utils import run_bass_kernel_spmd as _run

    nc = _bacc.Bacc("TRN2", target_bir_lowering=False, num_devices=1)
    arrays, w = {}, {}
    for name, short in _INS.items():
        a = _np.ascontiguousarray(inputs[name])
        arrays[f"in_{name}_dram"] = a
        w[short] = nc.dram_tensor(f"in_{name}_dram", a.shape, _mybir.dt.from_np(a.dtype), kind="ExternalInput").ap()
    out = nc.dram_tensor("out_dram", (B, S, D), F32, kind="ExternalOutput").ap()
    decoder_layer(nc, w, out)
    r = _run(nc, [arrays], core_ids=[0])
    return r.results[0]["out_dram"]
```
